# Optimizing a Trainium2 kernel written in Bass

```python
import numpy as np
import jax
import jax.numpy as jnp

def _softmax(x, axis=-1):
    return jax.nn.softmax(x, axis=axis)

def _gelu(x):
    return jax.nn.gelu(x, approximate=True)

def _silu(x):
    return jax.nn.silu(x)

def _sigmoid(x):
    return jax.nn.sigmoid(x)

def _layernorm(x, axis=-1, eps=1e-05):
    m = jnp.mean(x, axis=axis, keepdims=True)
    v = jnp.var(x, axis=axis, keepdims=True)
    return (x - m) / jnp.sqrt(v + eps)

def _scatter_add(tgt, idx, src, axis=0):
    return tgt.at[idx].add(src)

def _segment_sum(src, seg, n):
    return jax.ops.segment_sum(src, seg, n)
kernel_name = 'mk_pixart_seq_d2_seqx_r8_ae5c6a'

def setup_inputs(seed: int=0):
    np.random.seed(seed)
    _w = jnp.asarray

    def _rec_inputs():
        import jax
        import jax.numpy as jnp
        _rk = jax.random.key(seed)
        x = -0.0003929 + 0.9999 * jax.random.normal(jax.random.fold_in(_rk, 1), (4, 512, 128), jnp.float32)
        _lenS = 512 - jax.random.randint(jax.random.fold_in(_rk, 7), (4,), 0, max(1, 512 // 4) + 1, jnp.int32)
        _lenS2 = 77 - jax.random.randint(jax.random.fold_in(_rk, 8), (4,), 0, max(1, 77 // 4) + 1, jnp.int32)
        cond_1024 = 0.00782532 + 1.00527 * jax.random.normal(jax.random.fold_in(_rk, 11), (4, 128), jnp.float32)
        _ctx_1024P = jax.random.normal(jax.random.fold_in(_rk, 12), (4, 16, 128), jnp.float32)
        _ctx_1024c = jax.random.dirichlet(jax.random.fold_in(_rk, 512), 0.3 * jnp.ones((16,), jnp.float32), (4, 77))
        _ctx_1024t = jnp.einsum('bsk,bkd->bsd', _ctx_1024c, _ctx_1024P)
        _ctx_1024t = _ctx_1024t * jax.lax.rsqrt(jnp.mean(jnp.square(_ctx_1024t)) + 1e-12) * 0.953939
        ctx_1024 = -0.000761806 + 0.999296 * (_ctx_1024t + 0.3 * jax.random.normal(jax.random.fold_in(_rk, 612), (4, 77, 128), jnp.float32))
        return (x, cond_1024, ctx_1024)
    x, cond_1024, ctx_1024 = _rec_inputs()

    def _L0_xcond_setup():
        import jax, jax.numpy as jnp
        import numpy as np
        H = 128
        RH = 2 * H
        E = 3
        B, T, P = (8, 256, 64)
        LN_EPS = 1e-05

        def _layer_norm(x, gamma, beta):
            mu = jnp.mean(x, axis=-1, keepdims=True)
            var = jnp.mean(jnp.square(x - mu), axis=-1, keepdims=True)
            return (x - mu) * jax.lax.rsqrt(var + LN_EPS) * gamma + beta
        key = jax.random.key(seed)
        ks = jax.random.split(key, 24)
        s = lambda fan_in: 1.0 / np.sqrt(fan_in)
        inp = {'mix_hidden_states': jax.random.normal(ks[0], (B, T, H), jnp.float32), 'global_anchor': jax.random.normal(ks[1], (B, H), jnp.float32), 'prototype_bank': jax.random.normal(ks[2], (B, P, H), jnp.float32), 'ln_gamma': jnp.ones((H,), jnp.float32), 'ln_beta': jnp.zeros((H,), jnp.float32), 'Wq': jax.random.normal(ks[3], (H, H), jnp.float32) * s(H), 'Wk': jax.random.normal(ks[4], (H, H), jnp.float32) * s(H), 'Wv': jax.random.normal(ks[5], (H, H), jnp.float32) * s(H), 'router_W': jax.random.normal(ks[6], (3 * H, E), jnp.float32) * s(3 * H), 'router_b': jnp.zeros((E,), jnp.float32), 'e_w1': jax.random.normal(ks[7], (E, 3 * H, RH), jnp.float32) * s(3 * H), 'e_b1': jnp.zeros((E, RH), jnp.float32), 'e_w2': jax.random.normal(ks[8], (E, RH, H), jnp.float32) * s(RH), 'e_b2': jnp.zeros((E, H), jnp.float32), 'gate_w1': jax.random.normal(ks[9], (3 * H, H), jnp.float32) * s(3 * H), 'gate_b1': jnp.zeros((H,), jnp.float32), 'gate_w2': jax.random.normal(ks[10], (H, H), jnp.float32) * s(H), 'gate_b2': jnp.zeros((H,), jnp.float32), 'out_w': jax.random.normal(ks[11], (H, H), jnp.float32) * s(H), 'out_b': jnp.zeros((H,), jnp.float32)}
        return inp
    _L0_xcond_all = _L0_xcond_setup()
    _L0_xcond_in = {k: v for k, v in _L0_xcond_all.items() if k in ('ln_gamma', 'ln_beta', 'Wq', 'Wk', 'Wv', 'router_W', 'router_b', 'e_w1', 'e_b1', 'e_w2', 'e_b2', 'gate_w1', 'gate_b1', 'gate_w2', 'gate_b2', 'out_w', 'out_b')}
    del _L0_xcond_all

    def _L1_xcond_setup():
        import jax, jax.numpy as jnp
        import numpy as np
        LN_EPS = 1e-06

        def _ln(x):
            mu = jnp.mean(x, axis=-1, keepdims=True)
            var = jnp.var(x, axis=-1, keepdims=True)
            return (x - mu) * jax.lax.rsqrt(var + LN_EPS)
        key = jax.random.key(seed)
        H, NH = (128, 16)
        B, N, S = (4, 128, 77)
        MLP = int(H * 4.0)
        ks = jax.random.split(key, 20)
        s = 1.0 / np.sqrt(H)
        return {'x': jax.random.normal(ks[0], (B, N, H), jnp.float32), 'c': jax.random.normal(ks[1], (B, H), jnp.float32), 'context': jax.random.normal(ks[2], (B, S, H), jnp.float32), 'W_mod': jax.random.normal(ks[3], (H, 6 * H), jnp.float32) * s, 'b_mod': jnp.zeros((6 * H,), jnp.float32), 'W_qkv': jax.random.normal(ks[4], (H, 3 * H), jnp.float32) * s, 'b_qkv': jnp.zeros((3 * H,), jnp.float32), 'W_proj': jax.random.normal(ks[5], (H, H), jnp.float32) * s, 'b_proj': jnp.zeros((H,), jnp.float32), 'W_qc': jax.random.normal(ks[6], (H, H), jnp.float32) * s, 'b_qc': jnp.zeros((H,), jnp.float32), 'W_kvc': jax.random.normal(ks[7], (H, 2 * H), jnp.float32) * s, 'b_kvc': jnp.zeros((2 * H,), jnp.float32), 'W_cproj': jax.random.normal(ks[8], (H, H), jnp.float32) * s, 'b_cproj': jnp.zeros((H,), jnp.float32), 'W_mlp1': jax.random.normal(ks[9], (H, MLP), jnp.float32) * s, 'b_mlp1': jnp.zeros((MLP,), jnp.float32), 'W_mlp2': jax.random.normal(ks[10], (MLP, H), jnp.float32) * (1.0 / np.sqrt(MLP)), 'b_mlp2': jnp.zeros((H,), jnp.float32)}
    _L1_xcond_all = _L1_xcond_setup()
    _L1_xcond_in = {k: v for k, v in _L1_xcond_all.items() if k in ('W_mod', 'b_mod', 'W_qkv', 'b_qkv', 'W_proj', 'b_proj', 'W_qc', 'b_qc', 'W_kvc', 'b_kvc', 'W_cproj', 'b_cproj', 'W_mlp1', 'b_mlp1', 'W_mlp2', 'b_mlp2')}
    del _L1_xcond_all
    return {'x': x, 'cond_1024': cond_1024, 'ctx_1024': ctx_1024, 'L0_xcond_ln_gamma': _L0_xcond_in['ln_gamma'], 'L0_xcond_ln_beta': _L0_xcond_in['ln_beta'], 'L0_xcond_Wq': _L0_xcond_in['Wq'], 'L0_xcond_Wk': _L0_xcond_in['Wk'], 'L0_xcond_Wv': _L0_xcond_in['Wv'], 'L0_xcond_router_W': _L0_xcond_in['router_W'], 'L0_xcond_router_b': _L0_xcond_in['router_b'], 'L0_xcond_e_w1': _L0_xcond_in['e_w1'], 'L0_xcond_e_b1': _L0_xcond_in['e_b1'], 'L0_xcond_e_w2': _L0_xcond_in['e_w2'], 'L0_xcond_e_b2': _L0_xcond_in['e_b2'], 'L0_xcond_gate_w1': _L0_xcond_in['gate_w1'], 'L0_xcond_gate_b1': _L0_xcond_in['gate_b1'], 'L0_xcond_gate_w2': _L0_xcond_in['gate_w2'], 'L0_xcond_gate_b2': _L0_xcond_in['gate_b2'], 'L0_xcond_out_w': _L0_xcond_in['out_w'], 'L0_xcond_out_b': _L0_xcond_in['out_b'], 'L1_xcond_W_mod': _L1_xcond_in['W_mod'], 'L1_xcond_b_mod': _L1_xcond_in['b_mod'], 'L1_xcond_W_qkv': _L1_xcond_in['W_qkv'], 'L1_xcond_b_qkv': _L1_xcond_in['b_qkv'], 'L1_xcond_W_proj': _L1_xcond_in['W_proj'], 'L1_xcond_b_proj': _L1_xcond_in['b_proj'], 'L1_xcond_W_qc': _L1_xcond_in['W_qc'], 'L1_xcond_b_qc': _L1_xcond_in['b_qc'], 'L1_xcond_W_kvc': _L1_xcond_in['W_kvc'], 'L1_xcond_b_kvc': _L1_xcond_in['b_kvc'], 'L1_xcond_W_cproj': _L1_xcond_in['W_cproj'], 'L1_xcond_b_cproj': _L1_xcond_in['b_cproj'], 'L1_xcond_W_mlp1': _L1_xcond_in['W_mlp1'], 'L1_xcond_b_mlp1': _L1_xcond_in['b_mlp1'], 'L1_xcond_W_mlp2': _L1_xcond_in['W_mlp2'], 'L1_xcond_b_mlp2': _L1_xcond_in['b_mlp2']}

def reference(x, cond_1024, ctx_1024, L0_xcond_ln_gamma, L0_xcond_ln_beta, L0_xcond_Wq, L0_xcond_Wk, L0_xcond_Wv, L0_xcond_router_W, L0_xcond_router_b, L0_xcond_e_w1, L0_xcond_e_b1, L0_xcond_e_w2, L0_xcond_e_b2, L0_xcond_gate_w1, L0_xcond_gate_b1, L0_xcond_gate_w2, L0_xcond_gate_b2, L0_xcond_out_w, L0_xcond_out_b, L1_xcond_W_mod, L1_xcond_b_mod, L1_xcond_W_qkv, L1_xcond_b_qkv, L1_xcond_W_proj, L1_xcond_b_proj, L1_xcond_W_qc, L1_xcond_b_qc, L1_xcond_W_kvc, L1_xcond_b_kvc, L1_xcond_W_cproj, L1_xcond_b_cproj, L1_xcond_W_mlp1, L1_xcond_b_mlp1, L1_xcond_W_mlp2, L1_xcond_b_mlp2):
    import jax
    import jax.numpy as jnp

    def _L0_xcond_ref(mix_hidden_states, global_anchor, prototype_bank, ln_gamma, ln_beta, Wq, Wk, Wv, router_W, router_b, e_w1, e_b1, e_w2, e_b2, gate_w1, gate_b1, gate_w2, gate_b2, out_w, out_b):
        import jax, jax.numpy as jnp
        import numpy as np
        H = 128
        RH = 2 * H
        E = 3
        B, T, P = (8, 256, 64)
        LN_EPS = 1e-05

        def _layer_norm(x, gamma, beta):
            mu = jnp.mean(x, axis=-1, keepdims=True)
            var = jnp.mean(jnp.square(x - mu), axis=-1, keepdims=True)
            return (x - mu) * jax.lax.rsqrt(var + LN_EPS) * gamma + beta
        x = mix_hidden_states
        nx = _layer_norm(x, ln_gamma, ln_beta)
        q = nx @ Wq
        k = prototype_bank @ Wk
        v = prototype_bank @ Wv
        scores = jnp.einsum('bth,bph->btp', q, k) * H ** (-0.5)
        weights = jax.nn.softmax(scores, axis=-1)
        evidence = jnp.einsum('btp,bph->bth', weights, v)
        anchor = jnp.broadcast_to(global_anchor[:, None, :], nx.shape)
        combined = jnp.concatenate([nx, evidence, anchor], axis=-1)
        router_logits = combined @ router_W + router_b
        router_probs = jax.nn.softmax(router_logits, axis=-1)
        h = jax.nn.silu(jnp.einsum('btc,ecr->bter', combined, e_w1) + e_b1)
        expert_out = jnp.einsum('bter,erh->bteh', h, e_w2) + e_b2
        routed = jnp.sum(expert_out * router_probs[..., None], axis=-2)
        g = jax.nn.sigmoid(jax.nn.silu(combined @ gate_w1 + gate_b1) @ gate_w2 + gate_b2)
        refined_delta = g * (routed @ out_w + out_b)
        return x + refined_delta

    def _L1_xcond_ref(x, c, context, W_mod, b_mod, W_qkv, b_qkv, W_proj, b_proj, W_qc, b_qc, W_kvc, b_kvc, W_cproj, b_cproj, W_mlp1, b_mlp1, W_mlp2, b_mlp2):
        import jax, jax.numpy as jnp
        import numpy as np
        LN_EPS = 1e-06

        def _ln(x):
            mu = jnp.mean(x, axis=-1, keepdims=True)
            var = jnp.var(x, axis=-1, keepdims=True)
            return (x - mu) * jax.lax.rsqrt(var + LN_EPS)
        B, N, H = x.shape
        NH = 16
        hd = H // NH
        scale = hd ** (-0.5)
        c_proj = jax.nn.silu(c) @ W_mod + b_mod
        shift_a, scale_a, gate_a, shift_m, scale_m, gate_m = jnp.split(c_proj, 6, axis=-1)

        def modulate(t, shift, sc):
            return t * (1 + sc[:, None]) + shift[:, None]
        x_norm = modulate(_ln(x), shift_a, scale_a)
        qkv = x_norm @ W_qkv + b_qkv
        q, k, v = jnp.split(qkv, 3, axis=-1)
        q = q.reshape(B, N, NH, hd).transpose(0, 2, 1, 3)
        k = k.reshape(B, N, NH, hd).transpose(0, 2, 1, 3)
        v = v.reshape(B, N, NH, hd).transpose(0, 2, 1, 3)
        attn_w = jax.nn.softmax(jnp.einsum('bhqd,bhkd->bhqk', q, k) * scale, axis=-1)
        attn_out = jnp.einsum('bhqk,bhkd->bhqd', attn_w, v)
        attn_out = attn_out.transpose(0, 2, 1, 3).reshape(B, N, H)
        attn_out = attn_out @ W_proj + b_proj
        x = x + gate_a[:, None] * attn_out
        S = context.shape[1]
        q_c = _ln(x) @ W_qc + b_qc
        kv_c = _ln(context) @ W_kvc + b_kvc
        k_c, v_c = jnp.split(kv_c, 2, axis=-1)
        q_c = q_c.reshape(B, N, NH, hd).transpose(0, 2, 1, 3)
        k_c = k_c.reshape(B, S, NH, hd).transpose(0, 2, 1, 3)
        v_c = v_c.reshape(B, S, NH, hd).transpose(0, 2, 1, 3)
        c_attn_w = jax.nn.softmax(jnp.einsum('bhqd,bhsd->bhqs', q_c, k_c) * scale, axis=-1)
        c_attn_out = jnp.einsum('bhqs,bhsd->bhqd', c_attn_w, v_c)
        c_attn_out = c_attn_out.transpose(0, 2, 1, 3).reshape(B, N, H)
        c_attn_out = c_attn_out @ W_cproj + b_cproj
        x = x + c_attn_out
        x_norm2 = modulate(_ln(x), shift_m, scale_m)
        h = jax.nn.gelu(x_norm2 @ W_mlp1 + b_mlp1)
        h = h @ W_mlp2 + b_mlp2
        x = x + gate_m[:, None] * h
        return x
    x = _L0_xcond_ref(x, cond_1024, ctx_1024, L0_xcond_ln_gamma, L0_xcond_ln_beta, L0_xcond_Wq, L0_xcond_Wk, L0_xcond_Wv, L0_xcond_router_W, L0_xcond_router_b, L0_xcond_e_w1, L0_xcond_e_b1, L0_xcond_e_w2, L0_xcond_e_b2, L0_xcond_gate_w1, L0_xcond_gate_b1, L0_xcond_gate_w2, L0_xcond_gate_b2, L0_xcond_out_w, L0_xcond_out_b)
    x = _L1_xcond_ref(x, cond_1024, ctx_1024, L1_xcond_W_mod, L1_xcond_b_mod, L1_xcond_W_qkv, L1_xcond_b_qkv, L1_xcond_W_proj, L1_xcond_b_proj, L1_xcond_W_qc, L1_xcond_b_qc, L1_xcond_W_kvc, L1_xcond_b_kvc, L1_xcond_W_cproj, L1_xcond_b_cproj, L1_xcond_W_mlp1, L1_xcond_b_mlp1, L1_xcond_W_mlp2, L1_xcond_b_mlp2)
    return x

_drawn_inputs = setup_inputs


def setup_inputs(seed=0):
    import zlib

    import numpy as np

    out = dict(_drawn_inputs(seed))
    spreads = {'L0_xcond_ln_gamma': (1.0, 0.547),
     'L0_xcond_ln_beta': (0.0, 0.657),
     'L0_xcond_router_b': (0.0, 0.8),
     'L0_xcond_e_b1': (0.0, 0.381),
     'L0_xcond_e_b2': (0.0, 0.269),
     'L0_xcond_gate_b1': (0.0, 0.8),
     'L0_xcond_gate_b2': (0.0, 0.8),
     'L0_xcond_out_b': (0.0, 0.1),
     'L1_xcond_b_mod': (0.0, 0.1),
     'L1_xcond_b_qkv': (0.0, 0.1),
     'L1_xcond_b_proj': (0.0, 0.1),
     'L1_xcond_b_qc': (0.0, 0.484),
     'L1_xcond_b_kvc': (0.0, 0.1),
     'L1_xcond_b_cproj': (0.0, 0.1),
     'L1_xcond_b_mlp1': (0.0, 0.1),
     'L1_xcond_b_mlp2': (0.0, 0.1)}
    factors = {}
    for name, (base, spread) in spreads.items():
        noise = np.random.default_rng([zlib.crc32(name.encode()), seed]).standard_normal(out[name].shape)
        drawn = base * np.exp(spread * noise) if base else spread * noise
        out[name] = jnp.asarray(drawn.astype(out[name].dtype))
    for name, factor in factors.items():
        out[name] = (out[name] * factor).astype(out[name].dtype)
    return out
```

```python
from contextlib import ExitStack

import concourse.bass as bass
from concourse import mybir

ALU = mybir.AluOpType
ACT = mybir.ActivationFunctionType
AX_X = mybir.AxisListType.X
F32 = mybir.dt.float32
BF16 = mybir.dt.bfloat16

P = 128
NB = 4
C = 4
T = C * P
H = 128
S = 77
NH = 16
HD = H // NH
E = 3
G = 4
NG = NH // G
TILE = 32
KP = 96
SP_ = 96
ROW_M = 64
NZ = 7
PAIRS = [(0, 0), (0, 1), (1, 0), (1, 1), (0, 2), (2, 0)]
SELF_SCALE = float(HD) ** -0.5
PROTO_SCALE = float(H) ** -0.5
LAG = 6
RING = 8

F_G, F_WR, F_VP, F_HB, F_SHA, F_SCA, F_RB, F_N = 0, S, S + E, S + E + H, S + E + H + NZ, S + E + H + NZ + 1, \
    S + E + H + NZ + 2, S + E + H + NZ + 2 + E
B_SHM, B_SCM, B_VC, B_N = 0, 1, 2, 2 + NH * TILE

FRONT = ["nxT", "scores", "wT", "evT", "router"] + [f"h{z}" for z in range(NZ)] + \
    ["gate", "e0", "e1", "e2", "xnT", "q", "k", "v"]
BACK = ["cT", "qc", "cm"] + [f"{w}{g}" for g in range(NG) for w in ("cav", "co")] + \
    ["caT", "cproj", "xT", "m0", "m1", "m2", "m3", "mlp"]
OUT = ["o0", "o1", "o2", "o3", "aT", "proj"]

PLAN = [
    [["f:ln0"], [], ["t:av", "f:nxT"]],
    [["t:o3", "f:scores"], ["f:wT"], ["t:aT", "f:evT"]],
    [["t:proj", "f:router"], ["a:m1", "f:h0"], ["f:probs", "b:ln1"]],
    [["f:h1", "b:cT"], ["f:h2"], ["b:qc", "f:h3"]],
    [["f:h4"], ["f:h5"], ["f:h6"]],
    [["a:o0", "f:gate"], ["f:e0"], ["b:cn0"]],
    [["a:m2", "f:e1"], ["f:e2"], ["b:cn1"]],
    [["f:ln1"], ["b:cm"], ["f:xnT"]],
    [["f:q"], ["f:k"], ["f:v"]],
    [["a:o1"], ["b:cs0"], ["b:cav0", "b:cs1"]],
    [["a:m3", "b:co0"], ["b:cav1", "b:cs2"], ["b:co1", "b:cav2", "b:cs3"]],
    [["b:co2"], ["b:cav3"], ["b:co3"]],
    [["b:caT"], ["b:cproj"], ["b:ln2"]],
    [["a:o2"], ["b:xT"], ["b:m0"]],
    [["n:m0"], ["b:m1", "b:m2"], ["b:m3"]],
    [[], ["b:mlp"], []],
]
CN_SLOTS = (5, 6)
CS_SLOTS = (9, 10)


def do_place(plan, engine, b, has_attn, has_front, has_back):
    for entry in plan:
        chain, step = entry.split(":")
        if chain == "f" and has_front:
            engine["front"](step, b + 1)
        elif chain == "n" and has_front:
            engine["attn"](step, b + 1)
        elif chain == "a" and has_attn:
            engine["attn"](step, b)
        elif chain == "t" and has_back:
            engine["attn"](step, b - 1)
        elif chain == "b" and has_back:
            engine["back"](step, b - 1, has_attn)


def iterations(engine, run):
    run(-1, has_attn=False, has_front=True, has_back=False)
    run(0, has_attn=True, has_front=True, has_back=False)
    for b in range(1, NB - 1):
        run(b, has_attn=True, has_front=True, has_back=True)
    run(NB - 1, has_attn=True, has_front=False, has_back=True)
    run(NB, has_attn=False, has_front=False, has_back=True)


def build(nc, a, out):
    ctx = ExitStack()
    with ctx:
        def sb(name, shape, dt=F32):
            return ctx.enter_context(nc.sbuf_tensor(name, shape, dt))

        wqkv0 = sb("wqkv0", [P, 3, H])
        w1 = sb("w1", [P, 3, NZ, H])
        wr = sb("wr", [P, 3, E])
        w2o = sb("w2o", [P, 2 * E, H])
        gw2 = sb("gw2", [P, H])
        wqkv = sb("wqkv", [P, 3 * H])
        wproj = sb("wproj", [P, H])
        wqc = sb("wqc", [P, H])
        wkvc = sb("wkvc", [P, 2 * H])
        wcproj = sb("wcproj", [P, H])
        wm1 = sb("wm1", [P, 4 * H])
        wm2 = sb("wm2", [P, 4, H])
        cols = sb("cols", [P, 40])
        bcast = sb("bcast", [P, 5, H])
        rbb = sb("rbb", [P, E])
        b2oB = sb("b2oB", [P, E, H])
        identf = sb("identf", [P, P])
        identb = sb("identb", [P, P], BF16)
        minus_half = sb("minus_half", [P, C])
        fpar_all = sb("fpar_all", [P, NB, F_N])
        bpar_all = sb("bpar_all", [P, NB, B_N])
        gates = sb("gates", [P, NB, 2, H])
        fpar = sb("fpar", [P, F_N])
        x = sb("x", [P, C, H])
        st = sb("st", [P, C, 6])
        mv = sb("mv", [P, C, 2])
        rstd = sb("rstd", [P, C])
        xh = sb("xh", [P, C, H])
        nxT = sb("nxT", [P, T])
        pm = sb("pm", [P, 4, C])
        pw = sb("pw", [P, C, S])
        lg = sb("lg", [P, 4, C, E])
        lm = sb("lm", [P, 3, C])
        wT = sb("wT", [P, T])
        evT = sb("evT", [P, T])
        z = sb("z", [P, NZ, T])
        gz = sb("gz", [P, C, H])
        acc = sb("acc", [P, C, H])
        rb = acc
        rt = sb("rt", [P, C, H])
        x0 = sb("x0", [P, C, H])
        xnT = nxT
        qf = sb("qf", [P, T])
        kf = sb("kf", [P, T])
        qp = sb("qp", [P, 3, T], BF16)
        kp = sb("kp", [P, 3, T], BF16)
        vst = sb("vst", [P, C, NH, HD])
        qS = sb("qS", [KP, NH, T], BF16)
        kS = sb("kS", [KP, NH, T], BF16)
        vS = sb("vS", [P, C, NH, TILE])
        mx = sb("mx", [P, C, NH])
        mr = sb("mr", [P, C, G])
        mp = sb("mp", [P, C, 3, G], BF16)
        mrow = sb("mrow", [3 * G, T], BF16)
        pT = sb("pT", [P, RING, T])
        oT = sb("oT", [P, T])
        rec = sb("rec", [P, C, G])
        an = sb("an", [P, C, NH, HD])
        aT = oT
        wpg = sb("wpg", [P, H])
        gbp = sb("gbp", [P, H])
        x0gb = sb("x0gb", [P, C, H])
        bpar = sb("bpar", [P, B_N])
        kcS = sb("kcS", [KP, NH, S], BF16)
        x1 = sb("x1", [P, C, H])
        x1b = x2 = x2gb = yo = x1
        bst = sb("bst", [P, C, 6])
        bmv = sb("bmv", [P, C, 2])
        brstd = sb("brstd", [P, C])
        bxh = sb("bxh", [P, C, H])
        cT = sb("cT", [P, T])
        coT = caT = mT = cT
        qcf = sb("qcf", [P, T])
        qcp = sb("qcp", [P, 3, T], BF16)
        qcS = sb("qcS", [KP, NH, T], BF16)
        cmx = sb("cmx", [P, C, NH])
        cmr = sb("cmr", [P, C, NH])
        cmp_ = sb("cmp", [P, C, 3, NH], BF16)
        cmrow = sb("cmrow", [3 * NH, T], BF16)
        cpT = sb("cpT", [SP_, G, T])
        crec = sb("crec", [P, C, G])
        can = sb("can", [P, C, NH, HD])
        hm = z[:, 0:4, :]
        w2g = sb("w2g", [P, 4, H])
        gbm = sb("gbm", [P, H])
        spare = {"pT": [pT[:, :, :].rearrange("p r t -> p (r t)"), 0], "z": [z[:, :, :].rearrange("p z t -> p (z t)"), 0]}

        def within(where, *shape):
            n = 1
            for d in shape:
                n *= d
            t = spare[where][0][:, spare[where][1]:spare[where][1] + n]
            spare[where][1] += n
            return t.rearrange("p (j n) -> p j n", j=shape[0]) if len(shape) == 2 else t

        ew2, ew2T = within("pT", 2 * E, H), within("pT", 2 * E, H)
        condrep, silurep = within("pT", NB, H), within("pT", NB, H)
        b2rep, ctxn = within("pT", E, H), within("pT", NB, H)
        ctxh, ctxT, ctxhT, kpT = within("z", NB, H), within("z", NB, S), within("z", NB, S), within("z", NB, S)
        kcf, wq0T, silc = within("z", NB * S), within("z", H), within("z", NB)
        wmod, bgates, bvc = within("z", 6, H), within("z", 2, H), within("z", H)
        rows, outw, bout = within("pT", H), within("pT", H), within("pT", H)
        kcp = within("z", 3 * NB * S // 2).bitcast(BF16).rearrange("p (j n) -> p j n", j=3)
        q_dram = nc.dram_tensor("q_parts", (3, P, T), BF16, kind="Internal").ap()
        k_dram = nc.dram_tensor("k_parts", (3, P, T), BF16, kind="Internal").ap()
        qc_dram = nc.dram_tensor("qc_parts", (3, P, T), BF16, kind="Internal").ap()
        m_dram = nc.dram_tensor("m_parts", (3 * G, T), BF16, kind="Internal").ap()
        cm_dram = nc.dram_tensor("cm_parts", (3 * NH, T), BF16, kind="Internal").ap()
        kc_dram = nc.dram_tensor("kc_parts", (3, P, NB * S), BF16, kind="Internal").ap()

        ps = ctx.enter_context(nc.psum_tensor("ps", [P, 8, T], F32))
        nat, sco, avb = ps[:, 0:2, :], ps[:, 2:4, :], ps[:, 4, :]
        xb, fb, bb = ps[:, 5, :], ps[:, 6, :], ps[:, 7, :]

        FRONT_VEC = ["stats", "aggr", "xhat", "pmax", "lg0", "pneg", "prec", "pnorm", "lmax", "lsub", "lsum", "lrec",
                     "probs", "gated", "x0", "stats1", "aggr1", "xhat1", "qrest", "qpart2", "q_parts"]
        FRONT_POOL = ["eps", "rstd", "rb0", "rt1", "rb1", "rt2", "rb2", "eps1", "rstd1", "krest", "kpart2", "k_parts"]
        FRONT_ACT = ["rexp", "silu", "tanh"]
        BACK_VEC = ["stats1", "aggr1", "xhat1", "n1", "nrest", "n2", "n3", "stats2", "aggr2", "xhat2"]
        BACK_POOL = ["w2g", "gbm", "eps1", "rstd1", "qrest", "qpart2", "qc_parts", "x1b", "eps2", "rstd2", "x2gb"]
        ATTN_POOL = ["wpg", "gbp", "x0gb"]
        HALF = 2 * len(PAIRS) + 1

        per = {
            "x_loaded": 16, "fpar_loaded": 16, "q_kept": 16, "k_kept": 16, "half0": 16 * HALF, "half1": 16 * HALF,
            "front_filled": len(FRONT), "front_drained": len(FRONT), "front_vec": len(FRONT_VEC),
            "front_pool": len(FRONT_POOL), "front_act": len(FRONT_ACT),
            "nat_scored": NH * C, "nat_reduced": NH * C, "s_scored": NH * C, "exp_done": NH * C, "av_used": NH * C,
            "av_drained": NG, "m_vec": 4 * NG, "m_filled": NG, "m_drained": NG, "m_kept": 16 * NG,
            "m_placed": 16 * NG, "o_filled": len(OUT), "o_drained": len(OUT), "o_vec": NG, "v_placed": 1,
            "attn_pool": len(ATTN_POOL), "bpar_loaded": 16 * (3 + len(PAIRS)), "back_filled": len(BACK),
            "back_drained": len(BACK), "back_vec": len(BACK_VEC), "back_pool": len(BACK_POOL), "qc_kept": 16,
            "qc_placed": 16 * len(PAIRS), "cn_scored": NH, "cn_reduced": NH, "cm_kept": 16, "cm_placed": 16,
            "cs_scored": NH, "cexp_done": NH, "gelu_done": 1, "co_vec": NG, "y_stored": 16,
        }
        sem = {name: ctx.enter_context(nc.semaphore(name)) for name in per}

        def upto(name, b, k):
            return (b + 1) * per[name] + k

        def begin(engine, names):
            for name in names:
                engine.sem_inc(sem[name], per[name])

        def after(engine, name, b, steps, step):
            engine.wait_ge(sem[name], upto(name, b, steps.index(step) + 1))

        FILLS = ["cols", "ctxT", "ctxhT", "wq0T", "kpT", "G", "vp", "kc", "vc", "hb", "rbias", "mod", "gates0",
                 "gates1", "ew2Ta", "ew2Tb", "w2oa", "w2ob", "b2o"]
        SETUP_VEC = ["stats", "aggr", "cols", "ctxT", "ctxhat", "condrep", "b2rep", "ctxhT", "wq0T", "kpT", "G",
                     "wr", "vp", "kcf", "kpart1", "krest", "kpart2", "kc_parts", "vc", "hb", "rbias", "silurep",
                     "mod", "gates0", "gates1", "ew2Ta", "ew2Tb", "w2oa", "w2ob", "b2o"]
        s_filled = ctx.enter_context(nc.semaphore("setup_filled"))
        s_vec = ctx.enter_context(nc.semaphore("setup_vec"))
        s_silu = ctx.enter_context(nc.semaphore("setup_silu"))
        s_rstd = ctx.enter_context(nc.semaphore("setup_rstd"))
        s_consts = ctx.enter_context(nc.semaphore("constants_ready"))
        s_zeros = ctx.enter_context(nc.semaphore("zeros_ready"))
        s_vzeros = ctx.enter_context(nc.semaphore("vector_zeros_ready"))
        kc_kept = ctx.enter_context(nc.semaphore("kc_kept"))
        CONSTS, ZEROS = 5, 4
        VZEROS = 8

        def filled(engine, step):
            engine.wait_ge(s_filled, FILLS.index(step) + 1)

        def drained(engine, step):
            engine.wait_ge(s_vec, SETUP_VEC.index(step) + 1)

        def fill_bank(step):
            return ps[:, FILLS.index(step) % 8, :]

        loads = {w: [] for w in ("ctx", "rows", "w0", "w1", "mod", "experts", "rest")}
        loaded = {w: ctx.enter_context(nc.semaphore(f"loaded_{w}")) for w in loads}
        loads["ctx"].append((ctxn[0:S, :, :], a["ctx_1024"].rearrange("b s h -> s b h")))
        row_of, at = {}, 0
        for name, n in (("L0_xcond_e_b1", 2 * E), ("L0_xcond_gate_b1", 1), ("L0_xcond_ln_gamma", 1),
                        ("L0_xcond_ln_beta", 1), ("L1_xcond_b_mod", 6), ("L1_xcond_b_qkv", 3), ("L1_xcond_b_qc", 1),
                        ("L1_xcond_b_kvc", 2), ("L1_xcond_b_mlp1", 4), ("cond_1024", NB), ("L0_xcond_e_b2", E)):
            src = a[name]
            if name == "L0_xcond_e_b1":
                src = src.rearrange("e (j p) -> (e j) p", p=P)
            elif n == 1 or name.startswith("L1"):
                src = src.rearrange("(j p) -> j p", p=P)
            loads["rows"].append((rows[at:at + n, :], src))
            row_of[name] = at
            at += n
        NR = at

        def col(name, j=0, n=1):
            return cols[:, row_of[name] + j:row_of[name] + j + n]

        def keep(when, dst, src):
            loads[when].append((dst, src))

        for i, w in enumerate(("Wq", "Wk", "Wv")):
            keep("w0", wqkv0[:, i, :], a[f"L0_xcond_{w}"])
        keep("w0", wr[:, :, :], a["L0_xcond_router_W"].rearrange("(k p) e -> p k e", p=P))
        keep("w0", wkvc[:, :], a["L1_xcond_W_kvc"])
        for k in range(3):
            keep("w1", w1[:, k, 0:2 * E, :].rearrange("p (e j) r -> p e (j r)", e=E),
                 a["L0_xcond_e_w1"][:, k * P:(k + 1) * P, :].rearrange("e p r -> p e r"))
        keep("w1", w1[:, :, 2 * E, :], a["L0_xcond_gate_w1"].rearrange("(k p) h -> p k h", p=P))
        keep("mod", wmod[:, :, :], a["L1_xcond_W_mod"].rearrange("p (j h) -> p j h", h=H))
        keep("experts", ew2[:, :, :], a["L0_xcond_e_w2"].rearrange("e (j p) h -> p (e j) h", p=P))
        keep("experts", outw[:, :], a["L0_xcond_out_w"])
        BC = {}
        for i, (name, src) in enumerate((
                ("gate_b2", a["L0_xcond_gate_b2"]), ("bv", a["L1_xcond_b_qkv"][2 * H:3 * H]),
                ("bproj", a["L1_xcond_b_proj"]), ("bcproj", a["L1_xcond_b_cproj"]), ("bm2", a["L1_xcond_b_mlp2"]))):
            keep("rest", bcast[:, i, :], src.partition_broadcast(P))
            BC[name] = bcast[:, i, :]
        keep("mod", bvc, a["L1_xcond_b_kvc"][H:2 * H].partition_broadcast(P))
        for i, j in enumerate((2, 5)):
            keep("mod", bgates[:, i, :], a["L1_xcond_b_mod"][j * H:(j + 1) * H].partition_broadcast(P))
        keep("experts", bout, a["L0_xcond_out_b"].partition_broadcast(P))
        keep("w0", rbb[:, :], a["L0_xcond_router_b"].partition_broadcast(P))
        keep("rest", gw2[:, :], a["L0_xcond_gate_w2"])
        keep("rest", wqkv[:, :], a["L1_xcond_W_qkv"])
        keep("rest", wproj[:, :], a["L1_xcond_W_proj"])
        keep("rest", wqc[:, :], a["L1_xcond_W_qc"])
        keep("rest", wcproj[:, :], a["L1_xcond_W_cproj"])
        keep("rest", wm1[:, :], a["L1_xcond_W_mlp1"])
        keep("rest", wm2[:, :, :], a["L1_xcond_W_mlp2"].rearrange("(j p) h -> p j h", p=P))

        def weights(engine, *when):
            for w in when:
                engine.wait_ge(loaded[w], 16 * len(loads[w]))

        def over(t, n):
            return t.unsqueeze(1).to_broadcast([t.shape[0], n, t.shape[1]])

        def along(t, n):
            return t.unsqueeze(len(t.shape)).to_broadcast([*t.shape, n])

        def chunk(t, c):
            return t[:, c * P:(c + 1) * P]

        def chunks(t):
            return t.rearrange("p (c h) -> p c h", c=C)

        m_bank = xb.bitcast(BF16)
        cm_bank = bb.bitcast(BF16)

        block = ctx.enter_context(nc.Block())

        @block.sync
        def _(sp):
            begin(sp, ["x_loaded", "fpar_loaded", "q_kept", "k_kept", "half0", "half1", "m_kept", "m_placed",
                       "bpar_loaded", "qc_kept", "qc_placed", "cm_kept", "cm_placed", "y_stored"])
            for w, pairs in loads.items():
                for dst, src in pairs:
                    sp.dma_start(dst, src).then_inc(loaded[w], 16)
            drained(sp, "kc_parts")
            sp.dma_start(kc_dram.rearrange("j p n -> p j n"), kcp[:, :, :]).then_inc(kc_kept, 16)
            sp.wait_ge(kc_kept, 16)
            sp.wait_ge(s_zeros, ZEROS)
            drained(sp, "b2o")
            sp.wait_ge(s_vzeros, VZEROS)

            def place_half(b, half):
                heads = slice(half * NH // 2, (half + 1) * NH // 2)
                lines = slice(half * P // 2, (half + 1) * P // 2)
                sp.wait_ge(sem["s_scored"], upto("s_scored", b - 1, NH * C // 2 * (half + 1)))
                sp.wait_ge(sem["q_kept"], upto("q_kept", b, 16))
                sp.wait_ge(sem["k_kept"], upto("k_kept", b, 16))
                done = sem[f"half{half}"]
                for t, (qpart, kpart) in enumerate(PAIRS):
                    rows_t = slice(HD * t, HD * (t + 1))
                    sp.dma_start(qS[rows_t, heads, :],
                                 q_dram[qpart, lines, :].rearrange("(h d) n -> d h n", d=HD)).then_inc(done, 16)
                    sp.dma_start(kS[rows_t, heads, :],
                                 k_dram[kpart, lines, :].rearrange("(h d) n -> d h n", d=HD)).then_inc(done, 16)
                sp.dma_start(qS[ROW_M:ROW_M + 3, heads, :], kS[KP - 3:KP, 0:NH // 2, :]
                             ).then_inc(done, 16)

            def front(step, b):
                if step == "ln0":
                    after(sp, "front_vec", b - 1, FRONT_VEC, "x0")
                    sp.dma_start(x[:, :, :], a["x"][bass.ds(b, 1)].rearrange("o (p c) h -> p (o c) h", c=C)
                                 ).then_inc(sem["x_loaded"], 16)
                    after(sp, "front_drained", b - 1, FRONT, "xnT")
                    sp.dma_start(fpar[:, :], fpar_all[:, bass.ds(b, 1), :].rearrange("p o n -> p (o n)")
                                 ).then_inc(sem["fpar_loaded"], 16)
                if step == "q":
                    after(sp, "front_vec", b, FRONT_VEC, "q_parts")
                    sp.wait_ge(sem["half1"], upto("half1", b - 1, 16 * HALF))
                    sp.dma_start(q_dram.rearrange("j p n -> p j n"), qp[:, :, :]).then_inc(sem["q_kept"], 16)
                if step == "k":
                    after(sp, "front_pool", b, FRONT_POOL, "k_parts")
                    sp.dma_start(k_dram.rearrange("j p n -> p j n"), kp[:, :, :]).then_inc(sem["k_kept"], 16)
                    place_half(b, 0)

            def attn(step, b):
                if step[0] == "m":
                    g = int(step[1])
                    after(sp, "m_drained", b, range(NG), g)
                    sp.wait_ge(sem["m_placed"], upto("m_placed", b, 16 * g))
                    sp.dma_start(m_dram, mrow[:, :]).then_inc(sem["m_kept"], 16)
                    sp.wait_ge(sem["m_kept"], upto("m_kept", b, 16 * (g + 1)))
                    sp.dma_start(qS[ROW_M:ROW_M + 3, g * G:g * G + G, :], m_dram.rearrange("(s h) n -> s h n", s=3)
                                 ).then_inc(sem["m_placed"], 16)

            def back(step, b, _):
                if step == "ln1":
                    after(sp, "back_drained", b - 1, BACK, "mlp")
                    sp.wait_ge(sem["cs_scored"], upto("cs_scored", b - 1, NH))
                    sp.dma_start(bpar[:, :], bpar_all[:, bass.ds(b, 1), :].rearrange("p o n -> p (o n)")
                                 ).then_inc(sem["bpar_loaded"], 16)
                    for t, (_, kpart) in enumerate(PAIRS):
                        sp.dma_start(kcS[HD * t:HD * (t + 1), :, :],
                                     kc_dram[kpart].rearrange("(h d) n -> d h n", d=HD)[:, :, bass.ds(b * S, S)]
                                     ).then_inc(sem["bpar_loaded"], 16)
                    for half in range(2):
                        sp.dma_start(qcS[ROW_M:ROW_M + 3, half * NH // 2:(half + 1) * NH // 2, :],
                                     kS[KP - 3:KP, 0:NH // 2, :]
                                     ).then_inc(sem["bpar_loaded"], 16)
                if step == "qc":
                    after(sp, "back_pool", b, BACK_POOL, "qc_parts")
                    sp.dma_start(qc_dram.rearrange("j p n -> p j n"), qcp[:, :, :]).then_inc(sem["qc_kept"], 16)
                    sp.wait_ge(sem["qc_kept"], upto("qc_kept", b, 16))
                    for t, (qpart, _) in enumerate(PAIRS):
                        sp.dma_start(qcS[HD * t:HD * (t + 1), :, :],
                                     qc_dram[qpart].rearrange("(h d) n -> d h n", d=HD)
                                     ).then_inc(sem["qc_placed"], 16)
                if step == "cm":
                    after(sp, "back_drained", b, BACK, "cm")
                    sp.dma_start(cm_dram, cmrow[:, :]).then_inc(sem["cm_kept"], 16)
                    sp.wait_ge(sem["cm_kept"], upto("cm_kept", b, 16))
                    sp.dma_start(qcS[ROW_M:ROW_M + 3, :, :], cm_dram.rearrange("(s h) n -> s h n", s=3)
                                 ).then_inc(sem["cm_placed"], 16)
                if step == "mlp":
                    after(sp, "back_drained", b, BACK, "mlp")
                    sp.dma_start(out[bass.ds(b, 1)].rearrange("o (p c) h -> p (o c) h", c=C), yo[:, :, :]
                                 ).then_inc(sem["y_stored"], 16)

            def run(b, has_attn, has_front, has_back):
                if has_attn:
                    place_half(b, 1)
                for places in PLAN:
                    for place in places:
                        do_place(place, {"front": front, "attn": attn, "back": back}, b,
                                 has_attn, has_front, has_back)

            iterations(sp, run)
            sp.wait_ge(sem["y_stored"], upto("y_stored", NB - 1, 16))

        @block.gpsimd
        def _(pool):
            begin(pool, ["front_pool", "back_pool", "attn_pool"])

            def const(ins, sem_=s_consts):
                ins.then_inc(sem_, 1)

            const(nc.gpsimd.memset(identf[:, :], 0.0))
            const(nc.gpsimd.memset(identb[:, :], 0.0))
            pool.wait_ge(s_consts, 2)
            for m in (identf, identb):
                const(nc.gpsimd.affine_select(out=m[:, :], in_=m[:, :], compare_op=ALU.not_equal, fill=1.0,
                                              base=0, pattern=[[-1, P]], channel_multiplier=1))
            const(nc.gpsimd.memset(minus_half[:, :], -0.5))
            pool.wait_ge(s_consts, CONSTS)

            def inv_sqrt(done, steps, b, var, eps, out_, name_eps, name_rstd):
                nc.gpsimd.tensor_scalar(out_, var, eps, None, ALU.add).then_inc(sem[done], 1)
                after(pool, done, b, steps, name_eps)
                nc.gpsimd.tensor_tensor(out_, out_, minus_half[:, :], ALU.pow).then_inc(sem[done], 1)

            drained(pool, "aggr")
            nc.gpsimd.tensor_scalar(rstd[0:S, :], mv[0:S, :, 1], 1e-6, None, ALU.add).then_inc(s_rstd, 1)
            pool.wait_ge(s_rstd, 1)
            nc.gpsimd.tensor_tensor(rstd[0:S, :], rstd[0:S, :], minus_half[0:S, :], ALU.pow).then_inc(s_rstd, 1)
            const(nc.gpsimd.memset(kcS[0:KP, :, :], 0.0), s_zeros)
            const(nc.gpsimd.memset(kS[0:KP, :, :].bitcast(F32), 0.0), s_zeros)
            pool.wait_ge(s_zeros, 2)
            const(nc.gpsimd.memset(kcS[ROW_M:ROW_M + 3, :, :], 1.0), s_zeros)
            const(nc.gpsimd.memset(kS[ROW_M:ROW_M + 3, :, :], 1.0), s_zeros)

            def front(step, b):
                def did(ins):
                    ins.then_inc(sem["front_pool"], 1)

                if step == "ln0":
                    after(pool, "front_vec", b, FRONT_VEC, "aggr")
                    inv_sqrt("front_pool", FRONT_POOL, b, mv[:, :, 1], 1e-5, rstd[:, :], "eps", "rstd")
                if step == "probs":
                    after(pool, "front_vec", b, FRONT_VEC, "probs")
                    after(pool, "front_vec", b - 1, FRONT_VEC, "x0")
                    probs = lg[:, 3, :, :]
                    did(nc.gpsimd.tensor_tensor(rb[:, :, :], over(b2oB[:, 0, :], C), along(probs[:, :, 0], H), ALU.mult))
                    for e in (1, 2):
                        if e == 2:
                            after(pool, "front_pool", b, FRONT_POOL, "rb1")
                        did(nc.gpsimd.tensor_tensor(rt[:, :, :], over(b2oB[:, e, :], C), along(probs[:, :, e], H), ALU.mult))
                        after(pool, "front_pool", b, FRONT_POOL, f"rt{e}")
                        did(nc.gpsimd.tensor_tensor(rb[:, :, :], rb[:, :, :], rt[:, :, :], ALU.add))
                if step == "ln1":
                    after(pool, "front_vec", b, FRONT_VEC, "aggr1")
                    inv_sqrt("front_pool", FRONT_POOL, b, mv[:, :, 1], 1e-6, rstd[:, :], "eps1", "rstd1")
                if step == "k":
                    after(pool, "front_drained", b, FRONT, "k")
                    did(nc.gpsimd.tensor_tensor(kf[:, :], kf[:, :], kp[:, 0, :], ALU.subtract))
                    after(pool, "front_pool", b, FRONT_POOL, "krest")
                    did(nc.gpsimd.tensor_scalar(kp[:, 1, :], kf[:, :], 1.0, 0.0, ALU.mult, ALU.add))
                    after(pool, "front_pool", b, FRONT_POOL, "kpart2")
                    did(nc.gpsimd.tensor_tensor(kp[:, 2, :], kf[:, :], kp[:, 1, :], ALU.subtract))

            def back(step, b, _):
                def did(ins):
                    ins.then_inc(sem["back_pool"], 1)

                if step == "ln1":
                    after(pool, "back_filled", b - 1, BACK, "mlp")
                    gm = gates[:, bass.ds(b, 1), 1, :]
                    did(nc.gpsimd.tensor_tensor(w2g[:, :, :], wm2[:, :, :], gm.to_broadcast([P, 4, H]), ALU.mult))
                    after(pool, "back_pool", b - 1, BACK_POOL, "x2gb")
                    did(nc.gpsimd.tensor_tensor(gbm[:, :].unsqueeze(1), BC["bm2"].unsqueeze(1), gm, ALU.mult))
                    after(pool, "back_vec", b, BACK_VEC, "aggr1")
                    inv_sqrt("back_pool", BACK_POOL, b, bmv[:, :, 1], 1e-6, brstd[:, :], "eps1", "rstd1")
                if step == "qc":
                    after(pool, "back_drained", b, BACK, "qc")
                    did(nc.gpsimd.tensor_tensor(qcf[:, :], qcf[:, :], qcp[:, 0, :], ALU.subtract))
                    after(pool, "back_pool", b, BACK_POOL, "qrest")
                    did(nc.gpsimd.tensor_scalar(qcp[:, 1, :], qcf[:, :], 1.0, 0.0, ALU.mult, ALU.add))
                    after(pool, "back_pool", b, BACK_POOL, "qpart2")
                    did(nc.gpsimd.tensor_tensor(qcp[:, 2, :], qcf[:, :], qcp[:, 1, :], ALU.subtract))
                    after(pool, "back_vec", b, BACK_VEC, "xhat1")
                    did(nc.gpsimd.tensor_tensor(x1b[:, :, :], x1[:, :, :], over(BC["bcproj"], C), ALU.add))
                if step == "xT":
                    after(pool, "back_vec", b, BACK_VEC, "xhat2")
                    did(nc.gpsimd.tensor_tensor(x2gb[:, :, :], x2[:, :, :], over(gbm[:, :], C), ALU.add))
                if step == "ln2":
                    after(pool, "back_vec", b, BACK_VEC, "aggr2")
                    inv_sqrt("back_pool", BACK_POOL, b, bmv[:, :, 1], 1e-6, brstd[:, :], "eps2", "rstd2")

            def fold(b):
                def did(ins):
                    ins.then_inc(sem["attn_pool"], 1)

                after(pool, "o_drained", b - 1, OUT, "proj")
                after(pool, "front_vec", b, FRONT_VEC, "x0")
                ga = gates[:, bass.ds(b, 1), 0, :]
                did(nc.gpsimd.tensor_tensor(wpg[:, :].unsqueeze(1), wproj[:, :].unsqueeze(1), ga, ALU.mult))
                did(nc.gpsimd.tensor_tensor(gbp[:, :].unsqueeze(1), BC["bproj"].unsqueeze(1), ga, ALU.mult))
                after(pool, "attn_pool", b, ATTN_POOL, "gbp")
                did(nc.gpsimd.tensor_tensor(x0gb[:, :, :], x0[:, :, :], over(gbp[:, :], C), ALU.add))

            weights(pool, "rest")
            drained(pool, "b2o")

            def run(b, has_attn, has_front, has_back):
                for s, places in enumerate(PLAN):
                    if s == 3 and has_attn:
                        fold(b)
                    for place in places:
                        do_place(place, {"front": front, "attn": lambda step, b: None, "back": back}, b,
                                 has_attn, has_front, has_back)

            iterations(pool, run)

        @block.scalar
        def _(act):
            begin(act, ["front_drained", "front_act", "exp_done", "av_drained", "m_drained", "o_drained",
                        "back_drained", "cexp_done", "gelu_done"])
            drained(act, "cols")
            nc.scalar.activation(silc[:, :], col("cond_1024", 0, NB), ACT.Silu).then_inc(s_silu, 1)
            drained(act, "b2o")
            act.wait_ge(kc_kept, 16)
            act.wait_ge(s_vzeros, VZEROS)

            def drain(out_, in_, done, **kw):
                nc.scalar.activation(out_, in_, ACT.Identity if kw else ACT.Copy, **kw).then_inc(sem[done], 1)

            def front(step, b):
                done = "front_drained"
                if step in FRONT:
                    after(act, "front_filled", b, FRONT, step)
                if step == "nxT":
                    drain(nxT[:, :], fb, done, scale=col("L0_xcond_ln_gamma"), bias=col("L0_xcond_ln_beta"))
                if step == "scores":
                    after(act, "front_vec", b, FRONT_VEC, "pneg")
                    for c in range(C):
                        ins = nc.scalar.activation(pw[:, c, :], fb[:, c * (S + E):c * (S + E) + S], ACT.Exp,
                                                   bias=pm[:, 1, c:c + 1], scale=PROTO_SCALE,
                                                   accum_out=pm[:, 2, c:c + 1])
                    ins.then_inc(sem[done], 1)
                if step == "wT":
                    drain(wT[0:S, :], fb[0:S, :], done)
                if step == "evT":
                    drain(evT[:, :], fb, done)
                if step == "router":
                    after(act, "front_vec", b, FRONT_VEC, "lsub")
                    nc.scalar.activation(lg[:, 2, :, :], lg[:, 1, :, :], ACT.Exp).then_inc(sem["front_act"], 1)
                if step[0] == "h":
                    zi = int(step[1])
                    if zi == 0:
                        if not isinstance(b, int) or b == NB - 1:
                            after(act, "back_filled", b - 3, BACK, "mlp")
                        after(act, "fpar_loaded", b, range(16), 15)
                    drain(z[:, zi, :], fb, done, bias=fpar[:, F_HB + zi:F_HB + zi + 1])
                    if zi == NZ - 1:
                        after(act, done, b, FRONT, step)
                        flat = z[:, :, :].rearrange("p z t -> p (z t)")
                        nc.scalar.activation(flat, flat, ACT.Silu).then_inc(sem["front_act"], 1)
                if step == "gate":
                    after(act, done, b, FRONT, "gate")
                    nc.scalar.activation(gz[:, :, :], gz[:, :, :], ACT.Tanh, scale=0.5).then_inc(sem["front_act"], 1)
                if step == "xnT":
                    drain(xnT[:, :], fb, done, scale=fpar[:, F_SCA:F_SCA + 1], bias=fpar[:, F_SHA:F_SHA + 1])
                if step in ("q", "k"):
                    part, whole = (qp, qf) if step == "q" else (kp, kf)
                    bias = col("L1_xcond_b_qkv", "qk".index(step))
                    after(act, f"{step}_kept", b - 1, range(16), 15)
                    nc.scalar.activation(part[:, 0, :], fb, ACT.Identity, bias=bias)
                    drain(whole[:, :], fb, done, bias=bias)

            def attn(step, b):
                if step == "av":
                    take(b, NG - 1)
                if step[0] == "m":
                    g = int(step[1])
                    after(act, "m_filled", b, range(NG), g)
                    act.wait_ge(sem["m_kept"], upto("m_kept", b, 16 * g))
                    drain(mrow[:, :], m_bank[0:3 * G, 0:T], "m_drained")
                if step == "aT":
                    after(act, "o_filled", b, OUT, "aT")
                    drain(aT[:, :], xb, "o_drained")

            def take(b, g):
                act.wait_ge(sem["av_used"], upto("av_used", b, G * C * (g + 1)))
                if g == 0:
                    after(act, "o_filled", b - 1, OUT, "proj")
                else:
                    after(act, "o_filled", b, OUT, f"o{g - 1}")
                drain(oT[:, :], avb, "av_drained")

            def back(step, b, has_attn):
                done = "back_drained"
                if step in BACK:
                    after(act, "back_filled", b, BACK, step)
                if step == "cT":
                    drain(cT[:, :], bb, done)
                if step == "qc":
                    after(act, "qc_kept", b - 1, range(16), 15)
                    nc.scalar.activation(qcp[:, 0, :], bb, ACT.Identity, bias=col("L1_xcond_b_qc"))
                    drain(qcf[:, :], bb, done, bias=col("L1_xcond_b_qc"))
                if step == "cm":
                    act.wait_ge(sem["cm_kept"], upto("cm_kept", b - 1, 16))
                    drain(cmrow[:, :], cm_bank[0:3 * NH, 0:T], done)
                if step[:2] == "cs":
                    g = int(step[2])
                    for hh in range(G):
                        i = g * G + hh
                        act.wait_ge(sem["cs_scored"], upto("cs_scored", b, i + 1))
                        if hh == 0:
                            after(act, "back_filled", b if g else b - 1, BACK, f"cav{(g - 1) % NG}")
                        nc.scalar.activation(cpT[0:S, i % G, :], sco[0:S, i % 2, :], ACT.Exp, scale=SELF_SCALE
                                             ).then_inc(sem["cexp_done"], 1)
                if step[:3] == "cav":
                    drain(coT[:, :], bb, done)
                if step == "caT":
                    drain(caT[:, :], bb, done)
                if step == "xT":
                    drain(mT[:, :], bb, done, scale=bpar[:, B_SCM:B_SCM + 1], bias=bpar[:, B_SHM:B_SHM + 1])
                if step in ("m0", "m1", "m2", "m3"):
                    j = int(step[1])
                    if j == 0 and has_attn:
                        after(act, "front_filled", b + 2 if not isinstance(b, int) else min(b + 2, NB - 1), FRONT, "e2")
                    drain(hm[:, j, :], bb, done, bias=col("L1_xcond_b_mlp1", j))
                    if j == 3:
                        after(act, done, b, BACK, "m3")
                        flat = hm[:, :, :].rearrange("p j t -> p (j t)")
                        nc.scalar.activation(flat, flat, ACT.Gelu_apprx_tanh).then_inc(sem["gelu_done"], 1)

            def exps(b, s, pair):
                for hh in (2 * pair, 2 * pair + 1):
                    j = s * G + hh
                    act.wait_ge(sem["s_scored"], upto("s_scored", b, j + 1))
                    act.wait_ge(sem["av_used"], upto("av_used", b, j + 1 - RING))
                    nc.scalar.activation(pT[:, j % RING, :], sco[:, j % 2, :], ACT.Exp, scale=SELF_SCALE
                                         ).then_inc(sem["exp_done"], 1)

            def run(b, has_attn, has_front, has_back):
                engine = {"front": front, "attn": attn, "back": back}
                for s, places in enumerate(PLAN):
                    for n, place in enumerate(places):
                        if has_attn and n < 2:
                            exps(b, s, n)
                        if has_attn and n == 2 and s % C == 0 and s:
                            take(b, s // C - 1)
                        do_place(place, engine, b, has_attn, has_front, has_back)

            iterations(act, run)

        @block.vector
        def _(dve):
            begin(dve, ["front_vec", "nat_reduced", "m_vec", "o_vec", "v_placed", "back_vec", "cn_reduced", "co_vec"])

            def zero(ins):
                ins.then_inc(s_vzeros, 1)

            def setup(ins):
                ins.then_inc(s_vec, 1)

            zero(nc.vector.memset(fpar_all[:, :, :], 0.0))
            zero(nc.vector.memset(bpar_all[:, :, :], 0.0))
            dve.wait_ge(s_vzeros, 2)
            vc_all = bpar_all[:, :, B_VC:B_N].rearrange("p b (h n) -> p b h n", n=TILE)
            weights(dve, "ctx")
            for b in range(NB):
                ins = nc.vector.bn_stats(st[0:S, b, :], ctxn[0:S, b, :])
            setup(ins)
            drained(dve, "stats")
            for b in range(NB):
                ins = nc.vector.bn_aggr(mv[0:S, b, :], st[0:S, b, :])
            setup(ins)
            filled(dve, "cols")
            setup(nc.vector.tensor_copy(cols[:, 0:NR], fill_bank("cols")[:, 0:NR]))
            filled(dve, "ctxT")
            setup(nc.vector.tensor_copy(ctxT[:, :, :].rearrange("p b s -> p (b s)"), fill_bank("ctxT")[:, 0:NB * S]))
            dve.wait_ge(s_rstd, 2)
            drained(dve, "aggr")
            for b in range(NB):
                ins = nc.vector.tensor_scalar(ctxh[0:S, b, :], ctxn[0:S, b, :], mv[0:S, b, 0:1], rstd[0:S, b:b + 1],
                                              ALU.subtract, ALU.mult)
            setup(ins)
            drained(dve, "cols")
            setup(nc.vector.tensor_copy(condrep[:, :, :], along(col("cond_1024", 0, NB), H)))
            setup(nc.vector.tensor_copy(b2rep[:, :, :], along(col("L0_xcond_e_b2", 0, E), H)))
            filled(dve, "ctxhT")
            setup(nc.vector.tensor_copy(ctxhT[:, :, :].rearrange("p b s -> p (b s)"), fill_bank("ctxhT")[:, 0:NB * S]))
            filled(dve, "wq0T")
            setup(nc.vector.tensor_copy(wq0T[:, :], fill_bank("wq0T")[:, 0:H]))
            filled(dve, "kpT")
            setup(nc.vector.tensor_copy(kpT[:, :, :].rearrange("p b s -> p (b s)"), fill_bank("kpT")[:, 0:NB * S]))
            filled(dve, "G")
            setup(nc.vector.tensor_copy(fpar_all[:, :, F_G:F_G + S],
                                        fill_bank("G")[:, 0:NB * S].rearrange("p (b s) -> p b s", b=NB)))
            weights(dve, "w0")
            setup(nc.vector.tensor_copy(fpar_all[:, :, F_WR:F_WR + E],
                                        wr[:, 0:1, :].to_broadcast([P, NB, E])))
            filled(dve, "vp")
            setup(nc.vector.tensor_copy(fpar_all[0:S, :, F_VP:F_VP + H],
                                        fill_bank("vp")[0:S, :].rearrange("p (b h) -> p b h", b=NB)))
            filled(dve, "kc")
            setup(nc.vector.tensor_scalar(kcf[:, :], fill_bank("kc")[:, 0:NB * S], col("L1_xcond_b_kvc"), None, ALU.add))
            drained(dve, "kcf")
            setup(nc.vector.tensor_copy(kcp[:, 0, :], kcf[:, :]))
            drained(dve, "kpart1")
            setup(nc.vector.tensor_tensor(kcf[:, :], kcf[:, :], kcp[:, 0, :], ALU.subtract))
            drained(dve, "krest")
            setup(nc.vector.tensor_copy(kcp[:, 1, :], kcf[:, :]))
            drained(dve, "kpart2")
            setup(nc.vector.tensor_tensor(kcp[:, 2, :], kcf[:, :], kcp[:, 1, :], ALU.subtract))
            filled(dve, "vc")
            weights(dve, "mod")
            for b in range(NB):
                ins = nc.vector.tensor_tensor(vc_all[0:S, b, :, 0:HD],
                                              chunk(fill_bank("vc"), b)[0:S, :].rearrange("p (h d) -> p h d", d=HD),
                                              bvc[0:S, :].rearrange("p (h d) -> p h d", d=HD), ALU.add)
            setup(ins)
            filled(dve, "hb")
            setup(nc.vector.tensor_tensor(fpar_all[:, :, F_HB:F_HB + NZ],
                                          fill_bank("hb")[:, 0:NZ * NB].rearrange("p (z b) -> p b z", b=NB),
                                          over(cols[:, 0:NZ], NB), ALU.add))
            filled(dve, "rbias")
            setup(nc.vector.tensor_tensor(fpar_all[:, :, F_RB:F_RB + E],
                                          fill_bank("rbias")[:, 0:NB * E].rearrange("p (b e) -> p b e", e=E),
                                          over(rbb[:, :], NB), ALU.add))
            dve.wait_ge(s_silu, 1)
            setup(nc.vector.tensor_copy(silurep[:, :, :], along(silc[:, :], H)))
            filled(dve, "mod")
            mods = fill_bank("mod")[:, 0:4 * NB].rearrange("p (j b) -> p j b", b=NB)
            for n, (j, plus, dst) in enumerate(((0, 0.0, fpar_all[:, :, F_SHA]), (1, 1.0, fpar_all[:, :, F_SCA]),
                                                (3, 0.0, bpar_all[:, :, B_SHM]), (4, 1.0, bpar_all[:, :, B_SCM]))):
                ins = nc.vector.tensor_scalar(dst, mods[:, n, :], col("L1_xcond_b_mod", j), plus, ALU.add, ALU.add)
            setup(ins)
            for half in range(2):
                filled(dve, f"gates{half}")
                setup(nc.vector.tensor_tensor(
                    gates[:, 2 * half:2 * half + 2, :, :],
                    fill_bank(f"gates{half}").rearrange("p (b j h) -> p b j h", b=2, j=2),
                    bgates[:, :, :].unsqueeze(1).to_broadcast([P, 2, 2, H]), ALU.add))
            for step, dst, n, w in (("ew2Ta", ew2T, 4, 0), ("ew2Tb", ew2T, 2, 4), ("w2oa", w2o, 4, 0), ("w2ob", w2o, 2, 4)):
                filled(dve, step)
                setup(nc.vector.tensor_copy(dst[:, w:w + n, :].rearrange("p j h -> p (j h)"), fill_bank(step)[:, 0:n * H]))
            filled(dve, "b2o")
            weights(dve, "experts", "rest")
            setup(nc.vector.tensor_tensor(b2oB[:, :, :], fill_bank("b2o")[:, 0:E * H].rearrange("p (e h) -> p e h", e=E),
                                          over(bout, E), ALU.add))
            zero(nc.vector.memset(vS[:, :, :, :], 0.0))
            zero(nc.vector.memset(wT[2 * TILE:KP, :], 0.0))
            zero(nc.vector.memset(cpT[2 * TILE:KP, :, :], 0.0))
            zero(nc.vector.memset(qS[0:KP, :, :].bitcast(F32), 0.0))
            zero(nc.vector.memset(qcS[0:KP, :, :].bitcast(F32), 0.0))
            dve.wait_ge(s_vzeros, VZEROS - 1)
            nc.vector.memset(vc_all[:, :, :, HD], 1.0)
            zero(nc.vector.memset(vS[:, :, :, HD], 1.0))
            dve.wait_ge(s_vzeros, VZEROS)
            drained(dve, "b2o")

            def stats(src, st_, mv_, done, steps, b, name):
                for c in range(C):
                    ins = nc.vector.bn_stats(st_[:, c, :], src[:, c, :])
                ins.then_inc(sem[done], 1)
                after(dve, done, b, steps, name)
                for c in range(C):
                    ins = nc.vector.bn_aggr(mv_[:, c, :], st_[:, c, :])
                ins.then_inc(sem[done], 1)

            def normalize(out_, src, mv_, rstd_, done):
                for c in range(C):
                    ins = nc.vector.tensor_scalar(out_[:, c, :], src[:, c, :], mv_[:, c, 0:1], rstd_[:, c:c + 1],
                                                  ALU.subtract, ALU.mult)
                ins.then_inc(sem[done], 1)

            def front(step, b):
                def did(ins):
                    ins.then_inc(sem["front_vec"], 1)

                def wait(name):
                    after(dve, "front_vec", b, FRONT_VEC, name)

                if step in ("router", "gate", "e0", "e1", "e2", "v", "scores"):
                    after(dve, "front_filled", b, FRONT, step)
                if step == "ln0":
                    dve.wait_ge(sem["x_loaded"], upto("x_loaded", b, 16))
                    stats(x, st, mv, "front_vec", FRONT_VEC, b, "stats")
                if step == "nxT":
                    after(dve, "front_pool", b, FRONT_POOL, "rstd")
                    normalize(xh, x, mv, rstd, "front_vec")
                if step == "scores":
                    dve.wait_ge(sem["fpar_loaded"], upto("fpar_loaded", b, 16))
                    sc = fb[:, 0:C * (S + E)].rearrange("p (c n) -> p c n", c=C)
                    did(nc.vector.reduce_max(pm[:, 0, :], sc[:, :, 0:S], AX_X))
                    did(nc.vector.tensor_tensor(lg[:, 0, :, :], sc[:, :, S:S + E], over(fpar[:, F_RB:F_RB + E], C), ALU.add))
                    wait("pmax")
                    did(nc.vector.tensor_scalar(pm[:, 1, :], pm[:, 0, :], -PROTO_SCALE, None, ALU.mult))
                if step == "wT":
                    after(dve, "front_drained", b, FRONT, "scores")
                    did(nc.vector.reciprocal(pm[:, 3, :], pm[:, 2, :]))
                    wait("prec")
                    did(nc.vector.tensor_tensor(pw[:, :, :], pw[:, :, :], along(pm[:, 3, :], S), ALU.mult))
                if step == "router":
                    nc.vector.tensor_tensor(lg[:, 1, :, :], fb[:, 0:C * E].rearrange("p (c e) -> p c e", c=C),
                                            lg[:, 0, :, :], ALU.add).then_inc(sem["front_drained"], 1)
                    after(dve, "front_drained", b, FRONT, "router")
                    did(nc.vector.reduce_max(lm[:, 0, :], lg[:, 1, :, :], AX_X))
                    wait("lmax")
                    did(nc.vector.tensor_tensor(lg[:, 1, :, :], lg[:, 1, :, :], along(lm[:, 0, :], E), ALU.subtract))
                if step == "probs":
                    after(dve, "front_act", b, FRONT_ACT, "rexp")
                    did(nc.vector.reduce_sum(lm[:, 1, :], lg[:, 2, :, :], AX_X))
                    wait("lsum")
                    did(nc.vector.reciprocal(lm[:, 2, :], lm[:, 1, :]))
                    wait("lrec")
                    did(nc.vector.tensor_tensor(lg[:, 3, :, :], lg[:, 2, :, :], along(lm[:, 2, :], E), ALU.mult))
                if step == "gate":
                    nc.vector.tensor_tensor(gz[:, :, :], chunks(fb), over(BC["gate_b2"], C), ALU.add
                                            ).then_inc(sem["front_drained"], 1)
                if step in ("e0", "e1", "e2"):
                    e = int(step[1])
                    if e == 0:
                        after(dve, "front_pool", b, FRONT_POOL, "rb2")
                    else:
                        after(dve, "front_drained", b, FRONT, f"e{e - 1}")
                    for c in range(C):
                        ins = nc.vector.scalar_tensor_tensor(acc[:, c, :], chunk(fb, c), lg[:, 3, c, e:e + 1],
                                                             acc[:, c, :], ALU.mult, ALU.add)
                    ins.then_inc(sem["front_drained"], 1)
                if step == "ln1":
                    after(dve, "front_drained", b, FRONT, "e2")
                    after(dve, "front_act", b, FRONT_ACT, "tanh")
                    did(nc.vector.scalar_tensor_tensor(acc[:, :, :], gz[:, :, :], 1.0, acc[:, :, :], ALU.add, ALU.mult))
                    wait("gated")
                    after(dve, "attn_pool", b - 1, ATTN_POOL, "x0gb")
                    did(nc.vector.scalar_tensor_tensor(x0[:, :, :], acc[:, :, :], 0.5, x[:, :, :], ALU.mult, ALU.add))
                    wait("x0")
                    stats(x0, st, mv, "front_vec", FRONT_VEC, b, "stats1")
                if step == "xnT":
                    after(dve, "front_pool", b, FRONT_POOL, "rstd1")
                    normalize(xh, x0, mv, rstd, "front_vec")
                if step == "q":
                    after(dve, "front_drained", b, FRONT, "q")
                    did(nc.vector.tensor_tensor(qf[:, :], qf[:, :], qp[:, 0, :], ALU.subtract))
                    wait("qrest")
                    did(nc.vector.tensor_copy(qp[:, 1, :], qf[:, :]))
                    wait("qpart2")
                    did(nc.vector.tensor_tensor(qp[:, 2, :], qf[:, :], qp[:, 1, :], ALU.subtract))
                if step == "v":
                    nc.vector.tensor_tensor(vst[:, :, :, :].rearrange("p c h d -> p c (h d)"), chunks(fb),
                                            over(BC["bv"], C), ALU.add).then_inc(sem["front_drained"], 1)

            def attn(step, b):
                if step[0] == "m":
                    g = int(step[1])
                    src = mx[:, :, g * G:(g + 1) * G]
                    did = sem["m_vec"]
                    dve.wait_ge(sem["nat_reduced"], upto("nat_reduced", b, C * G * (g + 1)))
                    if g:
                        after(dve, "m_filled", b, range(NG), g - 1)
                    else:
                        after(dve, "m_filled", b - 1, range(NG), NG - 1)
                    nc.vector.tensor_scalar(mp[:, :, 0, :], src, -1.0, None, ALU.mult).then_inc(did, 1)
                    dve.wait_ge(did, upto("m_vec", b, 4 * g + 1))
                    nc.vector.scalar_tensor_tensor(mr[:, :, :], src, -1.0, mp[:, :, 0, :], ALU.mult, ALU.subtract
                                                   ).then_inc(did, 1)
                    dve.wait_ge(did, upto("m_vec", b, 4 * g + 2))
                    nc.vector.tensor_copy(mp[:, :, 1, :], mr[:, :, :]).then_inc(did, 1)
                    dve.wait_ge(did, upto("m_vec", b, 4 * g + 3))
                    nc.vector.tensor_tensor(mp[:, :, 2, :], mr[:, :, :], mp[:, :, 1, :], ALU.subtract).then_inc(did, 1)
                if step in ("o0", "o1", "o2", "o3"):
                    g = int(step[1])
                    after(dve, "o_filled", b, OUT, step)
                    bank = xb.rearrange("p (c g n) -> p c g n", c=C, g=G)
                    nc.vector.reciprocal(rec[:, :, :], bank[:, :, :, HD]).then_inc(sem["o_vec"], 1)
                    after(dve, "o_vec", b, range(NG), g)
                    nc.vector.tensor_tensor(an[:, :, g * G:(g + 1) * G, :], bank[:, :, :, 0:HD], along(rec[:, :, :], HD),
                                            ALU.mult).then_inc(sem["o_drained"], 1)
                if step == "proj":
                    after(dve, "o_filled", b, OUT, "proj")
                    after(dve, "attn_pool", b, ATTN_POOL, "x0gb")
                    after(dve, "y_stored", b - 1, range(16), 15)
                    nc.vector.tensor_tensor(x1[:, :, :], chunks(xb), x0gb[:, :, :], ALU.add).then_inc(sem["o_drained"], 1)

            def back(step, b, _):
                def did(ins):
                    ins.then_inc(sem["back_vec"], 1)

                def wait(name):
                    after(dve, "back_vec", b, BACK_VEC, name)

                done = "back_drained"
                if step == "ln1":
                    after(dve, "o_drained", b, OUT, "proj")
                    stats(x1, bst, bmv, "back_vec", BACK_VEC, b, "stats1")
                if step == "cT":
                    after(dve, "back_pool", b, BACK_POOL, "rstd1")
                    normalize(bxh, x1, bmv, brstd, "back_vec")
                if step[:2] == "cn":
                    for h in range(8 * int(step[2]), 8 * int(step[2]) + 8):
                        dve.wait_ge(sem["cn_scored"], upto("cn_scored", b, h + 1))
                        nc.vector.reduce_max(cmx[:, :, h], nat[:, h % 2, 0:C * S].rearrange("p (c s) -> p c s", c=C), AX_X
                                             ).then_inc(sem["cn_reduced"], 1)
                if step == "cm":
                    dve.wait_ge(sem["cn_reduced"], upto("cn_reduced", b, NH))
                    did(nc.vector.tensor_scalar(cmp_[:, :, 0, :], cmx[:, :, :], -1.0, None, ALU.mult))
                    wait("n1")
                    did(nc.vector.scalar_tensor_tensor(cmr[:, :, :], cmx[:, :, :], -1.0, cmp_[:, :, 0, :],
                                                       ALU.mult, ALU.subtract))
                    wait("nrest")
                    did(nc.vector.tensor_copy(cmp_[:, :, 1, :], cmr[:, :, :]))
                    wait("n2")
                    did(nc.vector.tensor_tensor(cmp_[:, :, 2, :], cmr[:, :, :], cmp_[:, :, 1, :], ALU.subtract))
                if step[:2] == "co":
                    g = int(step[2])
                    after(dve, "back_filled", b, BACK, step)
                    bank = bb.rearrange("p (c g n) -> p c g n", c=C, g=G)
                    nc.vector.reciprocal(crec[:, :, :], bank[:, :, :, HD]).then_inc(sem["co_vec"], 1)
                    after(dve, "co_vec", b, range(NG), g)
                    nc.vector.tensor_tensor(can[:, :, g * G:(g + 1) * G, :], bank[:, :, :, 0:HD], along(crec[:, :, :], HD),
                                            ALU.mult).then_inc(sem[done], 1)
                if step == "cproj":
                    after(dve, "back_filled", b, BACK, "cproj")
                    after(dve, "back_pool", b, BACK_POOL, "x1b")
                    nc.vector.tensor_tensor(x2[:, :, :], chunks(bb), x1b[:, :, :], ALU.add).then_inc(sem[done], 1)
                if step == "ln2":
                    after(dve, done, b, BACK, "cproj")
                    stats(x2, bst, bmv, "back_vec", BACK_VEC, b, "stats2")
                if step == "xT":
                    after(dve, "back_pool", b, BACK_POOL, "rstd2")
                    normalize(bxh, x2, bmv, brstd, "back_vec")
                if step == "mlp":
                    after(dve, "back_filled", b, BACK, "mlp")
                    after(dve, "back_pool", b, BACK_POOL, "x2gb")
                    nc.vector.tensor_tensor(yo[:, :, :], chunks(bb), x2gb[:, :, :], ALU.add).then_inc(sem[done], 1)

            def maxima(b, h, pair):
                for c in (2 * pair, 2 * pair + 1):
                    dve.wait_ge(sem["nat_scored"], upto("nat_scored", b, h * C + c + 1))
                    nc.vector.reduce_max(mx[:, c, h:h + 1], nat[:, c % 2, :], AX_X).then_inc(sem["nat_reduced"], 1)

            def place_v(b):
                dve.wait_ge(sem["av_used"], upto("av_used", b - 1, NH * C))
                after(dve, "front_drained", b, FRONT, "v")
                nc.vector.tensor_copy(vS[:, :, :, 0:HD].rearrange("p c h d -> p (c h) d"),
                                      vst[:, :, :, :].rearrange("p c h d -> p (c h) d")
                                      ).then_inc(sem["v_placed"], 1)

            def run(b, has_attn, has_front, has_back):
                engine = {"front": front, "attn": attn, "back": back}
                for s, places in enumerate(PLAN):
                    ahead = (b, s + LAG, has_attn) if s + LAG < NH else (b + 1, s + LAG - NH, has_front)
                    for n, place in enumerate(places):
                        if ahead[2] and n < 2:
                            maxima(ahead[0], ahead[1], n)
                        if has_attn and s == 0 and n == 2:
                            place_v(b)
                        do_place(place, engine, b, has_attn, has_front, has_back)

            iterations(dve, run)

        @block.tensor
        def _(pe):
            begin(pe, ["front_filled", "nat_scored", "s_scored", "av_used", "m_filled", "o_filled", "back_filled",
                       "cn_scored", "cs_scored"])
            mm = nc.tensor.matmul

            def transposes(out_, ins_, ident):
                rows_ = ins_[0].shape[0]
                for c, t in enumerate(ins_):
                    last = nc.tensor.transpose(out_[0:t.shape[1], c * rows_:(c + 1) * rows_], t, ident[0:rows_, 0:rows_])
                return last

            def fill(step):
                n = FILLS.index(step)
                if n >= 8:
                    drain_of = {"kc": "kcf"}.get(FILLS[n - 8], FILLS[n - 8])
                    drained(pe, drain_of)
                return fill_bank(step)

            def filled_by(ins):
                ins.then_inc(s_filled, 1)

            pe.wait_ge(s_consts, CONSTS)
            weights(pe, "rows")
            filled_by(transposes(fill("cols"), [rows[0:NR, :]], identf))
            weights(pe, "ctx")
            filled_by(transposes(fill("ctxT"), [ctxn[0:S, b, :] for b in range(NB)], identf))
            drained(pe, "ctxhat")
            filled_by(transposes(fill("ctxhT"), [ctxh[0:S, b, :] for b in range(NB)], identf))
            weights(pe, "w0")
            filled_by(transposes(fill("wq0T"), [wqkv0[:, 0, :]], identf))
            drained(pe, "ctxT")
            filled_by(mm(fill("kpT")[:, 0:NB * S], wqkv0[:, 1, :], ctxT[:, :, :].rearrange("p b s -> p (b s)"),
                         start=True, stop=True))
            drained(pe, "kpT")
            filled_by(mm(fill("G")[:, 0:NB * S], wq0T[:, :], kpT[:, :, :].rearrange("p b s -> p (b s)"),
                         start=True, stop=True))
            bank = fill("vp")
            for b in range(NB):
                ins = mm(chunk(bank, b)[0:S, :], ctxT[:, b, :], wqkv0[:, 2, :], start=True, stop=True)
            filled_by(ins)
            drained(pe, "ctxhT")
            filled_by(mm(fill("kc")[:, 0:NB * S], wkvc[:, 0:H], ctxhT[:, :, :].rearrange("p b s -> p (b s)"),
                         start=True, stop=True))
            bank = fill("vc")
            for b in range(NB):
                ins = mm(chunk(bank, b)[0:S, :], ctxhT[:, b, :], wkvc[:, H:2 * H], start=True, stop=True)
            filled_by(ins)
            weights(pe, "w1")
            bank = fill("hb")
            for zi in range(NZ):
                ins = mm(bank[:, zi * NB:(zi + 1) * NB], w1[:, 2, zi, :], col("cond_1024", 0, NB), start=True, stop=True)
            filled_by(ins)
            bank = fill("rbias")
            for b in range(NB):
                ins = mm(bank[:, b * E:(b + 1) * E], condrep[:, b, :], wr[:, 2, :], start=True, stop=True)
            filled_by(ins)
            weights(pe, "mod")
            pe.wait_ge(s_silu, 1)
            bank = fill("mod")
            for n, j in enumerate((0, 1, 3, 4)):
                ins = mm(bank[:, n * NB:(n + 1) * NB], wmod[:, j, :], silc[:, :], start=True, stop=True)
            filled_by(ins)
            drained(pe, "silurep")
            for half in range(2):
                bank = fill(f"gates{half}")
                for n in range(4):
                    ins = mm(chunk(bank, n), silurep[:, 2 * half + n // 2, :], wmod[:, (2, 5)[n % 2], :],
                             start=True, stop=True)
                filled_by(ins)
            weights(pe, "experts")
            filled_by(transposes(fill("ew2Ta"), [ew2[:, j, :] for j in range(4)], identf))
            filled_by(transposes(fill("ew2Tb"), [ew2[:, j, :] for j in (4, 5)], identf))
            for step, blocks, drain_of in (("w2oa", (0, 1, 2, 3), "ew2Ta"), ("w2ob", (4, 5), "ew2Tb")):
                drained(pe, drain_of)
                bank = fill(step)
                for n, j in enumerate(blocks):
                    ins = mm(chunk(bank, n), ew2T[:, j, :], outw[:, :], start=True, stop=True)
                filled_by(ins)
            bank = fill("b2o")
            for e in range(E):
                ins = mm(chunk(bank, e), b2rep[:, e, :], outw[:, :], start=True, stop=True)
            filled_by(ins)
            weights(pe, "rest")
            drained(pe, "b2o")
            pe.wait_ge(s_zeros, ZEROS)
            pe.wait_ge(s_vzeros, VZEROS)

            def front(step, b):
                if step not in FRONT:
                    return
                n = FRONT.index(step)
                pe.wait_ge(sem["front_drained"], upto("front_drained", b, n))
                if step in ("nxT", "xnT"):
                    after(pe, "front_vec", b, FRONT_VEC, "xhat" if step == "nxT" else "xhat1")
                    ins = transposes(fb, [xh[:, c, :] for c in range(C)], identf)
                if step == "scores":
                    pe.wait_ge(sem["fpar_loaded"], upto("fpar_loaded", b, 16))
                    for c in range(C):
                        ins = mm(fb[:, c * (S + E):(c + 1) * (S + E)], chunk(nxT, c), fpar[:, F_G:F_G + S + E],
                                 start=True, stop=True)
                if step == "wT":
                    after(pe, "front_vec", b, FRONT_VEC, "pnorm")
                    ins = transposes(fb, [pw[:, c, :] for c in range(C)], identf)
                if step == "evT":
                    ins = mm(fb, fpar[0:KP, F_VP:F_VP + H], wT[0:KP, :], start=True, stop=True)
                if step == "router":
                    for c in range(C):
                        ins = mm(fb[:, c * E:(c + 1) * E], chunk(evT, c), wr[:, 1, :], start=True, stop=True)
                if step[0] == "h":
                    mm(fb, w1[:, 0, int(step[1]), :], nxT[:, :], start=True, stop=False)
                    ins = mm(fb, w1[:, 1, int(step[1]), :], evT[:, :], start=False, stop=True)
                if step == "gate":
                    after(pe, "front_act", b, FRONT_ACT, "silu")
                    for c in range(C):
                        ins = mm(chunk(fb, c), chunk(z[:, 2 * E, :], c), gw2[:, :], start=True, stop=True)
                if step in ("e0", "e1", "e2"):
                    e = int(step[1])
                    for c in range(C):
                        for r in range(2):
                            ins = mm(chunk(fb, c), chunk(z[:, 2 * e + r, :], c), w2o[:, 2 * e + r, :],
                                     start=r == 0, stop=r == 1)
                if step in ("q", "k"):
                    ins = mm(fb, chunk(wqkv, "qk".index(step)), xnT[:, :], start=True, stop=True)
                if step == "v":
                    for c in range(C):
                        ins = mm(chunk(fb, c), chunk(xnT, c), wqkv[:, 2 * H:3 * H], start=True, stop=True)
                ins.then_inc(sem["front_filled"], 1)

            def attn(step, b):
                if step == "av":
                    weighted(b, NH - 1)
                if step[0] == "m":
                    g = int(step[1])
                    pe.wait_ge(sem["m_vec"], upto("m_vec", b, 4 * (g + 1)))
                    after(pe, "o_drained", b - 1, OUT, {0: "o2", 1: "proj"}.get(g, "o2")) if g < 2 else \
                        after(pe, "o_drained", b, OUT, f"o{g - 2}")
                    transposes(m_bank, [mp[:, c, :, :].rearrange("p s g -> p (s g)") for c in range(C)], identb
                               ).then_inc(sem["m_filled"], 1)
                if step in ("o0", "o1", "o2", "o3"):
                    g = int(step[1])
                    after(pe, "av_drained", b, range(NG), g)
                    if g < 3:
                        after(pe, "m_drained", b, range(NG), g + 1)
                    elif isinstance(b, int) and b == NB - 1:
                        after(pe, "o_drained", b, OUT, "o2")
                    else:
                        after(pe, "m_drained", b + 1, range(NG), 0)
                    transposes(xb, [chunk(oT, c) for c in range(C)], identf).then_inc(sem["o_filled"], 1)
                if step == "aT":
                    after(pe, "o_drained", b, OUT, "o3")
                    transposes(xb, [an[:, c, :, :].rearrange("p h d -> p (h d)") for c in range(C)], identf
                               ).then_inc(sem["o_filled"], 1)
                if step == "proj":
                    after(pe, "o_drained", b, OUT, "aT")
                    after(pe, "attn_pool", b, ATTN_POOL, "wpg")
                    for c in range(C):
                        ins = mm(chunk(xb, c), chunk(aT, c), wpg[:, :], start=True, stop=True)
                    ins.then_inc(sem["o_filled"], 1)

            def back(step, b, has_attn):
                if step[:2] == "cn":
                    first = 8 * int(step[2])
                    slot = CN_SLOTS[int(step[2])]
                    if first == 0:
                        pe.wait_ge(sem["qc_placed"], upto("qc_placed", b, 16 * len(PAIRS)))
                        pe.wait_ge(sem["bpar_loaded"], upto("bpar_loaded", b, per["bpar_loaded"]))
                    for h in range(first, first + 8):
                        if h < first + 2:
                            before = (b + 1, C * (slot + LAG) + 3 + h - first) if has_attn else (b, NH * C)
                            pe.wait_ge(sem["nat_reduced"], upto("nat_reduced", *before))
                        if h >= 2:
                            pe.wait_ge(sem["cn_reduced"], upto("cn_reduced", b, h - 1))
                        for c in range(C):
                            ins = mm(nat[:, h % 2, c * S:(c + 1) * S], chunk(qcS[:, h, :], c), kcS[:, h, :],
                                     start=True, stop=True)
                        ins.then_inc(sem["cn_scored"], 1)
                    return
                if step[:2] == "cs":
                    g = int(step[2])
                    slot = CS_SLOTS[g // 2]
                    if g == 0:
                        pe.wait_ge(sem["cm_placed"], upto("cm_placed", b, 16))
                    for h in range(g * G, g * G + G):
                        if g % 2 == 0 and h < g * G + 2:
                            before = (b + 1, G * slot + 3 + h - g * G) if has_attn else (b, NH * C)
                            pe.wait_ge(sem["exp_done"], upto("exp_done", *before))
                        if h >= 2:
                            pe.wait_ge(sem["cexp_done"], upto("cexp_done", b, h - 1))
                        mm(sco[0:S, h % 2, :], kcS[:, h, :], qcS[:, h, :], start=True, stop=True
                           ).then_inc(sem["cs_scored"], 1)
                    return
                if step not in BACK:
                    return
                n = BACK.index(step)
                pe.wait_ge(sem["back_drained"], upto("back_drained", b, n))
                if step == "cT":
                    after(pe, "back_vec", b, BACK_VEC, "xhat1")
                    ins = transposes(bb, [bxh[:, c, :] for c in range(C)], identf)
                if step == "qc":
                    ins = mm(bb, wqc[:, :], cT[:, :], start=True, stop=True)
                if step == "cm":
                    after(pe, "back_vec", b, BACK_VEC, "n3")
                    ins = transposes(cm_bank, [cmp_[:, c, :, :].rearrange("p s h -> p (s h)") for c in range(C)], identb)
                if step[:3] == "cav":
                    g = int(step[3])
                    for hh in range(G):
                        h = g * G + hh
                        pe.wait_ge(sem["cexp_done"], upto("cexp_done", b, h + 1))
                        ins = mm(bb[TILE * hh:TILE * (hh + 1), :], bpar[0:KP, B_VC + h * TILE:B_VC + (h + 1) * TILE],
                                 cpT[:, h % G, :], start=True, stop=True)
                if step in ("co0", "co1", "co2", "co3"):
                    ins = transposes(bb, [chunk(coT, c) for c in range(C)], identf)
                if step == "caT":
                    ins = transposes(bb, [can[:, c, :, :].rearrange("p h d -> p (h d)") for c in range(C)], identf)
                if step == "cproj":
                    for c in range(C):
                        ins = mm(chunk(bb, c), chunk(caT, c), wcproj[:, :], start=True, stop=True)
                if step == "xT":
                    after(pe, "back_vec", b, BACK_VEC, "xhat2")
                    ins = transposes(bb, [bxh[:, c, :] for c in range(C)], identf)
                if step in ("m0", "m1", "m2", "m3"):
                    ins = mm(bb, chunk(wm1, int(step[1])), mT[:, :], start=True, stop=True)
                if step == "mlp":
                    after(pe, "gelu_done", b, range(1), 0)
                    after(pe, "back_pool", b, BACK_POOL, "gbm")
                    for c in range(C):
                        for j in range(4):
                            ins = mm(chunk(bb, c), chunk(hm[:, j, :], c), w2g[:, j, :], start=j == 0, stop=j == 3)
                ins.then_inc(sem["back_filled"], 1)

            def natural(b, h, pair, s, has_back, it):
                if h % (NH // 2) == 0 and pair == 0:
                    half = h // (NH // 2)
                    pe.wait_ge(sem[f"half{half}"], upto(f"half{half}", b, 16 * HALF))
                for c in (2 * pair, 2 * pair + 1):
                    pe.wait_ge(sem["nat_reduced"], upto("nat_reduced", b, h * C + c - 1))
                    if has_back and pair == 0 and s - 1 in CN_SLOTS:
                        pe.wait_ge(sem["cn_reduced"], upto("cn_reduced", it - 1, 8 * (s - CN_SLOTS[0]) - 1 + c))
                    mm(nat[:, c % 2, :], chunk(qS[:, h, :], c), kS[:, h, :], start=True, stop=True
                       ).then_inc(sem["nat_scored"], 1)

            def scores(b, s, pair, has_back):
                g, kc = divmod(s, C)
                if kc == 0 and pair == 0:
                    pe.wait_ge(sem["m_placed"], upto("m_placed", b, 16 * (g + 1)))
                for hh in (2 * pair, 2 * pair + 1):
                    j, h = s * G + hh, g * G + hh
                    pe.wait_ge(sem["exp_done"], upto("exp_done", b, j - 1))
                    if has_back and pair == 0 and s - 1 in CS_SLOTS:
                        pe.wait_ge(sem["cexp_done"], upto("cexp_done", b - 1, 8 * (s - CS_SLOTS[0]) - 1 + hh))
                    mm(sco[:, j % 2, :], chunk(kS[:, h, :], kc), qS[:, h, :], start=True, stop=True
                       ).then_inc(sem["s_scored"], 1)

            def weighted(b, s):
                g, kc = divmod(s, C)
                if s == 0:
                    pe.wait_ge(sem["v_placed"], upto("v_placed", b, 1))
                if kc == 0:
                    pe.wait_ge(sem["av_drained"], upto("av_drained", b, g))
                for hh in range(G):
                    j = s * G + hh
                    pe.wait_ge(sem["exp_done"], upto("exp_done", b, j + 1))
                    mm(avb[TILE * hh:TILE * (hh + 1), :], vS[:, kc, g * G + hh, :], pT[:, j % RING, :],
                       start=kc == 0, stop=kc == C - 1).then_inc(sem["av_used"], 1)

            def run(b, has_attn, has_front, has_back):
                engine = {"front": front, "attn": attn, "back": back}
                for s, places in enumerate(PLAN):
                    ahead = (b, s + LAG, has_attn) if s + LAG < NH else (b + 1, s + LAG - NH, has_front)
                    for n, place in enumerate(places):
                        if has_attn and n < 2:
                            scores(b, s, n, has_back)
                        if ahead[2] and n < 2:
                            natural(ahead[0], ahead[1], n, s, has_back, b)
                        if has_attn and n == 2 and s:
                            weighted(b, s - 1)
                        do_place(place, engine, b, has_attn, has_front, has_back)

            iterations(pe, run)


_INS = ["x", "cond_1024", "ctx_1024"] + [f"L0_xcond_{n}" for n in (
    "ln_gamma", "ln_beta", "Wq", "Wk", "Wv", "router_W", "router_b", "e_w1", "e_b1", "e_w2", "e_b2", "gate_w1",
    "gate_b1", "gate_w2", "gate_b2", "out_w", "out_b")] + [f"L1_xcond_{n}" for n in (
        "W_mod", "b_mod", "W_qkv", "b_qkv", "W_proj", "b_proj", "W_qc", "b_qc", "W_kvc", "b_kvc", "W_cproj",
        "b_cproj", "W_mlp1", "b_mlp1", "W_mlp2", "b_mlp2")]


def kernel(**inputs):
    import numpy as _np
    import concourse.bacc as _bacc
    from concourse.bass_utils import run_bass_kernel_spmd as _run

    nc = _bacc.Bacc("TRN2", target_bir_lowering=False, num_devices=1)
    arrays, args = {}, {}
    for name in _INS:
        t = _np.ascontiguousarray(inputs[name])
        arrays[f"in_{name}"] = t
        args[name] = nc.dram_tensor(f"in_{name}", t.shape, mybir.dt.from_np(t.dtype), kind="ExternalInput").ap()
    out = nc.dram_tensor("out", (NB, T, H), F32, kind="ExternalOutput").ap()
    build(nc, args, out)
    r = _run(nc, [arrays], core_ids=[0])
    return r.results[0]["out"]
```

```python
from contextlib import ExitStack

import concourse.bass as bass
from concourse import mybir

ALU = mybir.AluOpType
ACT = mybir.ActivationFunctionType
AX_X = mybir.AxisListType.X
F32 = mybir.dt.float32
BF16 = mybir.dt.bfloat16

P = 128
NB = 4
C = 4
T = C * P
H = 128
S = 77
NH = 16
HD = H // NH
E = 3
G = 4
NG = NH // G
TILE = 32
KP = 96
SP_ = 96
ROW_M = 64
NZ = 7
PAIRS = [(0, 2), (1, 1), (2, 0), (0, 1), (1, 0), (0, 0)]
RUNS = [(0, 3, 0, 0), (3, 5, 0, 1), (5, 6, 0, 2)]
LO, MID, HI = 0, 1, 2
SELF_SCALE = float(HD) ** -0.5
PROTO_SCALE = float(H) ** -0.5
LAG = 6
RING = 8

F_G, F_WR, F_VP, F_HB, F_SHA, F_SCA, F_RB, F_N = 0, S, S + E, S + E + H, S + E + H + NZ, S + E + H + NZ + 1, \
    S + E + H + NZ + 2, S + E + H + NZ + 2 + E
HIDDEN = [2 * E] + list(range(2 * E))
B_SHM, B_SCM, B_VC, B_N = 0, 1, 2, 2 + NH * TILE

LOADS = {
    "w_first": {"Wq Wk Wv": 3 * H, "router_W": 3 * E, "W_kvc": 2 * H},
    "w_hidden": {"w1": 3 * NZ * H},
    "w_mod": {"W_mod": 6 * H},
    "w_experts": {"e_w2": 2 * E * H, "out_w": H},
    "w_front": {"gate_w2": H, "W_qkv": 3 * H},
    "w_back": {"W_proj": H, "W_qc": H, "W_cproj": H, "W_mlp1": 4 * H, "W_mlp2": 4 * H},
    "over_setup": {"router_b": E, "b_kvc v": H, "b_mod gates": 2 * H, "out_b": H},
    "over_front": {"gate_b2": H, "b_qkv v": H},
    "over_back": {"b_proj": H, "b_cproj": H, "b_mlp2": H},
}
WIDTHS = {load: sum(parts.values()) for load, parts in LOADS.items()}
ROWS = ["b1"] + (NZ - 1) * [""] + ["gamma", "beta", "b_mod"] + 5 * [""] + ["b_q", "b_k", "b_qc", "b_kc", "b_mlp1"] + \
    3 * [""] + ["cond"] + (NB - 1) * [""] + ["e_b2"] + (E - 1) * [""]

FRONT = ["nxT", "scores", "wT", "evT", "router", "h0", "h1", "h2", "h3", "h4", "gate", "e0", "h5", "h6", "e1", "e2",
         "xnT", "k", "q", "v"]
FRONT_LOOSE = ["h1", "h2", "h3", "h4", "e0", "h6", "e2", "q"]
BACK_LOOSE = ["m1", "m2", "m3"]
BACK = ["cT", "qc", "cm"] + [f"{w}{g}" for g in range(NG) for w in ("cav", "co")] + \
    ["caT", "cproj", "xT", "m0", "m1", "m2", "m3", "mlp"]
OUT = ["o0", "o1", "o2", "o3", "aT", "proj"]

PLAN = {
    "T": """
        . | f:h1 | t:av
        t:o3 l:xT | l:m0 | t:aT l:m1
        l:m2 f:h2 | l:m3 t:proj | f:h3 a:m1
        f:h4 | l:mlp f:gate | f:e0
        f:h5 b:cT | f:h6 | .
        a:o0 b:qc | f:e1 | f:e2
        . | a:m2 | .
        f:xnT | f:k | b:cn0 b:cn1 b:cn2 b:cn3
        . | f:q b:cn4 b:cn5 b:cn6 b:cn7 | a:o1
        b:cm | . | f:v
        a:m3 | b:cs0 | b:cs1 e:nxT
        b:cav0 b:cs2 e:scores | b:cs3 | .
        b:co0 | . | .
        a:o2 b:cav1 | b:cs4 | e:wT b:cs5 b:co1
        n:m0 e:evT | b:cav2 b:cs6 b:cs7 b:co2 | b:cav3
        b:co3 e:router | b:caT | b:cproj e:h0
        """,
    "V": """
        l:ln2 | f:h1 | l:xT
        t:o3 | . | .
        f:h2 a:m1 | t:proj | f:h3
        . | b:ln1 l:mlp | f:h4 f:gate f:e0 b:cT
        f:h5 | f:h6 | .
        a:o0 f:h7 | . | f:e1 f:e2
        a:m2 f:ln1 | . | f:xnT
        . | b:cn0 b:cn1 b:cn2 b:cn3 | .
        . | f:q b:cn4 b:cn5 b:cn6 b:cn7 | b:cm
        a:o1 e:ln0 | a:m3 | f:v
        . | e:nxT | .
        . | . | .
        b:co0 e:scores | . | .
        e:wT a:o2 | n:m0 | b:co1
        . | b:co2 | .
        b:co3 e:router | e:probs | b:cproj
        """,
    "A": """
        f:h0 | f:h1 | t:av
        l:xT | l:m0 t:aT | l:m1
        l:m2 f:h2 | l:m3 | a:m1 f:h3
        f:h4 | . | f:gate
        f:h5 b:cT | f:h6 | .
        b:qc f:h7 | . | .
        . | a:m2 | .
        f:xnT | f:k | .
        . | f:q | .
        b:cm | . | .
        a:m3 | . | b:cs0 b:cs1 e:nxT
        b:cav0 b:cs2 | b:cs3 | .
        . | e:scores | .
        b:cav1 | b:cs4 e:wT | b:cs5
        n:m0 | b:cav2 e:evT b:cs6 b:cs7 b:cav3 | .
        e:router | b:caT | .
        """,
    "G": """
        l:ln2 | . | f:probs l:xT
        . | . | .
        . | . | .
        . | b:ln1 | .
        . | . | .
        . | . | .
        . | b:qc | .
        . | f:ln1 f:k | .
        . | . | .
        . | . | .
        . | e:ln0 | .
        . | . | .
        . | . | .
        . | . | .
        . | . | .
        . | . | b:caT
        """,
    "S": """
        . | . | .
        . | . | .
        . | . | .
        . | b:ln1 | a:m1
        . | l:mlp | .
        . | b:qc | e:load
        . | a:m2 | .
        f:k | . | f:q
        . | . | .
        . | b:cm | .
        . | . | a:m3
        . | . | .
        . | . | .
        . | . | .
        . | . | .
        n:m0 | . | .
        """,
}
PLANS = {letter: [[place.replace(".", "").split() for place in line.split("|")] for line in text.split("\n") if line.strip()]
         for letter, text in PLAN.items()}
EARLY = [entry[2:] for places in PLANS["T"] for place in places for entry in place if entry[0] == "e"]
FIRST = ["load", "ln0", "nxT", "scores", "wT", "evT", "router"]
PAIR = 2


def do_place(plan, engine, b):
    for entry in plan:
        chain, step = entry.split(":")
        batch = b + {"e": 2, "f": 1, "n": 1, "a": 0, "t": -1, "b": -1, "l": -2}[chain]
        if not 0 <= batch < NB or batch == 0 and chain in "ef" and step in FIRST:
            continue
        if chain in "ef":
            engine["front"](step, batch)
        elif chain in "nat":
            engine["attn"](step, batch)
        else:
            engine["back"](step, batch, batch < NB - 1)


def iterations(run):
    for b in range(-2, NB + 2):
        run(b, has_attn=0 <= b < NB, has_front=0 <= b + 1 < NB, has_back=0 <= b - 1 < NB)


def build(nc, a, out):
    ctx = ExitStack()
    with ctx:
        def sb(name, shape, dt=F32):
            return ctx.enter_context(nc.sbuf_tensor(name, shape, dt))

        w_first = sb("w_first", [P, WIDTHS["w_first"]])
        w_hidden = sb("w_hidden", [P, WIDTHS["w_hidden"]])
        w_front = sb("w_front", [P, WIDTHS["w_front"]])
        w_back = sb("w_back", [P, WIDTHS["w_back"]])
        over_front = sb("over_front", [P, WIDTHS["over_front"]])
        over_back = sb("over_back", [P, WIDTHS["over_back"]])
        w2o = sb("w2o", [P, 2 * E, H])
        cols = sb("cols", [P, len(ROWS)])
        b2oB = sb("b2oB", [P, E, H])
        identf = sb("identf", [P, P])
        identb = sb("identb", [P, P], BF16)
        minus_half = sb("minus_half", [P, C])
        fpar_all = sb("fpar_all", [P, NB, F_N])
        bpar_all = sb("bpar_all", [P, NB, B_N])
        gates = sb("gates", [P, NB, 2, H])
        x = sb("x", [P, C, H])
        st = sb("st", [P, C, 6])
        mv = sb("mv", [P, C, 2])
        rstd = sb("rstd", [P, C])
        xh = sb("xh", [P, C, H])
        nxT = sb("nxT", [P, T])
        pm = sb("pm", [P, 4, C])
        pw = sb("pw", [P, C, S])
        lg = sb("lg", [P, 4, C, E])
        lm = sb("lm", [P, 3, C])
        wT = sb("wT", [P, T])
        evT = sb("evT", [P, T])
        z = sb("z", [P, NZ, T])
        th = sb("th", [P, 2, T])
        gz = sb("gz", [P, C, H])
        acc = sb("acc", [P, C, H])
        rb = acc
        rt = gz
        x0 = sb("x0", [P, C, H])
        xnT = nxT
        qf = sb("qf", [P, T])
        kf = sb("kf", [P, T])
        qp = sb("qp", [P, 3, T], BF16)
        kp = sb("kp", [P, 3, T], BF16)
        vst = sb("vst", [P, C, NH, HD])
        qS = sb("qS", [KP, NH, T], BF16)
        kS = sb("kS", [KP, NH, T], BF16)
        vS = sb("vS", [P, C, NH, TILE])
        mx = sb("mx", [P, C, NH])
        mr = sb("mr", [P, C, G])
        mp = sb("mp", [P, C, 3, G], BF16)
        mrow = sb("mrow", [3 * G, T], BF16)
        pT = sb("pT", [P, RING, T])
        oT = sb("oT", [P, T])
        rec = sb("rec", [P, C, G])
        an = sb("an", [P, C, NH, HD])
        aT = oT
        wpg = sb("wpg", [P, H])
        gbp = sb("gbp", [P, H])
        kcS = sb("kcS", [KP, NH, S], BF16)
        x1_two = sb("x1", [P, 2, C, H])
        bst = sb("bst", [P, C, 6])
        bmv = sb("bmv", [P, C, 2])
        brstd = sb("brstd", [P, C])
        bxh = sb("bxh", [P, C, H])
        cT = sb("cT", [P, T])
        coT = caT = mT = cT
        qcf = qf
        qcp = sb("qcp", [P, 3, T], BF16)
        qcS = sb("qcS", [KP, NH, T], BF16)
        cmx = sb("cmx", [P, C, NH])
        cmr = sb("cmr", [P, C, NH])
        cmp_ = sb("cmp", [P, C, 3, NH], BF16)
        cmrow = sb("cmrow", [3 * NH, T], BF16)
        cpT = sb("cpT", [SP_, G, T])
        crec = sb("crec", [P, C, G])
        can = sb("can", [P, C, NH, HD])
        hm = sb("hm", [P, 4, T])
        w2g = sb("w2g", [P, 4, H])
        gbm = sb("gbm", [P, H])
        spare = {"pT": [pT[:, :, :].rearrange("p r t -> p (r t)"), 0], "z": [z[:, :, :].rearrange("p z t -> p (z t)"), 0]}

        def within(where, *shape):
            n = 1
            for d in shape:
                n *= d
            t = spare[where][0][:, spare[where][1]:spare[where][1] + n]
            spare[where][1] += n
            return t.rearrange("p (j n) -> p j n", j=shape[0]) if len(shape) == 2 else t

        ew2T = within("pT", 2 * E, H)
        condrep, silurep = within("pT", NB, H), within("pT", NB, H)
        b2rep, ctxn = within("pT", E, H), within("pT", NB, H)
        ctxh, ctxT, ctxhT, kpT = within("z", NB, H), within("z", NB, S), within("pT", NB, S), within("z", NB, S)
        kcf, wq0T, silc = within("z", NB * S), within("z", H), within("z", NB)
        w_mod, over_setup = within("z", WIDTHS["w_mod"]), within("z", WIDTHS["over_setup"])
        rows, w_experts = within("pT", H), within("pT", WIDTHS["w_experts"])

        def part(name, *shape):
            for load, parts in LOADS.items():
                if name in parts:
                    at = sum(list(parts.values())[:list(parts).index(name)])
                    n = parts[name]
                    t = {"w_first": w_first, "w_hidden": w_hidden, "w_mod": w_mod, "w_experts": w_experts,
                         "w_front": w_front, "w_back": w_back, "over_setup": over_setup, "over_front": over_front,
                         "over_back": over_back}[load][:, at:at + n]
            return {1: lambda: t, 2: lambda: t.rearrange("p (j n) -> p j n", j=shape[0]),
                    3: lambda: t.rearrange("p (k j n) -> p k j n", k=shape[0], j=shape[1])}[len(shape)]()

        wqkv0, wr, wkvc = part("Wq Wk Wv", 3, H), part("router_W", 3, E), part("W_kvc", 2 * H)
        w1 = part("w1", 3, NZ, H)
        wmod, ew2, outw = part("W_mod", 6, H), part("e_w2", 2 * E, H), part("out_w", H)
        gw2, wqkv, wproj, wqc = part("gate_w2", H), part("W_qkv", 3 * H), part("W_proj", H), part("W_qc", H)
        wcproj, wm1, wm2 = part("W_cproj", H), part("W_mlp1", 4 * H), part("W_mlp2", 4, H)
        rbb, bvc, bgates, bout = part("router_b", E), part("b_kvc v", H), part("b_mod gates", 2, H), part("out_b", H)
        BC = {"gate_b2": part("gate_b2", H), "bv": part("b_qkv v", H), "bproj": part("b_proj", H),
              "bcproj": part("b_cproj", H), "bm2": part("b_mlp2", H)}
        kcp = within("z", 3 * NB * S // 2).bitcast(BF16).rearrange("p (j n) -> p j n", j=3)
        q_dram = nc.dram_tensor("q_parts", (3, P, T), BF16, kind="Internal").ap()
        k_dram = nc.dram_tensor("k_parts", (3, P, T), BF16, kind="Internal").ap()
        qc_dram = nc.dram_tensor("qc_parts", (3, P, T), BF16, kind="Internal").ap()
        m_dram = nc.dram_tensor("m_parts", (3 * G, T), BF16, kind="Internal").ap()
        cm_dram = nc.dram_tensor("cm_parts", (3 * NH, T), BF16, kind="Internal").ap()
        kc_dram = nc.dram_tensor("kc_parts", (3, P, NB * S), BF16, kind="Internal").ap()

        ps = ctx.enter_context(nc.psum_tensor("ps", [P, 8, T], F32))
        nat, sco, avb = ps[:, 0:2, :], ps[:, 2:4, :], ps[:, 4, :]
        xb, chain_banks = ps[:, 5, :], ps[:, 6:8, :]

        def front_alternates(step, b):
            return b <= (2 if step in EARLY else 1)

        def front_bank(step, b):
            return chain_banks[:, FRONT.index(step) % 2 if front_alternates(step, b) else 0, :]

        def back_bank(step, b):
            return chain_banks[:, (BACK.index(step) + 1) % 2 if b >= NB - 2 else 1, :]

        def cross_tile(h, has_attn):
            return cpT[:, h % G, :] if has_attn or h < G else pT[:, h % RING, :]

        FRONT_VEC = ["stats", "aggr", "xhat", "pmax", "lg0", "pneg", "prec", "pnorm", "lmax", "lsub", "lsum", "lrec",
                     "probs"] + [f"silu{z}" for z in range(NZ)] + ["gated", "x0", "stats1", "aggr1", "xhat1", "qrest", "qpart2", "q_parts"]
        FRONT_POOL = ["eps", "rstd", "rb0", "rt1", "rb1", "rt2", "rb2", "eps1", "rstd1", "krest", "kpart2", "k_parts"]
        FRONT_ACT = ["rexp"] + [f"tanh{z}" for z in range(4)] + ["gate"] + [f"tanh{z}" for z in range(4, NZ)]
        BACK_VEC = ["stats1", "aggr1", "xhat1", "n1", "nrest", "n2", "n3", "stats2", "aggr2", "xhat2"]
        BACK_POOL = ["eps1", "rstd1", "qrest", "qpart2", "qc_parts", "x1b", "w2g", "gbm", "eps2", "rstd2", "x2gb"]
        ATTN_POOL = ["wpg", "gbp", "x0gb"]
        HALF = 2 * len(RUNS) + 1

        per = {
            "x_loaded": 16, "q_kept": 16, "k_kept": 16, "half0": 16 * HALF, "half1": 16 * HALF,
            "front_filled": len(FRONT), "front_drained": len(FRONT), "front_vec": len(FRONT_VEC),
            "front_pool": len(FRONT_POOL), "front_act": len(FRONT_ACT),
            "nat_scored": NH * C, "nat_reduced": NH * C, "s_scored": NH * C, "exp_done": NH * C, "av_used": NH * C,
            "av_drained": NG, "m_vec": 4 * NG, "m_filled": NG, "m_drained": NG, "m_kept": 16 * NG,
            "m_placed": 16 * NG, "o_filled": len(OUT), "o_drained": len(OUT), "o_vec": NG, "v_placed": 1,
            "attn_pool": len(ATTN_POOL), "kc_placed": 16 * (2 + len(RUNS)), "back_filled": len(BACK),
            "back_drained": len(BACK), "back_vec": len(BACK_VEC), "back_pool": len(BACK_POOL), "qc_kept": 16,
            "qc_placed": 16 * len(RUNS), "cn_scored": NH, "cn_reduced": NH, "cm_kept": 16, "cm_placed": 16,
            "cs_scored": NH, "cexp_done": NH, "gelu_done": 1, "co_vec": NG, "y_stored": 16,
        }
        sem = {name: ctx.enter_context(nc.semaphore(name)) for name in per}

        def upto(name, b, k):
            return (b + 1) * per[name] + k

        def begin(engine, names):
            for name in names:
                engine.sem_inc(sem[name], per[name])

        def after(engine, name, b, steps, step):
            engine.wait_ge(sem[name], upto(name, b, steps.index(step) + 1))

        FILLS = ["cols", "ctxT", "ctxhT", "wq0T", "kpT", "G", "vp", "kc", "vc", "hb", "rbias", "mod", "gates0",
                 "gates1", "ew2Ta", "ew2Tb", "w2oa", "w2ob", "b2o"]
        SETUP_VEC = ["stats", "aggr", "cols", "ctxT", "ctxhat", "condrep", "b2rep", "ctxhT", "wq0T", "kpT", "G",
                     "wr", "vp", "kcf", "kpart1", "krest", "kpart2", "kc_parts", "vc", "hb", "rbias", "silurep",
                     "mod", "gates0", "gates1", "ew2Ta", "ew2Tb", "w2oa", "w2ob", "b2o"]
        s_filled = ctx.enter_context(nc.semaphore("setup_filled"))
        s_vec = ctx.enter_context(nc.semaphore("setup_vec"))
        s_silu = ctx.enter_context(nc.semaphore("setup_silu"))
        s_rstd = ctx.enter_context(nc.semaphore("setup_rstd"))
        s_consts = ctx.enter_context(nc.semaphore("constants_ready"))
        s_zeros = ctx.enter_context(nc.semaphore("zeros_ready"))
        s_vzeros = ctx.enter_context(nc.semaphore("vector_zeros_ready"))
        s_azeros = ctx.enter_context(nc.semaphore("scalar_zeros_ready"))
        kc_kept = ctx.enter_context(nc.semaphore("kc_kept"))
        SETUP_BANKS = 6
        CONSTS, ZEROS = 5, 6
        VZEROS = 5

        def filled(engine, step):
            engine.wait_ge(s_filled, FILLS.index(step) + 1)

        def drained(engine, step):
            engine.wait_ge(s_vec, SETUP_VEC.index(step) + 1)

        def fill_bank(step):
            return ps[:, FILLS.index(step) % SETUP_BANKS, :]

        loads = {
            "ctx": [(ctxn[0:S, :, :], a["ctx"].rearrange("b s h -> s b h"))],
            "rows": [(rows[0:len(ROWS), :], a["rows"])],
            "w0": [(w_first[:, :], a["w_first"])],
            "w1": [(w_hidden[:, :], a["w_hidden"])],
            "mod": [(over_setup, a["over_setup"].partition_broadcast(P)), (w_mod, a["w_mod"])],
            "experts": [(w_experts, a["w_experts"])],
            "front": [(over_front[:, :], a["over_front"].partition_broadcast(P)), (w_front[:, :], a["w_front"])],
            "rest": [(over_back[:, :], a["over_back"].partition_broadcast(P)), (w_back[:, :], a["w_back"])],
        }
        loaded = {w: ctx.enter_context(nc.semaphore(f"loaded_{w}")) for w in loads}

        def col(name, j=0, n=1):
            at = ROWS.index(name) + j
            return cols[:, at:at + n]

        def weights(engine, *when):
            for w in when:
                engine.wait_ge(loaded[w], 16 * len(loads[w]))

        def over(t, n):
            return t.unsqueeze(1).to_broadcast([t.shape[0], n, t.shape[1]])

        def along(t, n):
            return t.unsqueeze(len(t.shape)).to_broadcast([*t.shape, n])

        def chunk(t, c):
            return t[:, c * P:(c + 1) * P]

        def chunks(t):
            return t.rearrange("p (c h) -> p c h", c=C)

        m_bank = xb.bitcast(BF16)

        block = ctx.enter_context(nc.Block())

        @block.sync
        def _(sp):
            begin(sp, ["x_loaded", "q_kept", "k_kept", "half0", "half1", "m_kept", "m_placed",
                       "kc_placed", "qc_kept", "qc_placed", "cm_kept", "cm_placed", "y_stored"])

            def keep_context():
                drained(sp, "kc_parts")
                sp.dma_start(kc_dram.rearrange("j p n -> p j n"), kcp[:, :, :]).then_inc(kc_kept, 16)

            def run_of(parts, first, n):
                return parts[first:first + n].rearrange("j (d h) n -> (j d) h n", h=NH)

            def place_half(b, half):
                heads = slice(half * NH // 2, (half + 1) * NH // 2)
                if b == 0:
                    sp.wait_ge(s_zeros, ZEROS)
                    sp.wait_ge(s_vzeros, VZEROS)
                    sp.wait_ge(kc_kept, 16)
                sp.wait_ge(sem["s_scored"], upto("s_scored", b - 1, NH * C // 2 * (half + 1)))
                sp.wait_ge(sem["q_kept"], upto("q_kept", b, 16))
                sp.wait_ge(sem["k_kept"], upto("k_kept", b, 16))
                done = sem[f"half{half}"]
                for first, last, qpart, kpart in RUNS:
                    rows_t = slice(HD * first, HD * last)
                    sp.dma_start(qS[rows_t, heads, :], run_of(q_dram, qpart, last - first)[:, heads, :]
                                 ).then_inc(done, 16)
                    sp.dma_start(kS[rows_t, heads, :], run_of(k_dram, kpart, last - first)[:, heads, :]
                                 ).then_inc(done, 16)
                sp.dma_start(qS[ROW_M:ROW_M + 3, heads, :], kS[KP - 3:KP, 0:NH // 2, :]
                             ).then_inc(done, 16)

            def front(step, b):
                if step == "load":
                    after(sp, "front_vec", b - 1, FRONT_VEC, "x0")
                    sp.dma_start(x[:, :, :], a["x"][bass.ds(b, 1)].rearrange("o (p c) h -> p (o c) h", c=C)
                                 ).then_inc(sem["x_loaded"], 16)
                if step == "k":
                    after(sp, "front_pool", b, FRONT_POOL, "k_parts")
                    sp.wait_ge(sem["half1"], upto("half1", b - 1, 16 * HALF))
                    sp.dma_start(k_dram.rearrange("j p n -> p j n"), kp[:, :, :]).then_inc(sem["k_kept"], 16)
                if step == "q":
                    after(sp, "front_vec", b, FRONT_VEC, "q_parts")
                    sp.dma_start(q_dram.rearrange("j p n -> p j n"), qp[:, :, :]).then_inc(sem["q_kept"], 16)
                    place_half(b, 0)

            def attn(step, b):
                if step[0] == "m":
                    g = int(step[1])
                    after(sp, "m_drained", b, range(NG), g)
                    sp.wait_ge(sem["m_placed"], upto("m_placed", b, 16 * g))
                    sp.dma_start(m_dram, mrow[:, :]).then_inc(sem["m_kept"], 16)
                    sp.wait_ge(sem["m_kept"], upto("m_kept", b, 16 * (g + 1)))
                    sp.dma_start(qS[ROW_M:ROW_M + 3, g * G:g * G + G, :], m_dram.rearrange("(s h) n -> s h n", s=3)
                                 ).then_inc(sem["m_placed"], 16)

            def back(step, b, _):
                if step == "ln1":
                    sp.wait_ge(sem["cs_scored"], upto("cs_scored", b - 1, NH))
                    for first, last, _, kpart in RUNS:
                        sp.dma_start(kcS[HD * first:HD * last, :, :],
                                     run_of(kc_dram, kpart, last - first)[:, :, b * S:(b + 1) * S]
                                     ).then_inc(sem["kc_placed"], 16)
                    for half in range(2):
                        sp.dma_start(qcS[ROW_M:ROW_M + 3, half * NH // 2:(half + 1) * NH // 2, :],
                                     kS[KP - 3:KP, 0:NH // 2, :]
                                     ).then_inc(sem["kc_placed"], 16)
                if step == "qc":
                    after(sp, "back_pool", b, BACK_POOL, "qc_parts")
                    sp.dma_start(qc_dram.rearrange("j p n -> p j n"), qcp[:, :, :]).then_inc(sem["qc_kept"], 16)
                    sp.wait_ge(sem["qc_kept"], upto("qc_kept", b, 16))
                    for first, last, qpart, _ in RUNS:
                        sp.dma_start(qcS[HD * first:HD * last, :, :], run_of(qc_dram, qpart, last - first)
                                     ).then_inc(sem["qc_placed"], 16)
                if step == "cm":
                    after(sp, "back_drained", b, BACK, "cm")
                    sp.dma_start(cm_dram, cmrow[:, :]).then_inc(sem["cm_kept"], 16)
                    sp.wait_ge(sem["cm_kept"], upto("cm_kept", b, 16))
                    sp.dma_start(qcS[ROW_M:ROW_M + 3, :, :], cm_dram.rearrange("(s h) n -> s h n", s=3)
                                 ).then_inc(sem["cm_placed"], 16)
                if step == "mlp":
                    after(sp, "back_drained", b, BACK, "mlp")
                    sp.dma_start(out[bass.ds(b, 1)].rearrange("o (p c) h -> p (o c) h", c=C), x1_two[:, b % 2, :, :]
                                 ).then_inc(sem["y_stored"], 16)

            def run(b, has_attn, has_front, has_back):
                if has_attn:
                    place_half(b, 1)
                for places in PLANS["S"]:
                    for place in places:
                        do_place(place, {"front": front, "attn": attn, "back": back}, b)

            for w, pairs in loads.items():
                for dst, src in pairs:
                    sp.dma_start(dst, src).then_inc(loaded[w], 16)
                if w == "w0":
                    front("load", 0)
            keep_context()
            iterations(run)
            sp.wait_ge(sem["y_stored"], upto("y_stored", NB - 1, 16))

        @block.gpsimd
        def _(pool):
            begin(pool, ["front_pool", "back_pool", "attn_pool"])

            def const(ins, sem_=s_consts):
                ins.then_inc(sem_, 1)

            const(nc.gpsimd.memset(identf[:, :], 0.0))
            const(nc.gpsimd.memset(identb[:, :], 0.0))
            pool.wait_ge(s_consts, 2)
            for m in (identf, identb):
                const(nc.gpsimd.affine_select(out=m[:, :], in_=m[:, :], compare_op=ALU.not_equal, fill=1.0,
                                              base=0, pattern=[[-1, P]], channel_multiplier=1))
            const(nc.gpsimd.memset(minus_half[:, :], -0.5))
            pool.wait_ge(s_consts, CONSTS)

            def inv_sqrt(done, steps, b, var, eps, out_, name_eps, name_rstd):
                nc.gpsimd.tensor_scalar(out_, var, eps, None, ALU.add).then_inc(sem[done], 1)
                after(pool, done, b, steps, name_eps)
                nc.gpsimd.tensor_tensor(out_, out_, minus_half[:, :], ALU.pow).then_inc(sem[done], 1)

            def front(step, b):
                def did(ins):
                    ins.then_inc(sem["front_pool"], 1)

                if step == "ln0":
                    after(pool, "front_vec", b, FRONT_VEC, "aggr")
                    inv_sqrt("front_pool", FRONT_POOL, b, mv[:, :, 1], 1e-5, rstd[:, :], "eps", "rstd")
                if step == "probs" and b == 0:
                    weights(pool, "front", "rest")
                    drained(pool, "b2o")
                if step == "probs":
                    after(pool, "front_vec", b, FRONT_VEC, "probs")
                    after(pool, "front_vec", b - 1, FRONT_VEC, "x0")
                    probs = lg[:, 3, :, :]
                    did(nc.gpsimd.tensor_tensor(rb[:, :, :], over(b2oB[:, 0, :], C), along(probs[:, :, 0], H), ALU.mult))
                    for e in (1, 2):
                        if e == 2:
                            after(pool, "front_pool", b, FRONT_POOL, "rb1")
                        did(nc.gpsimd.tensor_tensor(rt[:, :, :], over(b2oB[:, e, :], C), along(probs[:, :, e], H), ALU.mult))
                        after(pool, "front_pool", b, FRONT_POOL, f"rt{e}")
                        did(nc.gpsimd.tensor_tensor(rb[:, :, :], rb[:, :, :], rt[:, :, :], ALU.add))
                if step == "ln1":
                    after(pool, "front_vec", b, FRONT_VEC, "aggr1")
                    inv_sqrt("front_pool", FRONT_POOL, b, mv[:, :, 1], 1e-6, rstd[:, :], "eps1", "rstd1")
                if step == "k":
                    after(pool, "front_drained", b, FRONT, "k")
                    did(nc.gpsimd.tensor_tensor(kf[:, :], kf[:, :], kp[:, HI, :], ALU.subtract))
                    after(pool, "front_pool", b, FRONT_POOL, "krest")
                    did(nc.gpsimd.tensor_scalar(kp[:, MID, :], kf[:, :], 1.0, 0.0, ALU.mult, ALU.add))
                    after(pool, "front_pool", b, FRONT_POOL, "kpart2")
                    did(nc.gpsimd.tensor_tensor(kp[:, LO, :], kf[:, :], kp[:, MID, :], ALU.subtract))

            def back(step, b, _):
                def did(ins):
                    ins.then_inc(sem["back_pool"], 1)

                if step == "ln1":
                    after(pool, "back_vec", b, BACK_VEC, "aggr1")
                    inv_sqrt("back_pool", BACK_POOL, b, bmv[:, :, 1], 1e-6, brstd[:, :], "eps1", "rstd1")
                if step == "qc":
                    after(pool, "back_drained", b, BACK, "qc")
                    did(nc.gpsimd.tensor_tensor(qcf[:, :], qcf[:, :], qcp[:, 0, :], ALU.subtract))
                    after(pool, "back_pool", b, BACK_POOL, "qrest")
                    did(nc.gpsimd.tensor_scalar(qcp[:, 1, :], qcf[:, :], 1.0, 0.0, ALU.mult, ALU.add))
                    after(pool, "back_pool", b, BACK_POOL, "qpart2")
                    did(nc.gpsimd.tensor_tensor(qcp[:, 2, :], qcf[:, :], qcp[:, 1, :], ALU.subtract))
                    after(pool, "back_vec", b, BACK_VEC, "xhat1")
                    did(nc.gpsimd.tensor_tensor(x1_two[:, b % 2, :, :], x1_two[:, b % 2, :, :], over(BC["bcproj"], C), ALU.add))
                if step == "caT":
                    after(pool, "back_filled", b - 1, BACK, "mlp")
                    gm = gates[:, bass.ds(b, 1), 1, :]
                    did(nc.gpsimd.tensor_tensor(w2g[:, :, :], wm2[:, :, :], gm.to_broadcast([P, 4, H]), ALU.mult))
                    after(pool, "back_pool", b - 1, BACK_POOL, "x2gb")
                    did(nc.gpsimd.tensor_tensor(gbm[:, :].unsqueeze(1), BC["bm2"].unsqueeze(1), gm, ALU.mult))
                if step == "xT":
                    after(pool, "back_vec", b, BACK_VEC, "xhat2")
                    did(nc.gpsimd.tensor_tensor(x1_two[:, b % 2, :, :], x1_two[:, b % 2, :, :], over(gbm[:, :], C), ALU.add))
                if step == "ln2":
                    after(pool, "back_vec", b, BACK_VEC, "aggr2")
                    inv_sqrt("back_pool", BACK_POOL, b, bmv[:, :, 1], 1e-6, brstd[:, :], "eps2", "rstd2")

            def fold(b):
                def did(ins):
                    ins.then_inc(sem["attn_pool"], 1)

                after(pool, "o_drained", b - 1, OUT, "proj")
                after(pool, "front_vec", b, FRONT_VEC, "x0")
                ga = gates[:, bass.ds(b, 1), 0, :]
                did(nc.gpsimd.tensor_tensor(wpg[:, :].unsqueeze(1), wproj.unsqueeze(1), ga, ALU.mult))
                did(nc.gpsimd.tensor_tensor(gbp[:, :].unsqueeze(1), BC["bproj"].unsqueeze(1), ga, ALU.mult))
                after(pool, "attn_pool", b, ATTN_POOL, "gbp")
                if b >= 2:
                    pool.wait_ge(sem["y_stored"], upto("y_stored", b - 2, 16))
                did(nc.gpsimd.tensor_tensor(x1_two[:, b % 2, :, :], x0[:, :, :], over(gbp[:, :], C), ALU.add))


            def run(b, has_attn, has_front, has_back):
                for s, places in enumerate(PLANS["G"]):
                    if s == 5 and has_attn:
                        fold(b)
                    for place in places:
                        do_place(place, {"front": front, "attn": lambda step, b: None, "back": back}, b)

            drained(pool, "aggr")
            nc.gpsimd.tensor_scalar(rstd[0:S, :], mv[0:S, :, 1], 1e-6, None, ALU.add).then_inc(s_rstd, 1)
            pool.wait_ge(s_rstd, 1)
            nc.gpsimd.tensor_tensor(rstd[0:S, :], rstd[0:S, :], minus_half[0:S, :], ALU.pow).then_inc(s_rstd, 1)
            front("ln0", 0)
            after(pool, "front_pool", 0, FRONT_POOL, "rstd")
            pool.wait_ge(s_rstd, 2)
            const(nc.gpsimd.memset(cpT[2 * TILE:KP, :, :], 0.0), s_zeros)
            pool.wait_ge(s_zeros, 1)
            const(nc.gpsimd.memset(kcS[0:KP, :, :], 0.0), s_zeros)
            const(nc.gpsimd.memset(kS[0:KP, :, :].bitcast(F32), 0.0), s_zeros)
            const(nc.gpsimd.memset(qcS[0:KP, :, :].bitcast(F32), 0.0), s_zeros)
            pool.wait_ge(s_zeros, 4)
            const(nc.gpsimd.memset(kcS[ROW_M:ROW_M + 3, :, :], 1.0), s_zeros)
            const(nc.gpsimd.memset(kS[ROW_M:ROW_M + 3, :, :], 1.0), s_zeros)
            pool.wait_ge(s_zeros, ZEROS)

            iterations(run)

        @block.scalar
        def _(act):
            begin(act, ["front_drained", "front_act", "exp_done", "av_drained", "m_drained", "o_drained",
                        "back_drained", "cexp_done", "gelu_done"])

            def drain(out_, in_, done, **kw):
                nc.scalar.activation(out_, in_, ACT.Identity if kw else ACT.Copy, **kw).then_inc(sem[done], 1)

            def front(step, b):
                fb = front_bank(step, b) if step in FRONT else None
                done = "front_drained"
                if step in FRONT:
                    after(act, "front_filled", b, FRONT, step)
                if step == "nxT":
                    drain(nxT[:, :], fb, done, scale=col("gamma"), bias=col("beta"))
                if step == "scores":
                    after(act, "front_vec", b, FRONT_VEC, "pneg")
                    for c in range(C):
                        ins = nc.scalar.activation(pw[:, c, :], fb[:, c * (S + E):c * (S + E) + S], ACT.Exp,
                                                   bias=pm[:, 1, c:c + 1], scale=PROTO_SCALE,
                                                   accum_out=pm[:, 2, c:c + 1])
                    ins.then_inc(sem[done], 1)
                if step == "wT":
                    drain(wT[0:S, :], fb[0:S, :], done)
                if step == "evT":
                    drain(evT[:, :], fb, done)
                if step == "router":
                    after(act, "front_vec", b, FRONT_VEC, "lsub")
                    nc.scalar.activation(lg[:, 2, :, :], lg[:, 1, :, :], ACT.Exp).then_inc(sem["front_act"], 1)
                if step[0] == "h":
                    n = int(step[1])
                    if n == 0:
                        if b == 0:
                            drained(act, "b2o")
                            act.wait_ge(kc_kept, 16)
                    if n < NZ:
                        zi = HIDDEN[n]
                        drain(z[:, zi, :], fb, done, bias=fpar_all[:, b, F_HB + zi:F_HB + zi + 1])
                    if n:
                        after(act, done, b, FRONT, f"h{n - 1}")
                        if n > 2:
                            after(act, "front_vec", b, FRONT_VEC, f"silu{n - 3}")
                        else:
                            after(act, "front_vec", b - 1, FRONT_VEC, f"silu{NZ - 1}")
                        nc.scalar.activation(th[:, n % 2, :], z[:, HIDDEN[n - 1], :], ACT.Tanh, scale=0.5
                                             ).then_inc(sem["front_act"], 1)
                if step == "gate":
                    after(act, done, b, FRONT, "gate")
                    nc.scalar.activation(gz[:, :, :], gz[:, :, :], ACT.Tanh, scale=0.5).then_inc(sem["front_act"], 1)
                if step == "xnT":
                    drain(xnT[:, :], fb, done, scale=fpar_all[:, b, F_SCA:F_SCA + 1], bias=fpar_all[:, b, F_SHA:F_SHA + 1])
                if step in ("q", "k"):
                    part, whole = (qp[:, 0, :], qf) if step == "q" else (kp[:, HI, :], kf)
                    bias = col(f"b_{step}")
                    after(act, f"{step}_kept", b - 1, range(16), 15)
                    if step == "q" and b >= 2:
                        after(act, "back_pool", b - 2, BACK_POOL, "qc_parts")
                    nc.scalar.activation(part, fb, ACT.Identity, bias=bias)
                    drain(whole[:, :], fb, done, bias=bias)

            def attn(step, b):
                if step == "av":
                    take(b, NG - 1)
                if step[0] == "m":
                    g = int(step[1])
                    after(act, "m_filled", b, range(NG), g)
                    act.wait_ge(sem["m_kept"], upto("m_kept", b, 16 * g))
                    drain(mrow[:, :], m_bank[0:3 * G, 0:T], "m_drained")
                if step == "aT":
                    after(act, "o_filled", b, OUT, "aT")
                    drain(aT[:, :], xb, "o_drained")

            def take(b, g):
                act.wait_ge(sem["av_used"], upto("av_used", b, G * C * (g + 1)))
                if g == 0:
                    after(act, "o_filled", b - 1, OUT, "proj")
                else:
                    after(act, "o_filled", b, OUT, f"o{g - 1}")
                drain(oT[:, :], avb, "av_drained")

            def back(step, b, has_attn):
                bb = back_bank(step, b) if step in BACK else None
                done = "back_drained"
                if step in BACK:
                    after(act, "back_filled", b, BACK, step)
                if step == "cT":
                    drain(cT[:, :], bb, done)
                if step == "qc":
                    after(act, "qc_kept", b - 1, range(16), 15)
                    after(act, "front_vec", min(b + 1, NB - 1), FRONT_VEC, "q_parts")
                    nc.scalar.activation(qcp[:, 0, :], bb, ACT.Identity, bias=col("b_qc"))
                    drain(qcf[:, :], bb, done, bias=col("b_qc"))
                if step == "cm":
                    act.wait_ge(sem["cm_kept"], upto("cm_kept", b - 1, 16))
                    drain(cmrow[:, :], bb.bitcast(BF16)[0:3 * NH, 0:T], done)
                if step[:2] == "cs":
                    first = PAIR * int(step[2])
                    g = first // G
                    if has_attn or g == 0 or g == 3:
                        after(act, "back_filled", b if g else b - 1, BACK, f"cav{(g - 1) % NG}")
                    for i in range(first, first + PAIR):
                        act.wait_ge(sem["cs_scored"], upto("cs_scored", b, i + 1))
                        nc.scalar.activation(cross_tile(i, has_attn)[0:S, :], sco[0:S, i % 2, :], ACT.Exp, scale=SELF_SCALE
                                             ).then_inc(sem["cexp_done"], 1)
                if step[:3] == "cav":
                    drain(coT[:, :], bb, done)
                if step == "caT":
                    drain(caT[:, :], bb, done)
                if step == "xT":
                    drain(mT[:, :], bb, done, scale=bpar_all[:, b, B_SCM:B_SCM + 1], bias=bpar_all[:, b, B_SHM:B_SHM + 1])
                if step in ("m0", "m1", "m2", "m3"):
                    j = int(step[1])
                    drain(hm[:, j, :], bb, done, bias=col("b_mlp1", j))
                    if j == 3:
                        after(act, done, b, BACK, "m3")
                        flat = hm[:, :, :].rearrange("p j t -> p (j t)")
                        nc.scalar.activation(flat, flat, ACT.Gelu_apprx_tanh).then_inc(sem["gelu_done"], 1)

            def exps(b, s, pair):
                for hh in (2 * pair, 2 * pair + 1):
                    j = s * G + hh
                    act.wait_ge(sem["s_scored"], upto("s_scored", b, j + 1))
                    act.wait_ge(sem["av_used"], upto("av_used", b, j + 1 - RING))
                    nc.scalar.activation(pT[:, j % RING, :], sco[:, j % 2, :], ACT.Exp, scale=SELF_SCALE
                                         ).then_inc(sem["exp_done"], 1)

            def run(b, has_attn, has_front, has_back):
                engine = {"front": front, "attn": attn, "back": back}
                for s, places in enumerate(PLANS["A"]):
                    for n, place in enumerate(places):
                        if has_attn and n < 2:
                            exps(b, s, n)
                        if has_attn and n == 2 and s % C == 0 and s:
                            take(b, s // C - 1)
                        do_place(place, engine, b)

            act.wait_ge(s_consts, CONSTS)
            for zeros in (qS[:, :, :].rearrange("p h t -> p (h t)").bitcast(F32), vS[:, :, :, :].rearrange("p c h n -> p (c h n)")):
                nc.scalar.activation(zeros, identf[0:zeros.shape[0], 0:1].to_broadcast(list(zeros.shape)), ACT.Copy,
                                     scale=0.0).then_inc(s_azeros, 1)
            drained(act, "cols")
            nc.scalar.activation(silc[:, :], col("cond", 0, NB), ACT.Silu).then_inc(s_silu, 1)
            front("nxT", 0)
            front("scores", 0)
            act.wait_ge(s_vzeros, 3)
            for step in ("wT", "evT", "router"):
                front(step, 0)
            iterations(run)

        @block.vector
        def _(dve):
            begin(dve, ["front_vec", "nat_reduced", "m_vec", "o_vec", "v_placed", "back_vec", "cn_reduced", "co_vec"])

            def zero(ins):
                ins.then_inc(s_vzeros, 1)

            def setup(ins):
                ins.then_inc(s_vec, 1)

            vc_all = bpar_all[:, :, B_VC:B_N].rearrange("p b (h n) -> p b h n", n=TILE)

            def stats(src, st_, mv_, done, steps, b, name):
                for c in range(C):
                    ins = nc.vector.bn_stats(st_[:, c, :], src[:, c, :])
                ins.then_inc(sem[done], 1)
                after(dve, done, b, steps, name)
                for c in range(C):
                    ins = nc.vector.bn_aggr(mv_[:, c, :], st_[:, c, :])
                ins.then_inc(sem[done], 1)

            def normalize(out_, src, mv_, rstd_, done):
                for c in range(C):
                    ins = nc.vector.tensor_scalar(out_[:, c, :], src[:, c, :], mv_[:, c, 0:1], rstd_[:, c:c + 1],
                                                  ALU.subtract, ALU.mult)
                ins.then_inc(sem[done], 1)

            def front(step, b):
                fb = front_bank(step, b) if step in FRONT else None
                def did(ins):
                    ins.then_inc(sem["front_vec"], 1)

                def wait(name):
                    after(dve, "front_vec", b, FRONT_VEC, name)

                if step in ("router", "gate", "e0", "e1", "e2", "v", "scores"):
                    after(dve, "front_filled", b, FRONT, step)
                if step == "ln0":
                    dve.wait_ge(sem["x_loaded"], upto("x_loaded", b, 16))
                    stats(x, st, mv, "front_vec", FRONT_VEC, b, "stats")
                if step == "nxT":
                    after(dve, "front_pool", b, FRONT_POOL, "rstd")
                    normalize(xh, x, mv, rstd, "front_vec")
                if step == "scores":
                    sc = fb[:, 0:C * (S + E)].rearrange("p (c n) -> p c n", c=C)
                    did(nc.vector.reduce_max(pm[:, 0, :], sc[:, :, 0:S], AX_X))
                    did(nc.vector.tensor_tensor(lg[:, 0, :, :], sc[:, :, S:S + E], over(fpar_all[:, b, F_RB:F_RB + E], C), ALU.add))
                    wait("pmax")
                    did(nc.vector.tensor_scalar(pm[:, 1, :], pm[:, 0, :], -PROTO_SCALE, None, ALU.mult))
                if step == "wT":
                    after(dve, "front_drained", b, FRONT, "scores")
                    did(nc.vector.reciprocal(pm[:, 3, :], pm[:, 2, :]))
                    wait("prec")
                    did(nc.vector.tensor_tensor(pw[:, :, :], pw[:, :, :], along(pm[:, 3, :], S), ALU.mult))
                if step == "router":
                    nc.vector.tensor_tensor(lg[:, 1, :, :], fb[:, 0:C * E].rearrange("p (c e) -> p c e", c=C),
                                            lg[:, 0, :, :], ALU.add).then_inc(sem["front_drained"], 1)
                    after(dve, "front_drained", b, FRONT, "router")
                    did(nc.vector.reduce_max(lm[:, 0, :], lg[:, 1, :, :], AX_X))
                    wait("lmax")
                    did(nc.vector.tensor_tensor(lg[:, 1, :, :], lg[:, 1, :, :], along(lm[:, 0, :], E), ALU.subtract))
                if step == "probs":
                    after(dve, "front_act", b, FRONT_ACT, "rexp")
                    did(nc.vector.reduce_sum(lm[:, 1, :], lg[:, 2, :, :], AX_X))
                    wait("lsum")
                    did(nc.vector.reciprocal(lm[:, 2, :], lm[:, 1, :]))
                    wait("lrec")
                    did(nc.vector.tensor_tensor(lg[:, 3, :, :], lg[:, 2, :, :], along(lm[:, 2, :], E), ALU.mult))
                if step == "gate":
                    after(dve, "front_pool", b, FRONT_POOL, "rb2")
                    nc.vector.tensor_tensor(gz[:, :, :], chunks(fb), over(BC["gate_b2"], C), ALU.add
                                            ).then_inc(sem["front_drained"], 1)
                if step in ("e0", "e1", "e2"):
                    e = int(step[1])
                    if e == 0:
                        after(dve, "front_pool", b, FRONT_POOL, "rb2")
                    else:
                        after(dve, "front_drained", b, FRONT, f"e{e - 1}")
                    for c in range(C):
                        ins = nc.vector.scalar_tensor_tensor(acc[:, c, :], chunk(fb, c), lg[:, 3, c, e:e + 1],
                                                             acc[:, c, :], ALU.mult, ALU.add)
                    ins.then_inc(sem["front_drained"], 1)
                if step[0] == "h" and step != "h0":
                    n = int(step[1])
                    after(dve, "front_act", b, FRONT_ACT, f"tanh{n - 1}")
                    hidden = z[:, HIDDEN[n - 1], :]
                    did(nc.vector.scalar_tensor_tensor(hidden, th[:, n % 2, :], 1.0, hidden, ALU.add, ALU.mult))
                if step == "ln1":
                    after(dve, "front_drained", b, FRONT, "e2")
                    after(dve, "front_act", b, FRONT_ACT, "gate")
                    did(nc.vector.scalar_tensor_tensor(acc[:, :, :], gz[:, :, :], 1.0, acc[:, :, :], ALU.add, ALU.mult))
                    wait("gated")
                    after(dve, "attn_pool", b - 1, ATTN_POOL, "x0gb")
                    did(nc.vector.scalar_tensor_tensor(x0[:, :, :], acc[:, :, :], 0.5, x[:, :, :], ALU.mult, ALU.add))
                    wait("x0")
                    stats(x0, st, mv, "front_vec", FRONT_VEC, b, "stats1")
                if step == "xnT":
                    after(dve, "front_pool", b, FRONT_POOL, "rstd1")
                    normalize(xh, x0, mv, rstd, "front_vec")
                if step == "q":
                    after(dve, "front_drained", b, FRONT, "q")
                    did(nc.vector.tensor_tensor(qf[:, :], qf[:, :], qp[:, 0, :], ALU.subtract))
                    wait("qrest")
                    did(nc.vector.tensor_copy(qp[:, 1, :], qf[:, :]))
                    wait("qpart2")
                    did(nc.vector.tensor_tensor(qp[:, 2, :], qf[:, :], qp[:, 1, :], ALU.subtract))
                if step == "v":
                    nc.vector.tensor_tensor(vst[:, :, :, :].rearrange("p c h d -> p c (h d)"), chunks(fb),
                                            over(BC["bv"], C), ALU.add).then_inc(sem["front_drained"], 1)

            def attn(step, b):
                if step[0] == "m":
                    g = int(step[1])
                    src = mx[:, :, g * G:(g + 1) * G]
                    did = sem["m_vec"]
                    dve.wait_ge(sem["nat_reduced"], upto("nat_reduced", b, C * G * (g + 1)))
                    if g:
                        after(dve, "m_filled", b, range(NG), g - 1)
                    else:
                        after(dve, "m_filled", b - 1, range(NG), NG - 1)
                    nc.vector.tensor_scalar(mp[:, :, 0, :], src, -1.0, None, ALU.mult).then_inc(did, 1)
                    dve.wait_ge(did, upto("m_vec", b, 4 * g + 1))
                    nc.vector.scalar_tensor_tensor(mr[:, :, :], src, -1.0, mp[:, :, 0, :], ALU.mult, ALU.subtract
                                                   ).then_inc(did, 1)
                    dve.wait_ge(did, upto("m_vec", b, 4 * g + 2))
                    nc.vector.tensor_copy(mp[:, :, 1, :], mr[:, :, :]).then_inc(did, 1)
                    dve.wait_ge(did, upto("m_vec", b, 4 * g + 3))
                    nc.vector.tensor_tensor(mp[:, :, 2, :], mr[:, :, :], mp[:, :, 1, :], ALU.subtract).then_inc(did, 1)
                if step in ("o0", "o1", "o2", "o3"):
                    g = int(step[1])
                    after(dve, "o_filled", b, OUT, step)
                    bank = xb.rearrange("p (c g n) -> p c g n", c=C, g=G)
                    nc.vector.reciprocal(rec[:, :, :], bank[:, :, :, HD]).then_inc(sem["o_vec"], 1)
                    after(dve, "o_vec", b, range(NG), g)
                    nc.vector.tensor_tensor(an[:, :, g * G:(g + 1) * G, :], bank[:, :, :, 0:HD], along(rec[:, :, :], HD),
                                            ALU.mult).then_inc(sem["o_drained"], 1)
                if step == "proj":
                    after(dve, "o_filled", b, OUT, "proj")
                    after(dve, "attn_pool", b, ATTN_POOL, "x0gb")
                    nc.vector.tensor_tensor(x1_two[:, b % 2, :, :], chunks(xb), x1_two[:, b % 2, :, :],
                                            ALU.add).then_inc(sem["o_drained"], 1)

            def back(step, b, _):
                bb = back_bank(step, b) if step in BACK else None
                def did(ins):
                    ins.then_inc(sem["back_vec"], 1)

                def wait(name):
                    after(dve, "back_vec", b, BACK_VEC, name)

                done = "back_drained"
                if step == "ln1":
                    after(dve, "o_drained", b, OUT, "proj")
                    stats(x1_two[:, b % 2, :, :], bst, bmv, "back_vec", BACK_VEC, b, "stats1")
                if step == "cT":
                    after(dve, "back_pool", b, BACK_POOL, "rstd1")
                    normalize(bxh, x1_two[:, b % 2, :, :], bmv, brstd, "back_vec")
                if step[:2] == "cn":
                    for h in range(PAIR * int(step[2]), PAIR * int(step[2]) + PAIR):
                        dve.wait_ge(sem["cn_scored"], upto("cn_scored", b, h + 1))
                        nc.vector.reduce_max(cmx[:, :, h], nat[:, h % 2, 0:C * S].rearrange("p (c s) -> p c s", c=C), AX_X
                                             ).then_inc(sem["cn_reduced"], 1)
                if step == "cm":
                    dve.wait_ge(sem["cn_reduced"], upto("cn_reduced", b, NH))
                    did(nc.vector.tensor_scalar(cmp_[:, :, 0, :], cmx[:, :, :], -1.0, None, ALU.mult))
                    wait("n1")
                    did(nc.vector.scalar_tensor_tensor(cmr[:, :, :], cmx[:, :, :], -1.0, cmp_[:, :, 0, :],
                                                       ALU.mult, ALU.subtract))
                    wait("nrest")
                    did(nc.vector.tensor_copy(cmp_[:, :, 1, :], cmr[:, :, :]))
                    wait("n2")
                    did(nc.vector.tensor_tensor(cmp_[:, :, 2, :], cmr[:, :, :], cmp_[:, :, 1, :], ALU.subtract))
                if step[:2] == "co":
                    g = int(step[2])
                    after(dve, "back_filled", b, BACK, step)
                    bank = bb.rearrange("p (c g n) -> p c g n", c=C, g=G)
                    nc.vector.reciprocal(crec[:, :, :], bank[:, :, :, HD]).then_inc(sem["co_vec"], 1)
                    after(dve, "co_vec", b, range(NG), g)
                    nc.vector.tensor_tensor(can[:, :, g * G:(g + 1) * G, :], bank[:, :, :, 0:HD], along(crec[:, :, :], HD),
                                            ALU.mult).then_inc(sem[done], 1)
                if step == "cproj":
                    after(dve, "back_filled", b, BACK, "cproj")
                    after(dve, "back_pool", b, BACK_POOL, "x1b")
                    nc.vector.tensor_tensor(x1_two[:, b % 2, :, :], chunks(bb), x1_two[:, b % 2, :, :], ALU.add).then_inc(sem[done], 1)
                if step == "ln2":
                    after(dve, done, b, BACK, "cproj")
                    stats(x1_two[:, b % 2, :, :], bst, bmv, "back_vec", BACK_VEC, b, "stats2")
                if step == "xT":
                    after(dve, "back_pool", b, BACK_POOL, "rstd2")
                    normalize(bxh, x1_two[:, b % 2, :, :], bmv, brstd, "back_vec")
                if step == "mlp":
                    after(dve, "back_filled", b, BACK, "mlp")
                    after(dve, "back_pool", b, BACK_POOL, "x2gb")
                    nc.vector.tensor_tensor(x1_two[:, b % 2, :, :], chunks(bb), x1_two[:, b % 2, :, :], ALU.add).then_inc(sem[done], 1)

            def maxima(b, h, pair):
                for c in (2 * pair, 2 * pair + 1):
                    dve.wait_ge(sem["nat_scored"], upto("nat_scored", b, h * C + c + 1))
                    nc.vector.reduce_max(mx[:, c, h:h + 1], nat[:, c % 2, :], AX_X).then_inc(sem["nat_reduced"], 1)

            def place_v(b):
                dve.wait_ge(sem["av_used"], upto("av_used", b - 1, NH * C))
                after(dve, "front_drained", b, FRONT, "v")
                nc.vector.tensor_copy(vS[:, :, :, 0:HD].rearrange("p c h d -> p (c h) d"),
                                      vst[:, :, :, :].rearrange("p c h d -> p (c h) d")
                                      ).then_inc(sem["v_placed"], 1)

            def run(b, has_attn, has_front, has_back):
                engine = {"front": front, "attn": attn, "back": back}
                for s, places in enumerate(PLANS["V"]):
                    ahead = (b, s + LAG, has_attn) if s + LAG < NH else (b + 1, s + LAG - NH, has_front)
                    for n, place in enumerate(places):
                        if ahead[2] and n < 2:
                            maxima(ahead[0], ahead[1], n)
                        if has_attn and s == 0 and n == 2:
                            place_v(b)
                        do_place(place, engine, b)

            zero(nc.vector.memset(fpar_all[:, :, :], 0.0))
            zero(nc.vector.memset(bpar_all[:, :, :], 0.0))
            zero(nc.vector.memset(wT[2 * TILE:KP, :], 0.0))
            dve.wait_ge(s_vzeros, 3)
            weights(dve, "ctx")
            for b in range(NB):
                ins = nc.vector.bn_stats(st[0:S, b, :], ctxn[0:S, b, :])
            setup(ins)
            drained(dve, "stats")
            for b in range(NB):
                ins = nc.vector.bn_aggr(mv[0:S, b, :], st[0:S, b, :])
            setup(ins)
            filled(dve, "cols")
            setup(nc.vector.tensor_copy(cols[:, 0:len(ROWS)], fill_bank("cols")[:, 0:len(ROWS)]))
            filled(dve, "ctxT")
            setup(nc.vector.tensor_copy(ctxT[:, :, :].rearrange("p b s -> p (b s)"), fill_bank("ctxT")[:, 0:NB * S]))
            dve.wait_ge(s_rstd, 2)
            drained(dve, "aggr")
            for b in range(NB):
                ins = nc.vector.tensor_scalar(ctxh[0:S, b, :], ctxn[0:S, b, :], mv[0:S, b, 0:1], rstd[0:S, b:b + 1],
                                              ALU.subtract, ALU.mult)
            setup(ins)
            front("ln0", 0)
            drained(dve, "cols")
            setup(nc.vector.tensor_copy(condrep[:, :, :], along(col("cond", 0, NB), H)))
            setup(nc.vector.tensor_copy(b2rep[:, :, :], along(col("e_b2", 0, E), H)))
            filled(dve, "ctxhT")
            setup(nc.vector.tensor_copy(ctxhT[:, :, :].rearrange("p b s -> p (b s)"), fill_bank("ctxhT")[:, 0:NB * S]))
            filled(dve, "wq0T")
            setup(nc.vector.tensor_copy(wq0T[:, :], fill_bank("wq0T")[:, 0:H]))
            front("nxT", 0)
            filled(dve, "kpT")
            setup(nc.vector.tensor_copy(kpT[:, :, :].rearrange("p b s -> p (b s)"), fill_bank("kpT")[:, 0:NB * S]))
            filled(dve, "G")
            setup(nc.vector.tensor_copy(fpar_all[:, :, F_G:F_G + S],
                                        fill_bank("G")[:, 0:NB * S].rearrange("p (b s) -> p b s", b=NB)))
            weights(dve, "w0")
            setup(nc.vector.tensor_copy(fpar_all[:, :, F_WR:F_WR + E],
                                        wr[:, 0:1, :].to_broadcast([P, NB, E])))
            filled(dve, "vp")
            setup(nc.vector.tensor_copy(fpar_all[0:S, :, F_VP:F_VP + H],
                                        fill_bank("vp")[0:S, :].rearrange("p (b h) -> p b h", b=NB)))
            filled(dve, "kc")
            setup(nc.vector.tensor_scalar(kcf[:, :], fill_bank("kc")[:, 0:NB * S], col("b_kc"), None, ALU.add))
            drained(dve, "kcf")
            setup(nc.vector.tensor_copy(kcp[:, HI, :], kcf[:, :]))
            drained(dve, "kpart1")
            setup(nc.vector.tensor_tensor(kcf[:, :], kcf[:, :], kcp[:, HI, :], ALU.subtract))
            drained(dve, "krest")
            setup(nc.vector.tensor_copy(kcp[:, MID, :], kcf[:, :]))
            drained(dve, "kpart2")
            setup(nc.vector.tensor_tensor(kcp[:, LO, :], kcf[:, :], kcp[:, MID, :], ALU.subtract))
            filled(dve, "vc")
            weights(dve, "mod")
            for b in range(NB):
                ins = nc.vector.tensor_tensor(vc_all[0:S, b, :, 0:HD],
                                              chunk(fill_bank("vc"), b)[0:S, :].rearrange("p (h d) -> p h d", d=HD),
                                              bvc[0:S, :].rearrange("p (h d) -> p h d", d=HD), ALU.add)
            setup(ins)
            filled(dve, "hb")
            setup(nc.vector.tensor_tensor(fpar_all[:, :, F_HB:F_HB + NZ],
                                          fill_bank("hb")[:, 0:NZ * NB].rearrange("p (z b) -> p b z", b=NB),
                                          over(cols[:, 0:NZ], NB), ALU.add))
            filled(dve, "rbias")
            weights(dve, "mod")
            setup(nc.vector.tensor_tensor(fpar_all[:, :, F_RB:F_RB + E],
                                          fill_bank("rbias")[:, 0:NB * E].rearrange("p (b e) -> p b e", e=E),
                                          over(rbb, NB), ALU.add))
            drained(dve, "rbias")
            front("scores", 0)
            dve.wait_ge(s_silu, 1)
            setup(nc.vector.tensor_copy(silurep[:, :, :], along(silc[:, :], H)))
            filled(dve, "mod")
            mods = fill_bank("mod")[:, 0:4 * NB].rearrange("p (j b) -> p j b", b=NB)
            for n, (j, plus, dst) in enumerate(((0, 0.0, fpar_all[:, :, F_SHA]), (1, 1.0, fpar_all[:, :, F_SCA]),
                                                (3, 0.0, bpar_all[:, :, B_SHM]), (4, 1.0, bpar_all[:, :, B_SCM]))):
                ins = nc.vector.tensor_scalar(dst, mods[:, n, :], col("b_mod", j), plus, ALU.add, ALU.add)
            setup(ins)
            front("wT", 0)
            for half in range(2):
                filled(dve, f"gates{half}")
                setup(nc.vector.tensor_tensor(
                    gates[:, 2 * half:2 * half + 2, :, :],
                    fill_bank(f"gates{half}").rearrange("p (b j h) -> p b j h", b=2, j=2),
                    bgates[:, :, :].unsqueeze(1).to_broadcast([P, 2, 2, H]), ALU.add))
            for step, dst, n, w in (("ew2Ta", ew2T, 4, 0), ("ew2Tb", ew2T, 2, 4), ("w2oa", w2o, 4, 0), ("w2ob", w2o, 2, 4)):
                filled(dve, step)
                half = 0.5 if dst is w2o else 1.0
                setup(nc.vector.tensor_scalar(dst[:, w:w + n, :].rearrange("p j h -> p (j h)"),
                                              fill_bank(step)[:, 0:n * H], half, None, ALU.mult))
            front("router", 0)
            filled(dve, "b2o")
            weights(dve, "experts", "front", "rest")
            zero(nc.vector.tensor_scalar(gw2, gw2, 0.5, None, ALU.mult))
            setup(nc.vector.tensor_tensor(b2oB[:, :, :], fill_bank("b2o")[:, 0:E * H].rearrange("p (e h) -> p e h", e=E),
                                          over(bout, E), ALU.add))
            dve.wait_ge(s_azeros, 2)
            nc.vector.memset(vc_all[0:S, :, :, HD], 1.0)
            zero(nc.vector.memset(vS[:, :, :, HD], 1.0))
            dve.wait_ge(s_vzeros, VZEROS)
            drained(dve, "b2o")


            iterations(run)

        @block.tensor
        def _(pe):
            begin(pe, ["front_filled", "nat_scored", "s_scored", "av_used", "m_filled", "o_filled", "back_filled",
                       "cn_scored", "cs_scored"])
            mm = nc.tensor.matmul

            def transposes(out_, ins_, ident):
                rows_ = ins_[0].shape[0]
                for c, t in enumerate(ins_):
                    last = nc.tensor.transpose(out_[0:t.shape[1], c * rows_:(c + 1) * rows_], t, ident[0:rows_, 0:rows_])
                return last

            def fill(step):
                n = FILLS.index(step)
                if n >= SETUP_BANKS:
                    before = FILLS[n - SETUP_BANKS]
                    drain_of = {"kc": "kcf"}.get(before, before)
                    drained(pe, drain_of)
                return fill_bank(step)

            def filled_by(ins):
                ins.then_inc(s_filled, 1)

            last_natural, last_scores = [upto("nat_reduced", 0, 0)], [upto("exp_done", 0, 0)]
            cross_in_nat, cross_in_sco = [None], [None]

            def front(step, b):
                fb = front_bank(step, b) if step in FRONT else None
                if step not in FRONT:
                    return
                n = FRONT.index(step)
                loose = front_alternates(step, b) and step in FRONT_LOOSE
                pe.wait_ge(sem["front_drained"], upto("front_drained", b, n - loose))
                if step in ("nxT", "xnT"):
                    after(pe, "front_vec", b, FRONT_VEC, "xhat" if step == "nxT" else "xhat1")
                    ins = transposes(fb, [xh[:, c, :] for c in range(C)], identf)
                if step == "scores":
                    for c in range(C):
                        ins = mm(fb[:, c * (S + E):(c + 1) * (S + E)], chunk(nxT, c), fpar_all[:, b, F_G:F_G + S + E],
                                 start=True, stop=True)
                if step == "wT":
                    after(pe, "front_vec", b, FRONT_VEC, "pnorm")
                    ins = transposes(fb, [pw[:, c, :] for c in range(C)], identf)
                if step == "evT":
                    ins = mm(fb, fpar_all[0:KP, b, F_VP:F_VP + H], wT[0:KP, :], start=True, stop=True)
                if step == "router":
                    for c in range(C):
                        ins = mm(fb[:, c * E:(c + 1) * E], chunk(evT, c), wr[:, 1, :], start=True, stop=True)
                if step[0] == "h":
                    zi = HIDDEN[int(step[1])]
                    mm(fb, w1[:, 0, zi, :], nxT[:, :], start=True, stop=False)
                    ins = mm(fb, w1[:, 1, zi, :], evT[:, :], start=False, stop=True)
                if step == "gate":
                    after(pe, "front_vec", b, FRONT_VEC, "silu0")
                    for c in range(C):
                        ins = mm(chunk(fb, c), chunk(z[:, 2 * E, :], c), gw2, start=True, stop=True)
                if step in ("e0", "e1", "e2"):
                    e = int(step[1])
                    after(pe, "front_vec", b, FRONT_VEC, f"silu{2 * e + 2}")
                    for c in range(C):
                        for r in range(2):
                            ins = mm(chunk(fb, c), chunk(z[:, 2 * e + r, :], c), w2o[:, 2 * e + r, :],
                                     start=r == 0, stop=r == 1)
                if step in ("q", "k"):
                    ins = mm(fb, chunk(wqkv, "qk".index(step)), xnT[:, :], start=True, stop=True)
                if step == "v":
                    for c in range(C):
                        ins = mm(chunk(fb, c), chunk(xnT, c), wqkv[:, 2 * H:3 * H], start=True, stop=True)
                ins.then_inc(sem["front_filled"], 1)

            def attn(step, b):
                if step == "av":
                    weighted(b, NH - 1)
                if step[0] == "m":
                    g = int(step[1])
                    pe.wait_ge(sem["m_vec"], upto("m_vec", b, 4 * (g + 1)))
                    after(pe, "o_drained", b - 1, OUT, {0: "o2", 1: "proj"}.get(g, "o2")) if g < 2 else \
                        after(pe, "o_drained", b, OUT, f"o{g - 2}")
                    transposes(m_bank, [mp[:, c, :, :].rearrange("p s g -> p (s g)") for c in range(C)], identb
                               ).then_inc(sem["m_filled"], 1)
                if step in ("o0", "o1", "o2", "o3"):
                    g = int(step[1])
                    after(pe, "av_drained", b, range(NG), g)
                    if g < 3:
                        after(pe, "m_drained", b, range(NG), g + 1)
                    elif b == NB - 1:
                        after(pe, "o_drained", b, OUT, "o2")
                    else:
                        after(pe, "m_drained", b + 1, range(NG), 0)
                    transposes(xb, [chunk(oT, c) for c in range(C)], identf).then_inc(sem["o_filled"], 1)
                if step == "aT":
                    after(pe, "o_drained", b, OUT, "o3")
                    transposes(xb, [an[:, c, :, :].rearrange("p h d -> p (h d)") for c in range(C)], identf
                               ).then_inc(sem["o_filled"], 1)
                if step == "proj":
                    after(pe, "o_drained", b, OUT, "aT")
                    after(pe, "attn_pool", b, ATTN_POOL, "wpg")
                    for c in range(C):
                        ins = mm(chunk(xb, c), chunk(aT, c), wpg[:, :], start=True, stop=True)
                    ins.then_inc(sem["o_filled"], 1)

            def back(step, b, has_attn):
                bb = back_bank(step, b) if step in BACK else None
                if step[:2] == "cn":
                    first = PAIR * int(step[2])
                    if first == 0:
                        pe.wait_ge(sem["qc_placed"], upto("qc_placed", b, 16 * len(RUNS)))
                        pe.wait_ge(sem["kc_placed"], upto("kc_placed", b, per["kc_placed"]))
                    if first:
                        pe.wait_ge(sem["cn_reduced"], upto("cn_reduced", b, first))
                    pe.wait_ge(sem["nat_reduced"], last_natural[0])
                    for h in range(first, first + PAIR):
                        for c in range(C):
                            ins = mm(nat[:, h % 2, c * S:(c + 1) * S], chunk(qcS[:, h, :], c), kcS[:, h, :],
                                     start=True, stop=True)
                        ins.then_inc(sem["cn_scored"], 1)
                    cross_in_nat[0] = upto("cn_reduced", b, first + PAIR)
                    return
                if step[:2] == "cs":
                    first = PAIR * int(step[2])
                    if first == 0:
                        pe.wait_ge(sem["cm_placed"], upto("cm_placed", b, 16))
                    if first:
                        pe.wait_ge(sem["cexp_done"], upto("cexp_done", b, first))
                    pe.wait_ge(sem["exp_done"], last_scores[0])
                    for h in range(first, first + PAIR):
                        mm(sco[0:S, h % 2, :], kcS[:, h, :], qcS[:, h, :], start=True, stop=True
                           ).then_inc(sem["cs_scored"], 1)
                    cross_in_sco[0] = upto("cexp_done", b, first + PAIR)
                    return
                if step not in BACK:
                    return
                n = BACK.index(step)
                loose = b >= NB - 2 and step in BACK_LOOSE
                pe.wait_ge(sem["back_drained"], upto("back_drained", b, n - loose))
                if step == "cT" and b == 0:
                    pe.wait_ge(sem["front_drained"], upto("front_drained", 2, len(EARLY)))
                if b == NB - 2:
                    after(pe, "front_drained", NB - 1, FRONT, "v")
                if step == "cT":
                    after(pe, "back_vec", b, BACK_VEC, "xhat1")
                    ins = transposes(bb, [bxh[:, c, :] for c in range(C)], identf)
                if step == "qc":
                    ins = mm(bb, wqc, cT[:, :], start=True, stop=True)
                if step == "cm":
                    after(pe, "back_vec", b, BACK_VEC, "n3")
                    ins = transposes(bb.bitcast(BF16), [cmp_[:, c, :, :].rearrange("p s h -> p (s h)") for c in range(C)], identb)
                if step[:3] == "cav":
                    g = int(step[3])
                    for hh in range(G):
                        h = g * G + hh
                        pe.wait_ge(sem["cexp_done"], upto("cexp_done", b, h + 1))
                        ins = mm(bb[TILE * hh:TILE * (hh + 1), :], bpar_all[0:KP, b, B_VC + h * TILE:B_VC + (h + 1) * TILE],
                                 cross_tile(h, has_attn)[0:KP, :], start=True, stop=True)
                if step in ("co0", "co1", "co2", "co3"):
                    ins = transposes(bb, [chunk(coT, c) for c in range(C)], identf)
                if step == "caT":
                    ins = transposes(bb, [can[:, c, :, :].rearrange("p h d -> p (h d)") for c in range(C)], identf)
                if step == "cproj":
                    for c in range(C):
                        ins = mm(chunk(bb, c), chunk(caT, c), wcproj, start=True, stop=True)
                if step == "xT":
                    after(pe, "back_vec", b, BACK_VEC, "xhat2")
                    ins = transposes(bb, [bxh[:, c, :] for c in range(C)], identf)
                if step in ("m0", "m1", "m2", "m3"):
                    ins = mm(bb, chunk(wm1, int(step[1])), mT[:, :], start=True, stop=True)
                if step == "mlp":
                    after(pe, "gelu_done", b, range(1), 0)
                    after(pe, "back_pool", b, BACK_POOL, "gbm")
                    for c in range(C):
                        for j in range(4):
                            ins = mm(chunk(bb, c), chunk(hm[:, j, :], c), w2g[:, j, :], start=j == 0, stop=j == 3)
                ins.then_inc(sem["back_filled"], 1)

            def natural(b, h, pair):
                if h % (NH // 2) == 0 and pair == 0:
                    half = h // (NH // 2)
                    pe.wait_ge(sem[f"half{half}"], upto(f"half{half}", b, 16 * HALF))
                for c in (2 * pair, 2 * pair + 1):
                    pe.wait_ge(sem["nat_reduced"], upto("nat_reduced", b, h * C + c - 1))
                    if cross_in_nat[0]:
                        pe.wait_ge(sem["cn_reduced"], cross_in_nat[0] - 1 + c % 2)
                    mm(nat[:, c % 2, :], chunk(qS[:, h, :], c), kS[:, h, :], start=True, stop=True
                       ).then_inc(sem["nat_scored"], 1)
                cross_in_nat[0] = None
                last_natural[0] = upto("nat_reduced", b, h * C + 2 * pair + 2)

            def scores(b, s, pair):
                g, kc = divmod(s, C)
                if kc == 0 and pair == 0:
                    pe.wait_ge(sem["m_placed"], upto("m_placed", b, 16 * (g + 1)))
                for hh in (2 * pair, 2 * pair + 1):
                    j, h = s * G + hh, g * G + hh
                    pe.wait_ge(sem["exp_done"], upto("exp_done", b, j - 1))
                    if cross_in_sco[0]:
                        pe.wait_ge(sem["cexp_done"], cross_in_sco[0] - 1 + j % 2)
                    mm(sco[:, j % 2, :], chunk(kS[:, h, :], kc), qS[:, h, :], start=True, stop=True
                       ).then_inc(sem["s_scored"], 1)
                cross_in_sco[0] = None
                last_scores[0] = upto("exp_done", b, s * G + 2 * pair + 2)

            def weighted(b, s):
                g, kc = divmod(s, C)
                if s == 0:
                    pe.wait_ge(sem["v_placed"], upto("v_placed", b, 1))
                if kc == 0:
                    pe.wait_ge(sem["av_drained"], upto("av_drained", b, g))
                for hh in range(G):
                    j = s * G + hh
                    pe.wait_ge(sem["exp_done"], upto("exp_done", b, j + 1))
                    mm(avb[TILE * hh:TILE * (hh + 1), :], vS[:, kc, g * G + hh, :], pT[:, j % RING, :],
                       start=kc == 0, stop=kc == C - 1).then_inc(sem["av_used"], 1)

            def run(b, has_attn, has_front, has_back):
                engine = {"front": front, "attn": attn, "back": back}
                for s, places in enumerate(PLANS["T"]):
                    ahead = (b, s + LAG, has_attn) if s + LAG < NH else (b + 1, s + LAG - NH, has_front)
                    for n, place in enumerate(places):
                        if has_attn and n < 2:
                            scores(b, s, n)
                        if ahead[2] and n < 2:
                            natural(ahead[0], ahead[1], n)
                        if has_attn and n == 2 and s:
                            weighted(b, s - 1)
                        do_place(place, engine, b)

            pe.wait_ge(s_consts, CONSTS)
            weights(pe, "rows")
            filled_by(transposes(fill("cols"), [rows[0:len(ROWS), :]], identf))
            weights(pe, "ctx")
            filled_by(transposes(fill("ctxT"), [ctxn[0:S, b, :] for b in range(NB)], identf))
            drained(pe, "ctxhat")
            filled_by(transposes(fill("ctxhT"), [ctxh[0:S, b, :] for b in range(NB)], identf))
            weights(pe, "w0")
            filled_by(transposes(fill("wq0T"), [wqkv0[:, 0, :]], identf))
            drained(pe, "ctxT")
            filled_by(mm(fill("kpT")[:, 0:NB * S], wqkv0[:, 1, :], ctxT[:, :, :].rearrange("p b s -> p (b s)"),
                         start=True, stop=True))
            drained(pe, "kpT")
            filled_by(mm(fill("G")[:, 0:NB * S], wq0T[:, :], kpT[:, :, :].rearrange("p b s -> p (b s)"),
                         start=True, stop=True))
            front("nxT", 0)
            bank = fill("vp")
            for b in range(NB):
                ins = mm(chunk(bank, b)[0:S, :], ctxT[:, b, :], wqkv0[:, 2, :], start=True, stop=True)
            filled_by(ins)
            drained(pe, "ctxhT")
            filled_by(mm(fill("kc")[:, 0:NB * S], wkvc[:, 0:H], ctxhT[:, :, :].rearrange("p b s -> p (b s)"),
                         start=True, stop=True))
            bank = fill("vc")
            for b in range(NB):
                ins = mm(chunk(bank, b)[0:S, :], ctxhT[:, b, :], wkvc[:, H:2 * H], start=True, stop=True)
            filled_by(ins)
            weights(pe, "w1")
            bank = fill("hb")
            for zi in range(NZ):
                ins = mm(bank[:, zi * NB:(zi + 1) * NB], w1[:, 2, zi, :], col("cond", 0, NB), start=True, stop=True)
            filled_by(ins)
            bank = fill("rbias")
            for b in range(NB):
                ins = mm(bank[:, b * E:(b + 1) * E], condrep[:, b, :], wr[:, 2, :], start=True, stop=True)
            filled_by(ins)
            drained(pe, "wr")
            front("scores", 0)
            weights(pe, "mod")
            pe.wait_ge(s_silu, 1)
            bank = fill("mod")
            for n, j in enumerate((0, 1, 3, 4)):
                ins = mm(bank[:, n * NB:(n + 1) * NB], wmod[:, j, :], silc[:, :], start=True, stop=True)
            filled_by(ins)
            front("wT", 0)
            drained(pe, "silurep")
            for half in range(2):
                bank = fill(f"gates{half}")
                for n in range(4):
                    ins = mm(chunk(bank, n), silurep[:, 2 * half + n // 2, :], wmod[:, (2, 5)[n % 2], :],
                             start=True, stop=True)
                filled_by(ins)
            drained(pe, "vp")
            front("evT", 0)
            weights(pe, "experts")
            filled_by(transposes(fill("ew2Ta"), [ew2[:, j, :] for j in range(4)], identf))
            filled_by(transposes(fill("ew2Tb"), [ew2[:, j, :] for j in (4, 5)], identf))
            for step, blocks, drain_of in (("w2oa", (0, 1, 2, 3), "ew2Ta"), ("w2ob", (4, 5), "ew2Tb")):
                drained(pe, drain_of)
                bank = fill(step)
                for n, j in enumerate(blocks):
                    ins = mm(chunk(bank, n), ew2T[:, j, :], outw, start=True, stop=True)
                filled_by(ins)
            front("router", 0)
            bank = fill("b2o")
            for e in range(E):
                ins = mm(chunk(bank, e), b2rep[:, e, :], outw, start=True, stop=True)
            filled_by(ins)
            weights(pe, "front", "rest")
            drained(pe, "b2o")
            pe.wait_ge(s_vzeros, VZEROS)

            iterations(run)


def kernel(x, cond_1024, ctx_1024, **w):
    import numpy as _np
    import concourse.bacc as _bacc
    from concourse.bass_utils import run_bass_kernel_spmd as _run

    first = {n[len("L0_xcond_"):]: _np.asarray(t) for n, t in w.items() if n.startswith("L0_xcond_")}
    second = {n[len("L1_xcond_"):]: _np.asarray(t) for n, t in w.items() if n.startswith("L1_xcond_")}

    def by_rows(t):
        return t.reshape(-1, P, t.shape[-1]).transpose(1, 0, 2)

    def by_feature(t):
        return t.reshape(*t.shape[:-1], NH, HD).swapaxes(-1, -2).reshape(t.shape)

    def lay(load, parts):
        assert list(LOADS[load]) == list(parts)
        return _np.concatenate([_np.ascontiguousarray(t).reshape(P, -1) for t in parts.values()], axis=1)

    def lay_over(load, parts):
        assert list(LOADS[load]) == list(parts)
        return _np.concatenate([t.reshape(-1) for t in parts.values()])

    w_qkv, b_qkv, w_kvc, b_kvc = second["W_qkv"], second["b_qkv"], second["W_kvc"], second["b_kvc"]
    hidden = _np.concatenate([first["e_w1"][e] for e in range(E)] + [first["gate_w1"]], axis=1)
    b_mod = second["b_mod"].reshape(6, H)
    arrays = {
        "x": _np.ascontiguousarray(x),
        "ctx": _np.ascontiguousarray(ctx_1024),
        "rows": _np.concatenate([t.reshape(-1, H) for t in (
            first["e_b1"], first["gate_b1"], first["ln_gamma"], first["ln_beta"], b_mod, by_feature(b_qkv[:H]),
            by_feature(b_qkv[H:2 * H]), by_feature(second["b_qc"]), by_feature(b_kvc[:H]), second["b_mlp1"],
            _np.asarray(cond_1024), first["e_b2"])]),
        "w_first": lay("w_first", {
            "Wq Wk Wv": _np.concatenate([first["Wq"], first["Wk"], first["Wv"]], axis=1),
            "router_W": by_rows(first["router_W"]),
            "W_kvc": _np.concatenate([by_feature(w_kvc[:, :H]), w_kvc[:, H:]], axis=1)}),
        "w_hidden": lay("w_hidden", {"w1": by_rows(hidden)}),
        "w_mod": lay("w_mod", {"W_mod": second["W_mod"]}),
        "w_experts": lay("w_experts", {"e_w2": by_rows(first["e_w2"].reshape(-1, H)), "out_w": first["out_w"]}),
        "w_front": lay("w_front", {
            "gate_w2": first["gate_w2"],
            "W_qkv": _np.concatenate([by_feature(w_qkv[:, :H]), by_feature(w_qkv[:, H:2 * H]), w_qkv[:, 2 * H:]],
                                     axis=1)}),
        "w_back": lay("w_back", {
            "W_proj": second["W_proj"], "W_qc": by_feature(second["W_qc"]), "W_cproj": second["W_cproj"],
            "W_mlp1": second["W_mlp1"], "W_mlp2": by_rows(second["W_mlp2"])}),
        "over_setup": lay_over("over_setup", {
            "router_b": first["router_b"], "b_kvc v": b_kvc[H:], "b_mod gates": b_mod[[2, 5]], "out_b": first["out_b"]}),
        "over_front": lay_over("over_front", {"gate_b2": first["gate_b2"], "b_qkv v": b_qkv[2 * H:]}),
        "over_back": lay_over("over_back", {
            "b_proj": second["b_proj"], "b_cproj": second["b_cproj"], "b_mlp2": second["b_mlp2"]}),
    }

    nc = _bacc.Bacc("TRN2", target_bir_lowering=False, num_devices=1)
    args = {name: nc.dram_tensor(f"in_{name}", t.shape, mybir.dt.from_np(t.dtype), kind="ExternalInput").ap()
            for name, t in arrays.items()}
    out = nc.dram_tensor("out", (NB, T, H), F32, kind="ExternalOutput").ap()
    build(nc, args, out)
    r = _run(nc, [{f"in_{name}": t for name, t in arrays.items()}], core_ids=[0])
    return r.results[0]["out"]
```

```python
from contextlib import ExitStack

import concourse.bass as bass
from concourse import mybir

ALU = mybir.AluOpType
ACT = mybir.ActivationFunctionType
AX_X = mybir.AxisListType.X
F32 = mybir.dt.float32
BF16 = mybir.dt.bfloat16

P = 128
NB = 4
C = 4
T = C * P
H = 128
S = 77
NH = 16
HD = H // NH
E = 3
G = 4
NG = NH // G
TILE = 32
KP = 96
SP_ = 96
ROW_M = 64
NZ = 7
RUNS = [(0, 3, 0, 0), (3, 5, 0, 1), (5, 6, 0, 2)]
LO, MID, HI = 0, 1, 2
SELF_SCALE = float(HD) ** -0.5
PROTO_SCALE = float(H) ** -0.5
LAG = 6
RING = 8

F_G, F_WR, F_VP, F_HB, F_SHA, F_SCA, F_RB, F_N = 0, S, S + E, S + E + H, S + E + H + NZ, S + E + H + NZ + 1, \
    S + E + H + NZ + 2, S + E + H + NZ + 2 + E
HIDDEN = [2 * E] + list(range(2 * E))
B_SHM, B_SCM, B_VC, B_N = 0, 1, 2, 2 + NH * TILE

LOADS = {
    "w_first": {"Wq Wk Wv": 3 * H, "router_W": 3 * E, "W_kvc": 2 * H},
    "w_hidden": {"w1": 3 * NZ * H},
    "w_mod": {"W_mod": 6 * H},
    "w_experts": {"e_w2": 2 * E * H, "out_w": H},
    "w_front": {"gate_w2": H, "W_qkv": 3 * H},
    "w_back": {"W_proj": H, "W_qc": H, "W_cproj": H, "W_mlp1": 4 * H, "W_mlp2": 4 * H},
    "over_setup": {"router_b": E, "b_kvc v": H, "b_mod gates": 2 * H, "out_b": H},
    "over_front": {"gate_b2": H, "b_qkv v": H},
    "over_back": {"b_proj": H, "b_cproj": H, "b_mlp2": H},
}
WIDTHS = {load: sum(parts.values()) for load, parts in LOADS.items()}
ROWS = ["b1"] + (NZ - 1) * [""] + ["gamma", "beta", "b_mod"] + 5 * [""] + ["b_q", "b_k", "b_qc", "b_kc", "b_mlp1"] + \
    3 * [""] + ["cond"] + (NB - 1) * [""] + ["e_b2"] + (E - 1) * [""]

FRONT = ["nxT", "scores", "wT", "evT", "router", "h0", "h1", "h2", "h3", "h4", "gate", "e0", "h5", "h6", "e1", "e2",
         "xnT", "k", "q", "v"]
BACK = ["cT", "qc", "cm"] + [f"{w}{g}" for g in range(NG) for w in ("cav", "co")] + \
    ["caT", "cproj", "xT", "m0", "m1", "m2", "m3", "mlp"]
DRAINS = {
    "front_v": [step for step in FRONT if step in ("router", "gate", "e0", "e1", "e2", "v")],
    "back_v": [step for step in BACK if step[:2] == "co" or step in ("cproj", "mlp")],
}
DRAINS["front_a"] = [step for step in FRONT if step not in DRAINS["front_v"]]
DRAINS["back_a"] = [step for step in BACK if step not in DRAINS["back_v"]]
NEEDS = {"scores": "nxT", "evT": "wT", "router": "evT", **{f"h{z}": "evT" for z in range(NZ)}, "k": "xnT", "q": "xnT",
         "v": "xnT", "qc": "cT", **{f"co{g}": f"cav{g}" for g in range(NG)}, "caT": "co3", "cproj": "caT",
         **{f"m{j}": "xT" for j in range(4)}}
OUT = ["o0", "o1", "o2", "o3", "aT", "proj"]

PLAN = {
    "T": {
        "front": """
            nxT@32.52 scores@33.5 wT@41.4 evT@42.23 router@45.37 h0@45.78 h1@48.63 h2@54.82 h3@56.25
            h4@57.1 gate@58.97 e0@59.9 h5@60.73 h6@63.8 e1@64.33 e2@64.47 xnT@69.25 k@70.8 q@73.4
            v@74.55
            """,
        "front of the first": """
            nxT@32.87 scores@38.55 wT@47.5 evT@52.83 router@58.62 h0@59.17 h1@59.18 h2@59.19 h3@59.47
            h4@59.48 gate@59.49 e0@62.5 h5@65.76 h6@66.92 e1@66.93 e2@66.94 xnT@66.95 k@72.11 q@73.12
            v@73.13
            """,
        "attn": """
            m0@42.67 m1@56.75 o0@63.65 m2@66.9 o1@76.6 m3@78.5 o2@87.1 av@97.97 o3@99.08 aT@101.07
            proj@103.9
            """,
        "back": """
            cT@12.37 qc@14.5 cn0@23.18 cn1@23.52 cn2@25.94 cn3@25.95 cn4@25.96 cn5@26.37 cn6@26.68
            cn7@26.88 cm@27.35 cs0@31.1 cs1@32.18 cav0@33.39 cs2@33.4 cs3@34.5 co0@36.65 cav1@37.8
            cs4@40.5 cs5@41.44 co1@41.45 cav2@43.73 cs6@43.74 cs7@44.25 co2@44.35 cav3@44.75 co3@45.18
            caT@47.77 cproj@48.5 xT@52.07 m0@52.73 m1@53.75 m2@54.03 m3@55.35 mlp@58.58
            """,
        "back of the last but one": """
            cT@12.24 qc@12.65 cn0@22.05 cn1@22.06 cn2@22.47 cn3@22.48 cn4@22.74 cn5@22.9 cn6@26.47
            cn7@26.48 cm@27.8 cs0@31.65 cs1@35.09 cav0@35.1 cs2@35.11 cs3@38.12 co0@38.13 cav1@38.14
            cs4@38.15 cs5@38.16 co1@38.17 cav2@38.18 cs6@38.19 cs7@38.2 co2@38.21 cav3@38.22 co3@41.48
            caT@41.67 cproj@45.05 xT@51.67 m0@54.22 m1@54.48 m2@54.49 m3@54.5 mlp@58.18
            """,
        "back of the last": """
            cT@11.32 qc@17.7 cn0@19.71 cn1@22.42 cn2@23.73 cn3@23.74 cn4@23.85 cn5@24.26 cn6@24.27
            cn7@24.88 cm@24.89 cs0@28.17 cs1@28.18 cav0@28.19 cs2@28.2 cs3@40.4 co0@40.41 cav1@46.42
            cs4@47.5 cs5@50.66 co1@50.67 cav2@50.68 cs6@50.69 cs7@50.7 co2@50.71 cav3@50.72 co3@50.73
            caT@50.74 cproj@50.75 xT@50.76 m0@50.77 m1@57.78 m2@57.79 m3@58.5 mlp@59.66
            """,
    },
    "V": {
        "back": """
            ln1@10.1 cT@11.6 cn0@22.18 cn1@23.52 cn2@25.02 cn3@25.03 cn4@25.04 cn5@25.45 cn6@25.76
            cn7@25.77 cm@25.78 co0@36.48 co1@41.18 co2@44.75 co3@45.52 cproj@48.35 ln2@48.65 xT@50.07
            mlp@59
            """,
        "back of the last but one": """
            ln1@7.85 cT@11.5 cn0@22.81 cn1@22.82 cn2@23.29 cn3@23.3 cn4@23.31 cn5@23.62 cn6@25.48
            cn7@25.49 cm@25.5 co0@35.33 co1@37.08 co2@37.5 co3@41.82 cproj@46.2 ln2@47.51 xT@50.52
            mlp@62.6
            """,
        "back of the last": """
            ln1@8.19 cT@8.2 qc@17.37 cn0@19.38 cn1@28.29 cn2@34.25 cn3@36.11 cn4@39.72 cn5@41.53
            cn6@41.54 cn7@46.15 cm@48.16 co0@48.17 co1@49.18 co2@49.19 co3@49.2 cproj@49.21 ln2@51.16
            xT@51.62 mlp@57.55
            """,
        "front": """
            ln0@25.5 nxT@32.1 scores@36.82 wT@39.52 router@44.93 probs@46.65 h1@51.43 h2@54.33 h3@56.67
            h4@58.65 gate@59.55 e0@59.9 h5@63.73 h6@64.37 h7@65.53 e1@65.69 e2@65.7 ln1@66.57 xnT@67.5
            q@73.4 v@75.25
            """,
        "front of the first": """
            ln0@27.1 nxT@36.5 scores@43.06 wT@45.62 router@58.88 probs@60.89 h1@60.9 h2@61.06 h3@61.07
            h4@63.98 gate@63.99 e0@67 h5@67.01 h6@67.02 h7@67.03 e1@67.04 e2@67.05 ln1@68.06 xnT@68.07
            q@70.08 v@73.39
            """,
        "attn": """
            m0@41.07 m1@54.07 o0@63 m2@65.73 o1@76.18 m3@77.82 o2@87.78 o3@99.1 proj@103.33
            """,
    },
    "A": {
        "front": """
            nxT@32.75 scores@37.27 wT@41.32 evT@42.25 router@46.14 h0@47.95 h1@49.63 h2@54.75 h3@56.33
            h4@57.67 gate@59.75 h5@60.48 h6@63.35 h7@63.91 xnT@69.2 k@69.8 q@73.8
            """,
        "front of the first": """
            nxT@32.95 scores@43.47 wT@46.22 evT@54.99 router@59.49 h0@59.5 h1@59.56 h2@59.57 h3@59.88
            h4@67.47 gate@67.48 h5@70.49 h6@70.5 h7@70.51 xnT@70.52 k@72.53 q@73.54
            """,
        "attn": """
            m0@42.35 m1@57.58 m2@68.65 m3@78.5 av@98.82 aT@102.9
            """,
        "back": """
            cT@11.97 qc@14.5 cm@27.2 cs0@32.65 cs1@32.66 cav0@33.63 cs2@33.97 cs3@34.9 cav1@37.63
            cs4@40.88 cs5@41.5 cav2@43.57 cs6@43.58 cs7@44.49 cav3@44.5 caT@47.6 xT@53.49 m0@53.9
            m1@53.91 m2@54.6 m3@55.52
            """,
        "back of the last but one": """
            cT@11.09 qc@12.5 cm@27.8 cs0@32.4 cs1@35.32 cav0@35.33 cs2@35.34 cs3@38.35 cav1@38.36
            cs4@38.37 cs5@38.38 cav2@38.39 cs6@38.4 cs7@38.41 cav3@38.42 caT@41.5 xT@54.5 m0@54.51
            m1@54.92 m2@55.66 m3@55.67
            """,
        "back of the last": """
            cT@11.32 qc@22.4 cm@28.51 cs0@28.52 cs1@28.58 cav0@39.73 cs2@39.74 cs3@39.75 cav1@39.76
            cs4@39.77 cs5@39.78 cav2@39.79 cs6@39.95 cs7@40.81 cav3@40.82 caT@40.83 xT@41.84 m0@41.85
            m1@50.76 m2@50.77 m3@55.52
            """,
    },
    "G": {
        "front": """
            ln0@34.5 probs@48.3 ln1@65.19 k@77
            """,
        "front of the first": """
            ln0@29.9 probs@59.85 ln1@68.44 k@68.45
            """,
        "back": """
            ln1@2.9 qc@10.65 caT@36.9 ln2@36.91 xT@48.77
            """,
        "back of the last but one": """
            ln1@5.25 qc@13.5 caT@42.25 ln2@50.5 xT@50.51
            """,
        "back of the last": """
            ln1@10.9 qc@32.25 caT@49.59 ln2@49.6 xT@49.61
            """,
    },
    "S": {
        "attn": """
            m0@47.1 m1@57.6 m2@67.73 m3@81.1
            """,
        "back": """
            ln1@8.2 qc@17.85 cm@28.2 mlp@65.55
            """,
        "back of the last but one": """
            ln1@11.5 qc@18.4 cm@25.45 mlp@65.25
            """,
        "back of the last": """
            ln1@7.75 qc@28.6 cm@28.61 mlp@72.2
            """,
        "front": """
            load@16.97 k@70.15 q@72.66
            """,
        "front of the first": """
            load@7.92 k@66.25 q@73.86
            """,
    },
}
CHAIN_START = {"front": -2, "attn": -1, "back": 1}
PLACES = 48
STANDS = {letter: {chain: [(word.split("@")[0], float(word.split("@")[1])) for word in text.split()]
                   for chain, text in chains.items()} for letter, chains in PLAN.items()}
EARLY = [step for step, at in STANDS["T"]["front"] if at < PLACES]


def variant(chain, batch):
    return {("front", 0): "front of the first", ("back", NB - 2): "back of the last but one",
            ("back", NB - 1): "back of the last"}.get((chain, batch), chain)


def places_of(letter, b):
    found = [[] for _ in range(PLACES)]
    for batch in range(NB):
        for chain, start in CHAIN_START.items():
            for step, at in STANDS[letter].get(variant(chain, batch), ()):
                at += PLACES * (batch + start - b)
                if 0 <= at < PLACES and not (batch == 0 and chain == "front" and step in FIRST):
                    found[int(at)].append((at, chain, step, batch))
    places = [[entry[1:] for entry in sorted(place)] for place in found]
    return [places[3 * s:3 * s + 3] for s in range(PLACES // 3)]


FIRST = ["load", "ln0", "nxT", "scores", "wT", "evT", "router"]
FOLD_SLOT = 5
BESIDE = 4
PAIR = 2


def do_place(place, engine):
    for chain, step, batch in place:
        if chain == "back":
            engine[chain](step, batch, batch < NB - 1)
        else:
            engine[chain](step, batch)


def iterations(run):
    for b in range(-2, NB + 2):
        run(b, has_attn=0 <= b < NB, has_front=0 <= b + 1 < NB)


def build(nc, a, out):
    ctx = ExitStack()
    with ctx:
        def sb(name, shape, dt=F32):
            return ctx.enter_context(nc.sbuf_tensor(name, shape, dt))

        w_first = sb("w_first", [P, WIDTHS["w_first"]])
        w_hidden = sb("w_hidden", [P, WIDTHS["w_hidden"]])
        w_front = sb("w_front", [P, WIDTHS["w_front"]])
        w_back = sb("w_back", [P, WIDTHS["w_back"]])
        over_front = sb("over_front", [P, WIDTHS["over_front"]])
        over_back = sb("over_back", [P, WIDTHS["over_back"]])
        w2o = sb("w2o", [P, 2 * E, H])
        cols = sb("cols", [P, len(ROWS)])
        b2oB = sb("b2oB", [P, E, H])
        identf = sb("identf", [P, P])
        identb = sb("identb", [P, P], BF16)
        minus_half = sb("minus_half", [P, C])
        of_head = sb("of_head", [3 * NH, NH], BF16)
        fpar_all = sb("fpar_all", [P, NB, F_N])
        bpar_all = sb("bpar_all", [P, NB, B_N])
        gates = sb("gates", [P, NB, 2, H])
        x = sb("x", [P, C, H])
        st = sb("st", [P, C, 6])
        mv = sb("mv", [P, C, 2])
        rstd = sb("rstd", [P, C])
        xh = sb("xh", [P, C, H])
        nxT = sb("nxT", [P, T])
        pm = sb("pm", [P, 4, C])
        pw = sb("pw", [P, C, S])
        lg = sb("lg", [P, 4, C, E])
        lm = sb("lm", [P, 3, C])
        wT = sb("wT", [P, T])
        evT = sb("evT", [P, T])
        z = sb("z", [P, NZ, T])
        th = sb("th", [P, 2, T])
        gz = sb("gz", [P, C, H])
        acc = sb("acc", [P, C, H])
        rb = acc
        rt = gz
        x0 = sb("x0", [P, C, H])
        xnT = nxT
        qf = sb("qf", [P, T])
        kf = sb("kf", [P, T])
        qp = sb("qp", [P, 3, T], BF16)
        kp = sb("kp", [P, 3, T], BF16)
        vst = sb("vst", [P, C, NH, HD])
        qS = sb("qS", [KP, NH, T], BF16)
        kS = sb("kS", [KP, NH, T], BF16)
        vS = sb("vS", [P, C, NH, TILE])
        mx = sb("mx", [P, C, NH])
        mr = sb("mr", [P, C, G])
        mp = sb("mp", [P, C, 3, G], BF16)
        mrow = sb("mrow", [3 * G, T], BF16)
        pT = sb("pT", [P, RING, T])
        oT = sb("oT", [P, T])
        rec = sb("rec", [P, C, G])
        an = sb("an", [P, C, NH, HD])
        aT = oT
        wpg = sb("wpg", [P, H])
        gbp = sb("gbp", [P, H])
        kcS = sb("kcS", [KP, NH, S], BF16)
        x1_two = sb("x1", [P, 2, C, H])
        bst = sb("bst", [P, C, 6])
        bmv = sb("bmv", [P, C, 2])
        brstd = sb("brstd", [P, C])
        bxh = sb("bxh", [P, C, H])
        cT = sb("cT", [P, T])
        coT = caT = mT = cT
        qcf = qf
        qcp = sb("qcp", [P, 3, T], BF16)
        qcS = sb("qcS", [KP, NH, T], BF16)
        cmx = sb("cmx", [P, C, NH])
        cmr = sb("cmr", [P, C, NH])
        cmp_ = sb("cmp", [P, C, 3, NH], BF16)
        cmrow = sb("cmrow", [3 * NH, T], BF16)
        cpT = sb("cpT", [SP_, G, T])
        crec = sb("crec", [P, C, G])
        can = sb("can", [P, C, NH, HD])
        hm = sb("hm", [P, 4, T])
        w2g = sb("w2g", [P, 4, H])
        gbm = sb("gbm", [P, H])
        spare = {"pT": [pT[:, :, :].rearrange("p r t -> p (r t)"), 0], "z": [z[:, :, :].rearrange("p z t -> p (z t)"), 0]}

        def within(where, *shape):
            n = 1
            for d in shape:
                n *= d
            t = spare[where][0][:, spare[where][1]:spare[where][1] + n]
            spare[where][1] += n
            return t.rearrange("p (j n) -> p j n", j=shape[0]) if len(shape) == 2 else t

        ew2T = within("pT", 2 * E, H)
        condrep, silurep = within("pT", NB, H), within("pT", NB, H)
        b2rep, ctxn = within("pT", E, H), within("pT", NB, H)
        ctxh, ctxT, ctxhT, kpT = within("z", NB, H), within("z", NB, S), within("pT", NB, S), within("z", NB, S)
        kcf, wq0T, silc = within("z", NB * S), within("z", H), within("z", NB)
        w_mod, over_setup = within("z", WIDTHS["w_mod"]), within("z", WIDTHS["over_setup"])
        rows, w_experts = within("pT", H), within("pT", WIDTHS["w_experts"])

        def part(name, *shape):
            for load, parts in LOADS.items():
                if name in parts:
                    at = sum(list(parts.values())[:list(parts).index(name)])
                    n = parts[name]
                    t = {"w_first": w_first, "w_hidden": w_hidden, "w_mod": w_mod, "w_experts": w_experts,
                         "w_front": w_front, "w_back": w_back, "over_setup": over_setup, "over_front": over_front,
                         "over_back": over_back}[load][:, at:at + n]
            return {1: lambda: t, 2: lambda: t.rearrange("p (j n) -> p j n", j=shape[0]),
                    3: lambda: t.rearrange("p (k j n) -> p k j n", k=shape[0], j=shape[1])}[len(shape)]()

        wqkv0, wr, wkvc = part("Wq Wk Wv", 3, H), part("router_W", 3, E), part("W_kvc", 2 * H)
        w1 = part("w1", 3, NZ, H)
        wmod, ew2, outw = part("W_mod", 6, H), part("e_w2", 2 * E, H), part("out_w", H)
        gw2, wqkv, wproj, wqc = part("gate_w2", H), part("W_qkv", 3 * H), part("W_proj", H), part("W_qc", H)
        wcproj, wm1, wm2 = part("W_cproj", H), part("W_mlp1", 4 * H), part("W_mlp2", 4, H)
        rbb, bvc, bgates, bout = part("router_b", E), part("b_kvc v", H), part("b_mod gates", 2, H), part("out_b", H)
        BC = {"gate_b2": part("gate_b2", H), "bv": part("b_qkv v", H), "bproj": part("b_proj", H),
              "bcproj": part("b_cproj", H), "bm2": part("b_mlp2", H)}
        kcp = within("z", 3 * NB * S // 2).bitcast(BF16).rearrange("p (j n) -> p j n", j=3)
        q_dram = nc.dram_tensor("q_parts", (3, P, T), BF16, kind="Internal").ap()
        k_dram = nc.dram_tensor("k_parts", (3, P, T), BF16, kind="Internal").ap()
        qc_dram = nc.dram_tensor("qc_parts", (3, P, T), BF16, kind="Internal").ap()
        m_dram = nc.dram_tensor("m_parts", (3 * G, T), BF16, kind="Internal").ap()
        cm_dram = nc.dram_tensor("cm_parts", (3 * NH, T), BF16, kind="Internal").ap()
        kc_dram = nc.dram_tensor("kc_parts", (3, P, NB * S), BF16, kind="Internal").ap()

        ps = ctx.enter_context(nc.psum_tensor("ps", [P, 8, T], F32))
        nat, sco, avb = ps[:, 0:2, :], ps[:, 2:4, :], ps[:, 4, :]
        xb, chain_banks = ps[:, 5, :], ps[:, 6:8, :]

        def front_width(step, b):
            return 2 if b <= (2 if step in EARLY else 1) else 1

        def front_bank(step, b):
            return chain_banks[:, FRONT.index(step) % front_width(step, b), :]

        def back_width(b):
            return {NB - 2: 2, NB - 1: 4}.get(b, 1)

        def back_bank(step, b):
            return ps[:, (7, 6, 4, 5)[BACK.index(step) % back_width(b)], :]

        def cross_bank(first, second, h, b):
            return (first, second)[h // PAIR % 2 if b == NB - 1 else 0][:, h % 2, :]

        def cross_banks(b):
            return 2 * PAIR if b == NB - 1 else PAIR

        def cross_tile(h, has_attn):
            return cpT[:, h % G, :] if has_attn or h < G else pT[:, h % RING, :]

        FRONT_VEC = ["stats", "aggr", "xhat", "pmax", "lg0", "pneg", "prec", "pnorm", "lmax", "lsub", "lsum", "lrec",
                     "probs"] + [f"silu{z}" for z in range(NZ)] + ["gated", "x0", "stats1", "aggr1", "xhat1", "qrest",
                                                                  "qpart2", "q_parts"]
        FRONT_POOL = ["eps", "rstd", "rb0", "rt1", "rb1", "rt2", "rb2", "eps1", "rstd1", "krest", "kpart2", "k_parts"]
        FRONT_ACT = ["rexp"] + [f"tanh{z}" for z in range(4)] + ["gate"] + [f"tanh{z}" for z in range(4, NZ)]
        BACK_VEC = ["stats1", "aggr1", "xhat1", "n1", "nrest", "n2", "n3", "stats2", "aggr2", "xhat2"]
        BACK_POOL = ["eps1", "rstd1", "qrest", "qpart2", "qc_parts", "x1b", "w2g", "gbm", "eps2", "rstd2", "x2gb"]
        ATTN_POOL = ["wpg", "gbp", "x0gb"]
        HALF = 2 * len(RUNS) + 1

        per = {
            "x_loaded": 16, "q_kept": 16, "k_kept": 16, "half0": 16 * HALF, "half1": 16 * HALF,
            **{f"{key[:-1]}drained_{key[-1]}": len(steps) for key, steps in DRAINS.items()},
            "front_filled": len(FRONT), "front_vec": len(FRONT_VEC), "front_pool": len(FRONT_POOL),
            "front_act": len(FRONT_ACT),
            "nat_scored": NH * C, "nat_reduced": NH * C, "s_scored": NH * C, "exp_done": NH * C, "av_used": NH * C,
            "av_drained": NG, "m_vec": 4 * NG, "m_filled": NG, "m_drained": NG, "m_kept": 16 * NG,
            "m_placed": 16 * NG, "o_filled": len(OUT), "o_drained": len(OUT), "o_vec": NG, "v_placed": 1,
            "attn_pool": len(ATTN_POOL), "kc_placed": 16 * (2 + len(RUNS)), "back_filled": len(BACK),
            "back_vec": len(BACK_VEC), "back_pool": len(BACK_POOL), "qc_kept": 16,
            "qc_placed": 16 * len(RUNS), "cn_scored": NH, "cn_reduced": NH, "cm_kept": 16, "cm_placed": 16,
            "cs_scored": NH, "cexp_done": NH, "gelu_done": 4, "co_vec": NG, "y_stored": 16,
        }
        sem = {name: ctx.enter_context(nc.semaphore(name)) for name in per}

        def upto(name, b, k):
            return (b + 1) * per[name] + k

        def begin(engine, names):
            for name in names:
                engine.sem_inc(sem[name], per[name])

        def after(engine, name, b, steps, step):
            engine.wait_ge(sem[name], upto(name, b, steps.index(step) + 1))

        def after_drain(engine, chain, b, step):
            who = "v" if step in DRAINS[f"{chain}_v"] else "a"
            after(engine, f"{chain}_drained_{who}", b, DRAINS[f"{chain}_{who}"], step)

        def after_batch(engine, chain, b):
            for who in "av":
                engine.wait_ge(sem[f"{chain}_drained_{who}"], upto(f"{chain}_drained_{who}", b + 1, 0))

        FILLS = ["cols", "ctxT", "ctxhT", "wq0T", "kpT", "G", "vp", "kc", "vc", "hb", "rbias", "mod", "gates0",
                 "gates1", "ew2Ta", "ew2Tb", "w2oa", "w2ob", "b2o"]
        SETUP_VEC = ["stats", "aggr", "cols", "ctxT", "ctxhat", "condrep", "b2rep", "ctxhT", "wq0T", "kpT", "G",
                     "wr", "vp", "kcf", "kpart1", "krest", "kpart2", "kc_parts", "vc", "hb", "rbias", "silurep",
                     "mod", "gates0", "gates1", "ew2Ta", "ew2Tb", "w2oa", "w2ob", "b2o"]
        s_filled = ctx.enter_context(nc.semaphore("setup_filled"))
        s_vec = ctx.enter_context(nc.semaphore("setup_vec"))
        s_silu = ctx.enter_context(nc.semaphore("setup_silu"))
        s_rstd = ctx.enter_context(nc.semaphore("setup_rstd"))
        s_consts = ctx.enter_context(nc.semaphore("constants_ready"))
        s_zeros = ctx.enter_context(nc.semaphore("zeros_ready"))
        s_vzeros = ctx.enter_context(nc.semaphore("vector_zeros_ready"))
        s_azeros = ctx.enter_context(nc.semaphore("scalar_zeros_ready"))
        kc_kept = ctx.enter_context(nc.semaphore("kc_kept"))
        SETUP_BANKS = 6
        last_q_split = ctx.enter_context(nc.semaphore("last_q_split"))
        s_heads = ctx.enter_context(nc.semaphore("of_head_ready"))
        CONSTS, ZEROS = 5, 6
        VZEROS = 5

        def filled(engine, step):
            engine.wait_ge(s_filled, FILLS.index(step) + 1)

        def drained(engine, step):
            engine.wait_ge(s_vec, SETUP_VEC.index(step) + 1)

        def fill_bank(step):
            return ps[:, FILLS.index(step) % SETUP_BANKS, :]

        loads = {
            "ctx": [(ctxn[0:S, :, :], a["ctx"].rearrange("b s h -> s b h"))],
            "rows": [(rows[0:len(ROWS), :], a["rows"])],
            "w0": [(w_first[:, :], a["w_first"])],
            "w1": [(w_hidden[:, :], a["w_hidden"])],
            "mod": [(over_setup, a["over_setup"].partition_broadcast(P)), (w_mod, a["w_mod"])],
            "experts": [(w_experts, a["w_experts"])],
            "front": [(over_front[:, :], a["over_front"].partition_broadcast(P)), (w_front[:, :], a["w_front"])],
            "rest": [(over_back[:, :], a["over_back"].partition_broadcast(P)), (w_back[:, :], a["w_back"])],
        }
        loaded = {w: ctx.enter_context(nc.semaphore(f"loaded_{w}")) for w in loads}

        def col(name, j=0, n=1):
            at = ROWS.index(name) + j
            return cols[:, at:at + n]

        def weights(engine, *when):
            for w in when:
                engine.wait_ge(loaded[w], 16 * len(loads[w]))

        def over(t, n):
            return t.unsqueeze(1).to_broadcast([t.shape[0], n, t.shape[1]])

        def along(t, n):
            return t.unsqueeze(len(t.shape)).to_broadcast([*t.shape, n])

        def chunk(t, c):
            return t[:, c * P:(c + 1) * P]

        def chunks(t):
            return t.rearrange("p (c h) -> p c h", c=C)

        m_bank = xb.bitcast(BF16)

        block = ctx.enter_context(nc.Block())

        @block.sync
        def _(sp):
            begin(sp, ["x_loaded", "q_kept", "k_kept", "half0", "half1", "m_kept", "m_placed",
                       "kc_placed", "qc_kept", "qc_placed", "cm_kept", "cm_placed", "y_stored"])

            def keep_context():
                drained(sp, "kc_parts")
                sp.dma_start(kc_dram.rearrange("j p n -> p j n"), kcp[:, :, :]).then_inc(kc_kept, 16)

            def run_of(parts, first, n):
                return parts[first:first + n].rearrange("j (d h) n -> (j d) h n", h=NH)

            def place_half(b, half):
                heads = slice(half * NH // 2, (half + 1) * NH // 2)
                if b == 0:
                    sp.wait_ge(s_zeros, ZEROS)
                    sp.wait_ge(s_vzeros, VZEROS)
                    sp.wait_ge(kc_kept, 16)
                sp.wait_ge(sem["s_scored"], upto("s_scored", b - 1, NH * C // 2 * (half + 1)))
                sp.wait_ge(sem["q_kept"], upto("q_kept", b, 16))
                sp.wait_ge(sem["k_kept"], upto("k_kept", b, 16))
                done = sem[f"half{half}"]
                for first, last, qpart, kpart in RUNS:
                    rows_t = slice(HD * first, HD * last)
                    sp.dma_start(qS[rows_t, heads, :], run_of(q_dram, qpart, last - first)[:, heads, :]
                                 ).then_inc(done, 16)
                    sp.dma_start(kS[rows_t, heads, :], run_of(k_dram, kpart, last - first)[:, heads, :]
                                 ).then_inc(done, 16)
                sp.dma_start(qS[ROW_M:ROW_M + 3, heads, :], kS[KP - 3:KP, 0:NH // 2, :]
                             ).then_inc(done, 16)

            def front(step, b):
                if step == "load":
                    after(sp, "front_vec", b - 1, FRONT_VEC, "x0")
                    sp.dma_start(x[:, :, :], a["x"][bass.ds(b, 1)].rearrange("o (p c) h -> p (o c) h", c=C)
                                 ).then_inc(sem["x_loaded"], 16)
                if step == "k":
                    after(sp, "front_pool", b, FRONT_POOL, "k_parts")
                    sp.wait_ge(sem["half1"], upto("half1", b - 1, 16 * HALF))
                    sp.dma_start(k_dram.rearrange("j p n -> p j n"), kp[:, :, :]).then_inc(sem["k_kept"], 16)
                if step == "q":
                    after(sp, "front_vec", b, FRONT_VEC, "q_parts")
                    sp.dma_start(q_dram.rearrange("j p n -> p j n"), qp[:, :, :]).then_inc(sem["q_kept"], 16)
                    place_half(b, 0)

            def attn(step, b):
                if step[0] == "m":
                    g = int(step[1])
                    after(sp, "m_drained", b, range(NG), g)
                    sp.wait_ge(sem["m_placed"], upto("m_placed", b, 16 * g))
                    sp.dma_start(m_dram, mrow[:, :]).then_inc(sem["m_kept"], 16)
                    sp.wait_ge(sem["m_kept"], upto("m_kept", b, 16 * (g + 1)))
                    sp.dma_start(qS[ROW_M:ROW_M + 3, g * G:g * G + G, :], m_dram.rearrange("(s h) n -> s h n", s=3)
                                 ).then_inc(sem["m_placed"], 16)

            def back(step, b, _):
                if step == "ln1":
                    sp.wait_ge(sem["cs_scored"], upto("cs_scored", b - 1, NH))
                    for first, last, _, kpart in RUNS:
                        sp.dma_start(kcS[HD * first:HD * last, :, :],
                                     run_of(kc_dram, kpart, last - first)[:, :, b * S:(b + 1) * S]
                                     ).then_inc(sem["kc_placed"], 16)
                    for half in range(2):
                        sp.dma_start(qcS[ROW_M:ROW_M + 3, half * NH // 2:(half + 1) * NH // 2, :],
                                     kS[KP - 3:KP, 0:NH // 2, :]
                                     ).then_inc(sem["kc_placed"], 16)
                if step == "qc":
                    if b == NB - 1:
                        sp.wait_ge(last_q_split, 3)
                    else:
                        after(sp, "back_pool", b, BACK_POOL, "qc_parts")
                    sp.dma_start(qc_dram.rearrange("j p n -> p j n"), qcp[:, :, :]).then_inc(sem["qc_kept"], 16)
                    sp.wait_ge(sem["qc_kept"], upto("qc_kept", b, 16))
                    for first, last, qpart, _ in RUNS:
                        sp.dma_start(qcS[HD * first:HD * last, :, :], run_of(qc_dram, qpart, last - first)
                                     ).then_inc(sem["qc_placed"], 16)
                if step == "cm":
                    first = BESIDE if b == NB - 1 else 0
                    after_drain(sp, "back", b, "cm")
                    sp.dma_start(cm_dram, cmrow[:, :]).then_inc(sem["cm_kept"], 16)
                    sp.wait_ge(sem["cm_kept"], upto("cm_kept", b, 16))
                    sp.dma_start(qcS[ROW_M:ROW_M + 3, first:, :],
                                 cm_dram.rearrange("(s h) n -> s h n", s=3)[:, first:, :]
                                 ).then_inc(sem["cm_placed"], 16)
                if step == "mlp":
                    after_drain(sp, "back", b, "mlp")
                    sp.dma_start(out[bass.ds(b, 1)].rearrange("o (p c) h -> p (o c) h", c=C), x1_two[:, b % 2, :, :]
                                 ).then_inc(sem["y_stored"], 16)

            def run(b, has_attn, has_front):
                if has_attn:
                    place_half(b, 1)
                for places in places_of("S", b):
                    for place in places:
                        do_place(place, {"front": front, "attn": attn, "back": back})

            for w, pairs in loads.items():
                for dst, src in pairs:
                    sp.dma_start(dst, src).then_inc(loaded[w], 16)
                if w == "w0":
                    front("load", 0)
            keep_context()
            iterations(run)
            sp.wait_ge(sem["y_stored"], upto("y_stored", NB - 1, 16))

        @block.gpsimd
        def _(pool):
            begin(pool, ["front_pool", "back_pool", "attn_pool"])

            def const(ins, sem_=s_consts):
                ins.then_inc(sem_, 1)

            const(nc.gpsimd.memset(identf[:, :], 0.0))
            const(nc.gpsimd.memset(identb[:, :], 0.0))
            pool.wait_ge(s_consts, 2)
            for m in (identf, identb):
                const(nc.gpsimd.affine_select(out=m[:, :], in_=m[:, :], compare_op=ALU.not_equal, fill=1.0,
                                              base=0, pattern=[[-1, P]], channel_multiplier=1))
            const(nc.gpsimd.memset(minus_half[:, :], -0.5))
            pool.wait_ge(s_consts, CONSTS)

            def inv_sqrt(done, steps, b, var, eps, out_, name_eps, name_rstd):
                nc.gpsimd.tensor_scalar(out_, var, eps, None, ALU.add).then_inc(sem[done], 1)
                after(pool, done, b, steps, name_eps)
                nc.gpsimd.tensor_tensor(out_, out_, minus_half[:, :], ALU.pow).then_inc(sem[done], 1)

            def front(step, b):
                def did(ins):
                    ins.then_inc(sem["front_pool"], 1)

                if step == "ln0":
                    after(pool, "front_vec", b, FRONT_VEC, "aggr")
                    inv_sqrt("front_pool", FRONT_POOL, b, mv[:, :, 1], 1e-5, rstd[:, :], "eps", "rstd")
                if step == "probs" and b == 0:
                    weights(pool, "front", "rest")
                    drained(pool, "b2o")
                if step == "probs":
                    after(pool, "front_vec", b, FRONT_VEC, "probs")
                    after(pool, "front_vec", b - 1, FRONT_VEC, "x0")
                    probs = lg[:, 3, :, :]
                    did(nc.gpsimd.tensor_tensor(rb[:, :, :], over(b2oB[:, 0, :], C), along(probs[:, :, 0], H), ALU.mult))
                    for e in (1, 2):
                        if e == 2:
                            after(pool, "front_pool", b, FRONT_POOL, "rb1")
                        did(nc.gpsimd.tensor_tensor(rt[:, :, :], over(b2oB[:, e, :], C), along(probs[:, :, e], H), ALU.mult))
                        after(pool, "front_pool", b, FRONT_POOL, f"rt{e}")
                        did(nc.gpsimd.tensor_tensor(rb[:, :, :], rb[:, :, :], rt[:, :, :], ALU.add))
                if step == "ln1":
                    after(pool, "front_vec", b, FRONT_VEC, "aggr1")
                    inv_sqrt("front_pool", FRONT_POOL, b, mv[:, :, 1], 1e-6, rstd[:, :], "eps1", "rstd1")
                if step == "k":
                    after_drain(pool, "front", b, "k")
                    did(nc.gpsimd.tensor_tensor(kf[:, :], kf[:, :], kp[:, HI, :], ALU.subtract))
                    after(pool, "front_pool", b, FRONT_POOL, "krest")
                    did(nc.gpsimd.tensor_scalar(kp[:, MID, :], kf[:, :], 1.0, 0.0, ALU.mult, ALU.add))
                    after(pool, "front_pool", b, FRONT_POOL, "kpart2")
                    did(nc.gpsimd.tensor_tensor(kp[:, LO, :], kf[:, :], kp[:, MID, :], ALU.subtract))

            def back(step, b, _):
                def did(ins):
                    ins.then_inc(sem["back_pool"], 1)

                if step == "ln1":
                    after(pool, "back_vec", b, BACK_VEC, "aggr1")
                    inv_sqrt("back_pool", BACK_POOL, b, bmv[:, :, 1], 1e-6, brstd[:, :], "eps1", "rstd1")
                if step == "qc" and b < NB - 1:
                    after_drain(pool, "back", b, "qc")
                    did(nc.gpsimd.tensor_tensor(qcf[:, :], qcf[:, :], qcp[:, 0, :], ALU.subtract))
                    after(pool, "back_pool", b, BACK_POOL, "qrest")
                    did(nc.gpsimd.tensor_scalar(qcp[:, 1, :], qcf[:, :], 1.0, 0.0, ALU.mult, ALU.add))
                    after(pool, "back_pool", b, BACK_POOL, "qpart2")
                    did(nc.gpsimd.tensor_tensor(qcp[:, 2, :], qcf[:, :], qcp[:, 1, :], ALU.subtract))
                if step == "qc":
                    after(pool, "back_vec", b, BACK_VEC, "xhat1")
                    x1 = x1_two[:, b % 2, :, :]
                    nc.gpsimd.tensor_tensor(x1, x1, over(BC["bcproj"], C), ALU.add
                                            ).then_inc(sem["back_pool"], 4 if b == NB - 1 else 1)
                if step == "caT":
                    after(pool, "back_filled", b - 1, BACK, "mlp")
                    gm = gates[:, bass.ds(b, 1), 1, :]
                    did(nc.gpsimd.tensor_tensor(w2g[:, :, :], wm2[:, :, :], gm.to_broadcast([P, 4, H]), ALU.mult))
                    after(pool, "back_pool", b - 1, BACK_POOL, "x2gb")
                    did(nc.gpsimd.tensor_tensor(gbm[:, :].unsqueeze(1), BC["bm2"].unsqueeze(1), gm, ALU.mult))
                if step == "xT":
                    after(pool, "back_vec", b, BACK_VEC, "xhat2")
                    did(nc.gpsimd.tensor_tensor(x1_two[:, b % 2, :, :], x1_two[:, b % 2, :, :], over(gbm[:, :], C), ALU.add))
                if step == "ln2":
                    after(pool, "back_vec", b, BACK_VEC, "aggr2")
                    inv_sqrt("back_pool", BACK_POOL, b, bmv[:, :, 1], 1e-6, brstd[:, :], "eps2", "rstd2")

            def fold(b):
                def did(ins):
                    ins.then_inc(sem["attn_pool"], 1)

                after(pool, "o_drained", b - 1, OUT, "proj")
                after(pool, "front_vec", b, FRONT_VEC, "x0")
                ga = gates[:, bass.ds(b, 1), 0, :]
                did(nc.gpsimd.tensor_tensor(wpg[:, :].unsqueeze(1), wproj.unsqueeze(1), ga, ALU.mult))
                did(nc.gpsimd.tensor_tensor(gbp[:, :].unsqueeze(1), BC["bproj"].unsqueeze(1), ga, ALU.mult))
                after(pool, "attn_pool", b, ATTN_POOL, "gbp")
                if b >= 2:
                    pool.wait_ge(sem["y_stored"], upto("y_stored", b - 2, 16))
                did(nc.gpsimd.tensor_tensor(x1_two[:, b % 2, :, :], x0[:, :, :], over(gbp[:, :], C), ALU.add))

            def mark_heads():
                same = identb[0:3 * NH, 0:3 * NH].rearrange("p (j h) -> p j h", j=3)
                nc.gpsimd.tensor_tensor(of_head[:, :], same[:, 0, :], same[:, 1, :], ALU.add).then_inc(s_heads, 1)
                pool.wait_ge(s_heads, 1)
                nc.gpsimd.tensor_tensor(of_head[:, :], of_head[:, :], same[:, 2, :], ALU.add).then_inc(s_heads, 1)

            def run(b, has_attn, has_front):
                for s, places in enumerate(places_of("G", b)):
                    if s == FOLD_SLOT and has_attn:
                        fold(b)
                    if s == FOLD_SLOT and b == NB - 1:
                        mark_heads()
                    for place in places:
                        do_place(place, {"front": front, "attn": lambda step, b: None, "back": back})

            drained(pool, "aggr")
            nc.gpsimd.tensor_scalar(rstd[0:S, :], mv[0:S, :, 1], 1e-6, None, ALU.add).then_inc(s_rstd, 1)
            pool.wait_ge(s_rstd, 1)
            nc.gpsimd.tensor_tensor(rstd[0:S, :], rstd[0:S, :], minus_half[0:S, :], ALU.pow).then_inc(s_rstd, 1)
            front("ln0", 0)
            after(pool, "front_pool", 0, FRONT_POOL, "rstd")
            pool.wait_ge(s_rstd, 2)
            const(nc.gpsimd.memset(cpT[2 * TILE:KP, :, :], 0.0), s_zeros)
            pool.wait_ge(s_zeros, 1)
            const(nc.gpsimd.memset(kcS[0:KP, :, :], 0.0), s_zeros)
            const(nc.gpsimd.memset(kS[0:KP, :, :].bitcast(F32), 0.0), s_zeros)
            const(nc.gpsimd.memset(qcS[0:KP, :, :].bitcast(F32), 0.0), s_zeros)
            pool.wait_ge(s_zeros, 4)
            const(nc.gpsimd.memset(kcS[ROW_M:ROW_M + 3, :, :], 1.0), s_zeros)
            const(nc.gpsimd.memset(kS[ROW_M:ROW_M + 3, :, :], 1.0), s_zeros)
            pool.wait_ge(s_zeros, ZEROS)

            iterations(run)

        @block.scalar
        def _(act):
            begin(act, ["front_drained_a", "front_act", "exp_done", "av_drained", "m_drained", "o_drained",
                        "back_drained_a", "cexp_done", "gelu_done"])

            def drain(out_, in_, done, **kw):
                nc.scalar.activation(out_, in_, ACT.Identity if kw else ACT.Copy, **kw).then_inc(sem[done], 1)

            def front(step, b):
                fb = front_bank(step, b) if step in FRONT else None
                done = "front_drained_a"
                if step in FRONT:
                    after(act, "front_filled", b, FRONT, step)
                if step == "nxT":
                    drain(nxT[:, :], fb, done, scale=col("gamma"), bias=col("beta"))
                if step == "scores":
                    after(act, "front_vec", b, FRONT_VEC, "pneg")
                    for c in range(C):
                        ins = nc.scalar.activation(pw[:, c, :], fb[:, c * (S + E):c * (S + E) + S], ACT.Exp,
                                                   bias=pm[:, 1, c:c + 1], scale=PROTO_SCALE,
                                                   accum_out=pm[:, 2, c:c + 1])
                    ins.then_inc(sem[done], 1)
                if step == "wT":
                    drain(wT[0:S, :], fb[0:S, :], done)
                if step == "evT":
                    drain(evT[:, :], fb, done)
                if step == "router":
                    after(act, "front_vec", b, FRONT_VEC, "lsub")
                    nc.scalar.activation(lg[:, 2, :, :], lg[:, 1, :, :], ACT.Exp).then_inc(sem["front_act"], 1)
                if step[0] == "h":
                    n = int(step[1])
                    if n == 0 and b == 0:
                        drained(act, "b2o")
                        act.wait_ge(kc_kept, 16)
                    if n < NZ:
                        zi = HIDDEN[n]
                        drain(z[:, zi, :], fb, done, bias=fpar_all[:, b, F_HB + zi:F_HB + zi + 1])
                    if n:
                        after_drain(act, "front", b, f"h{n - 1}")
                        if n > 2:
                            after(act, "front_vec", b, FRONT_VEC, f"silu{n - 3}")
                        else:
                            after(act, "front_vec", b - 1, FRONT_VEC, f"silu{NZ - 1}")
                        nc.scalar.activation(th[:, n % 2, :], z[:, HIDDEN[n - 1], :], ACT.Tanh, scale=0.5
                                             ).then_inc(sem["front_act"], 1)
                if step == "gate":
                    after_drain(act, "front", b, "gate")
                    nc.scalar.activation(gz[:, :, :], gz[:, :, :], ACT.Tanh, scale=0.5).then_inc(sem["front_act"], 1)
                if step == "xnT":
                    drain(xnT[:, :], fb, done, scale=fpar_all[:, b, F_SCA:F_SCA + 1], bias=fpar_all[:, b, F_SHA:F_SHA + 1])
                if step in ("q", "k"):
                    part, whole = (qp[:, 0, :], qf) if step == "q" else (kp[:, HI, :], kf)
                    bias = col(f"b_{step}")
                    after(act, f"{step}_kept", b - 1, range(16), 15)
                    if step == "q" and b >= 2:
                        after(act, "back_pool", b - 2, BACK_POOL, "qc_parts")
                    nc.scalar.activation(part, fb, ACT.Identity, bias=bias)
                    drain(whole[:, :], fb, done, bias=bias)

            def attn(step, b):
                if step == "av":
                    take(b, NG - 1)
                if step[0] == "m":
                    g = int(step[1])
                    after(act, "m_filled", b, range(NG), g)
                    act.wait_ge(sem["m_kept"], upto("m_kept", b, 16 * g))
                    drain(mrow[:, :], m_bank[0:3 * G, 0:T], "m_drained")
                if step == "aT":
                    after(act, "o_filled", b, OUT, "aT")
                    drain(aT[:, :], xb, "o_drained")

            def take(b, g):
                act.wait_ge(sem["av_used"], upto("av_used", b, G * C * (g + 1)))
                if g == 0:
                    after(act, "o_filled", b - 1, OUT, "proj")
                else:
                    after(act, "o_filled", b, OUT, f"o{g - 1}")
                drain(oT[:, :], avb, "av_drained")

            def back(step, b, has_attn):
                bb = back_bank(step, b) if step in BACK else None
                done = "back_drained_a"
                if step in BACK:
                    after(act, "back_filled", b, BACK, step)
                if step == "cT":
                    drain(cT[:, :], bb, done)
                if step == "qc":
                    after(act, "qc_kept", b - 1, range(16), 15)
                    after(act, "front_vec", min(b + 1, NB - 1), FRONT_VEC, "q_parts")
                    nc.scalar.activation(qcp[:, 0, :], bb, ACT.Identity, bias=col("b_qc"))
                    drain(qcf[:, :], bb, done, bias=col("b_qc"))
                if step == "cm":
                    act.wait_ge(sem["cm_kept"], upto("cm_kept", b - 1, 16))
                    drain(cmrow[:, :], bb.bitcast(BF16)[0:3 * NH, 0:T], done)
                if step[:2] == "cs":
                    first = PAIR * int(step[2])
                    g = first // G
                    if has_attn or g == 0 or g == 3:
                        after(act, "back_filled", b if g else b - 1, BACK, f"cav{(g - 1) % NG}")
                    for i in range(first, first + PAIR):
                        act.wait_ge(sem["cs_scored"], upto("cs_scored", b, i + 1))
                        nc.scalar.activation(cross_tile(i, has_attn)[0:S, :], cross_bank(sco, nat, i, b)[0:S, :],
                                             ACT.Exp, scale=SELF_SCALE).then_inc(sem["cexp_done"], 1)
                if step[:3] == "cav":
                    drain(coT[:, :], bb, done)
                if step == "caT":
                    drain(caT[:, :], bb, done)
                if step == "xT":
                    drain(mT[:, :], bb, done, scale=bpar_all[:, b, B_SCM:B_SCM + 1], bias=bpar_all[:, b, B_SHM:B_SHM + 1])
                if step in ("m0", "m1", "m2", "m3"):
                    j = int(step[1])
                    if b == NB - 1:
                        nc.scalar.activation(hm[:, j, :], bb, ACT.Gelu_apprx_tanh, bias=col("b_mlp1", j)
                                             ).then_inc(sem[done], 1)
                        return
                    drain(hm[:, j, :], bb, done, bias=col("b_mlp1", j))
                    if j == 3:
                        after_drain(act, "back", b, "m3")
                        for j in range(4):
                            nc.scalar.activation(hm[:, j, :], hm[:, j, :], ACT.Gelu_apprx_tanh
                                                 ).then_inc(sem["gelu_done"], 1)

            def exps(b, s, pair):
                for hh in (2 * pair, 2 * pair + 1):
                    j = s * G + hh
                    act.wait_ge(sem["s_scored"], upto("s_scored", b, j + 1))
                    act.wait_ge(sem["av_used"], upto("av_used", b, j + 1 - RING))
                    nc.scalar.activation(pT[:, j % RING, :], sco[:, j % 2, :], ACT.Exp, scale=SELF_SCALE
                                         ).then_inc(sem["exp_done"], 1)

            def run(b, has_attn, has_front):
                engine = {"front": front, "attn": attn, "back": back}
                for s, places in enumerate(places_of("A", b)):
                    for n, place in enumerate(places):
                        if has_attn and n < 2:
                            exps(b, s, n)
                        if has_attn and n == 2 and s % C == 0 and s:
                            take(b, s // C - 1)
                        do_place(place, engine)

            act.wait_ge(s_consts, CONSTS)
            for zeros in (qS[:, :, :].rearrange("p h t -> p (h t)").bitcast(F32),
                          vS[:, :, :, :].rearrange("p c h n -> p (c h n)")):
                nc.scalar.activation(zeros, identf[0:zeros.shape[0], 0:1].to_broadcast(list(zeros.shape)), ACT.Copy,
                                     scale=0.0).then_inc(s_azeros, 1)
            drained(act, "cols")
            nc.scalar.activation(silc[:, :], col("cond", 0, NB), ACT.Silu).then_inc(s_silu, 1)
            front("nxT", 0)
            front("scores", 0)
            act.wait_ge(s_vzeros, 3)
            for step in ("wT", "evT", "router"):
                front(step, 0)
            iterations(run)

        @block.vector
        def _(dve):
            begin(dve, ["front_drained_v", "back_drained_v", "front_vec", "nat_reduced", "m_vec", "o_vec", "v_placed",
                        "back_vec", "cn_reduced", "co_vec"])

            def zero(ins):
                ins.then_inc(s_vzeros, 1)

            def setup(ins):
                ins.then_inc(s_vec, 1)

            vc_all = bpar_all[:, :, B_VC:B_N].rearrange("p b (h n) -> p b h n", n=TILE)

            def stats(src, st_, mv_, done, steps, b, name):
                for c in range(C):
                    ins = nc.vector.bn_stats(st_[:, c, :], src[:, c, :])
                ins.then_inc(sem[done], 1)
                after(dve, done, b, steps, name)
                for c in range(C):
                    ins = nc.vector.bn_aggr(mv_[:, c, :], st_[:, c, :])
                ins.then_inc(sem[done], 1)

            def normalize(out_, src, mv_, rstd_, done):
                for c in range(C):
                    ins = nc.vector.tensor_scalar(out_[:, c, :], src[:, c, :], mv_[:, c, 0:1], rstd_[:, c:c + 1],
                                                  ALU.subtract, ALU.mult)
                ins.then_inc(sem[done], 1)

            def front(step, b):
                fb = front_bank(step, b) if step in FRONT else None
                def did(ins):
                    ins.then_inc(sem["front_vec"], 1)

                def wait(name):
                    after(dve, "front_vec", b, FRONT_VEC, name)

                if step in ("router", "gate", "e0", "e1", "e2", "v", "scores"):
                    after(dve, "front_filled", b, FRONT, step)
                if step == "ln0":
                    dve.wait_ge(sem["x_loaded"], upto("x_loaded", b, 16))
                    stats(x, st, mv, "front_vec", FRONT_VEC, b, "stats")
                if step == "nxT":
                    after(dve, "front_pool", b, FRONT_POOL, "rstd")
                    normalize(xh, x, mv, rstd, "front_vec")
                if step == "scores":
                    sc = fb[:, 0:C * (S + E)].rearrange("p (c n) -> p c n", c=C)
                    did(nc.vector.reduce_max(pm[:, 0, :], sc[:, :, 0:S], AX_X))
                    did(nc.vector.tensor_tensor(lg[:, 0, :, :], sc[:, :, S:S + E],
                                                over(fpar_all[:, b, F_RB:F_RB + E], C), ALU.add))
                    wait("pmax")
                    did(nc.vector.tensor_scalar(pm[:, 1, :], pm[:, 0, :], -PROTO_SCALE, None, ALU.mult))
                if step == "wT":
                    after_drain(dve, "front", b, "scores")
                    did(nc.vector.reciprocal(pm[:, 3, :], pm[:, 2, :]))
                    wait("prec")
                    did(nc.vector.tensor_tensor(pw[:, :, :], pw[:, :, :], along(pm[:, 3, :], S), ALU.mult))
                if step == "router":
                    nc.vector.tensor_tensor(lg[:, 1, :, :], fb[:, 0:C * E].rearrange("p (c e) -> p c e", c=C),
                                            lg[:, 0, :, :], ALU.add).then_inc(sem["front_drained_v"], 1)
                    after_drain(dve, "front", b, "router")
                    did(nc.vector.reduce_max(lm[:, 0, :], lg[:, 1, :, :], AX_X))
                    wait("lmax")
                    did(nc.vector.tensor_tensor(lg[:, 1, :, :], lg[:, 1, :, :], along(lm[:, 0, :], E), ALU.subtract))
                if step == "probs":
                    after(dve, "front_act", b, FRONT_ACT, "rexp")
                    did(nc.vector.reduce_sum(lm[:, 1, :], lg[:, 2, :, :], AX_X))
                    wait("lsum")
                    did(nc.vector.reciprocal(lm[:, 2, :], lm[:, 1, :]))
                    wait("lrec")
                    did(nc.vector.tensor_tensor(lg[:, 3, :, :], lg[:, 2, :, :], along(lm[:, 2, :], E), ALU.mult))
                if step == "gate":
                    after(dve, "front_pool", b, FRONT_POOL, "rb2")
                    nc.vector.tensor_tensor(gz[:, :, :], chunks(fb), over(BC["gate_b2"], C), ALU.add
                                            ).then_inc(sem["front_drained_v"], 1)
                if step in ("e0", "e1", "e2"):
                    e = int(step[1])
                    if e == 0:
                        after(dve, "front_pool", b, FRONT_POOL, "rb2")
                    else:
                        after_drain(dve, "front", b, f"e{e - 1}")
                    for c in range(C):
                        ins = nc.vector.scalar_tensor_tensor(acc[:, c, :], chunk(fb, c), lg[:, 3, c, e:e + 1],
                                                             acc[:, c, :], ALU.mult, ALU.add)
                    ins.then_inc(sem["front_drained_v"], 1)
                if step[0] == "h" and step != "h0":
                    n = int(step[1])
                    after(dve, "front_act", b, FRONT_ACT, f"tanh{n - 1}")
                    hidden = z[:, HIDDEN[n - 1], :]
                    did(nc.vector.scalar_tensor_tensor(hidden, th[:, n % 2, :], 1.0, hidden, ALU.add, ALU.mult))
                if step == "ln1":
                    after_drain(dve, "front", b, "e2")
                    after(dve, "front_act", b, FRONT_ACT, "gate")
                    did(nc.vector.scalar_tensor_tensor(acc[:, :, :], gz[:, :, :], 1.0, acc[:, :, :], ALU.add, ALU.mult))
                    wait("gated")
                    after(dve, "attn_pool", b - 1, ATTN_POOL, "x0gb")
                    did(nc.vector.scalar_tensor_tensor(x0[:, :, :], acc[:, :, :], 0.5, x[:, :, :], ALU.mult, ALU.add))
                    wait("x0")
                    stats(x0, st, mv, "front_vec", FRONT_VEC, b, "stats1")
                if step == "xnT":
                    after(dve, "front_pool", b, FRONT_POOL, "rstd1")
                    normalize(xh, x0, mv, rstd, "front_vec")
                if step == "q":
                    after_drain(dve, "front", b, "q")
                    did(nc.vector.tensor_tensor(qf[:, :], qf[:, :], qp[:, 0, :], ALU.subtract))
                    wait("qrest")
                    did(nc.vector.tensor_copy(qp[:, 1, :], qf[:, :]))
                    wait("qpart2")
                    did(nc.vector.tensor_tensor(qp[:, 2, :], qf[:, :], qp[:, 1, :], ALU.subtract))
                if step == "v":
                    nc.vector.tensor_tensor(vst[:, :, :, :].rearrange("p c h d -> p c (h d)"), chunks(fb),
                                            over(BC["bv"], C), ALU.add).then_inc(sem["front_drained_v"], 1)

            def attn(step, b):
                if step[0] == "m":
                    g = int(step[1])
                    src = mx[:, :, g * G:(g + 1) * G]
                    did = sem["m_vec"]
                    dve.wait_ge(sem["nat_reduced"], upto("nat_reduced", b, C * G * (g + 1)))
                    if g:
                        after(dve, "m_filled", b, range(NG), g - 1)
                    else:
                        after(dve, "m_filled", b - 1, range(NG), NG - 1)
                    nc.vector.tensor_scalar(mp[:, :, 0, :], src, -1.0, None, ALU.mult).then_inc(did, 1)
                    dve.wait_ge(did, upto("m_vec", b, 4 * g + 1))
                    nc.vector.scalar_tensor_tensor(mr[:, :, :], src, -1.0, mp[:, :, 0, :], ALU.mult, ALU.subtract
                                                   ).then_inc(did, 1)
                    dve.wait_ge(did, upto("m_vec", b, 4 * g + 2))
                    nc.vector.tensor_copy(mp[:, :, 1, :], mr[:, :, :]).then_inc(did, 1)
                    dve.wait_ge(did, upto("m_vec", b, 4 * g + 3))
                    nc.vector.tensor_tensor(mp[:, :, 2, :], mr[:, :, :], mp[:, :, 1, :], ALU.subtract).then_inc(did, 1)
                if step in ("o0", "o1", "o2", "o3"):
                    g = int(step[1])
                    after(dve, "o_filled", b, OUT, step)
                    bank = xb.rearrange("p (c g n) -> p c g n", c=C, g=G)
                    nc.vector.reciprocal(rec[:, :, :], bank[:, :, :, HD]).then_inc(sem["o_vec"], 1)
                    after(dve, "o_vec", b, range(NG), g)
                    nc.vector.tensor_tensor(an[:, :, g * G:(g + 1) * G, :], bank[:, :, :, 0:HD], along(rec[:, :, :], HD),
                                            ALU.mult).then_inc(sem["o_drained"], 1)
                if step == "proj":
                    after(dve, "o_filled", b, OUT, "proj")
                    after(dve, "attn_pool", b, ATTN_POOL, "x0gb")
                    nc.vector.tensor_tensor(x1_two[:, b % 2, :, :], chunks(xb), x1_two[:, b % 2, :, :],
                                            ALU.add).then_inc(sem["o_drained"], 1)

            def back(step, b, _):
                bb = back_bank(step, b) if step in BACK else None
                def did(ins):
                    ins.then_inc(sem["back_vec"], 1)

                def wait(name):
                    after(dve, "back_vec", b, BACK_VEC, name)

                done = "back_drained_v"
                if step == "ln1":
                    after(dve, "o_drained", b, OUT, "proj")
                    stats(x1_two[:, b % 2, :, :], bst, bmv, "back_vec", BACK_VEC, b, "stats1")
                if step == "cT":
                    after(dve, "back_pool", b, BACK_POOL, "rstd1")
                    normalize(bxh, x1_two[:, b % 2, :, :], bmv, brstd, "back_vec")
                if step == "qc":
                    after_drain(dve, "back", b, "qc")
                    nc.vector.tensor_tensor(qcf[:, :], qcf[:, :], qcp[:, 0, :], ALU.subtract).then_inc(last_q_split, 1)
                    dve.wait_ge(last_q_split, 1)
                    nc.vector.tensor_copy(qcp[:, 1, :], qcf[:, :]).then_inc(last_q_split, 1)
                    dve.wait_ge(last_q_split, 2)
                    nc.vector.tensor_tensor(qcp[:, 2, :], qcf[:, :], qcp[:, 1, :], ALU.subtract
                                            ).then_inc(last_q_split, 1)
                if step[:2] == "cn":
                    for h in range(PAIR * int(step[2]), PAIR * int(step[2]) + PAIR):
                        dve.wait_ge(sem["cn_scored"], upto("cn_scored", b, h + 1))
                        scores = cross_bank(nat, sco, h, b)[:, 0:C * S].rearrange("p (c s) -> p c s", c=C)
                        nc.vector.reduce_max(cmx[:, :, h], scores, AX_X).then_inc(sem["cn_reduced"], 1)
                if step == "cm":
                    dve.wait_ge(sem["cn_reduced"], upto("cn_reduced", b, NH))
                    did(nc.vector.tensor_scalar(cmp_[:, :, 0, :], cmx[:, :, :], -1.0, None, ALU.mult))
                    wait("n1")
                    did(nc.vector.scalar_tensor_tensor(cmr[:, :, :], cmx[:, :, :], -1.0, cmp_[:, :, 0, :],
                                                       ALU.mult, ALU.subtract))
                    wait("nrest")
                    did(nc.vector.tensor_copy(cmp_[:, :, 1, :], cmr[:, :, :]))
                    wait("n2")
                    did(nc.vector.tensor_tensor(cmp_[:, :, 2, :], cmr[:, :, :], cmp_[:, :, 1, :], ALU.subtract))
                if step[:2] == "co":
                    g = int(step[2])
                    after(dve, "back_filled", b, BACK, step)
                    bank = bb.rearrange("p (c g n) -> p c g n", c=C, g=G)
                    if g:
                        after_drain(dve, "back", b, f"co{g - 1}")
                    nc.vector.reciprocal(crec[:, :, :], bank[:, :, :, HD]).then_inc(sem["co_vec"], 1)
                    after(dve, "co_vec", b, range(NG), g)
                    nc.vector.tensor_tensor(can[:, :, g * G:(g + 1) * G, :], bank[:, :, :, 0:HD], along(crec[:, :, :], HD),
                                            ALU.mult).then_inc(sem[done], 1)
                if step == "cproj":
                    after(dve, "back_filled", b, BACK, "cproj")
                    after(dve, "back_pool", b, BACK_POOL, "x1b")
                    x1 = x1_two[:, b % 2, :, :]
                    nc.vector.tensor_tensor(x1, chunks(bb), x1, ALU.add).then_inc(sem[done], 1)
                if step == "ln2":
                    after_drain(dve, "back", b, "cproj")
                    stats(x1_two[:, b % 2, :, :], bst, bmv, "back_vec", BACK_VEC, b, "stats2")
                if step == "xT":
                    after(dve, "back_pool", b, BACK_POOL, "rstd2")
                    normalize(bxh, x1_two[:, b % 2, :, :], bmv, brstd, "back_vec")
                if step == "mlp":
                    after(dve, "back_filled", b, BACK, "mlp")
                    after(dve, "back_pool", b, BACK_POOL, "x2gb")
                    x1 = x1_two[:, b % 2, :, :]
                    nc.vector.tensor_tensor(x1, chunks(bb), x1, ALU.add).then_inc(sem[done], 1)

            def maxima(b, h, pair):
                for c in (2 * pair, 2 * pair + 1):
                    dve.wait_ge(sem["nat_scored"], upto("nat_scored", b, h * C + c + 1))
                    nc.vector.reduce_max(mx[:, c, h:h + 1], nat[:, c % 2, :], AX_X).then_inc(sem["nat_reduced"], 1)

            def place_v(b):
                dve.wait_ge(sem["av_used"], upto("av_used", b - 1, NH * C))
                after_drain(dve, "front", b, "v")
                nc.vector.tensor_copy(vS[:, :, :, 0:HD].rearrange("p c h d -> p (c h) d"),
                                      vst[:, :, :, :].rearrange("p c h d -> p (c h) d")
                                      ).then_inc(sem["v_placed"], 1)

            def run(b, has_attn, has_front):
                engine = {"front": front, "attn": attn, "back": back}
                for s, places in enumerate(places_of("V", b)):
                    ahead = (b, s + LAG, has_attn) if s + LAG < NH else (b + 1, s + LAG - NH, has_front)
                    for n, place in enumerate(places):
                        if ahead[2] and n < 2:
                            maxima(ahead[0], ahead[1], n)
                        if has_attn and s == 0 and n == 2:
                            place_v(b)
                        do_place(place, engine)

            zero(nc.vector.memset(fpar_all[:, :, :], 0.0))
            zero(nc.vector.memset(bpar_all[:, :, :], 0.0))
            zero(nc.vector.memset(wT[2 * TILE:KP, :], 0.0))
            dve.wait_ge(s_vzeros, 3)
            weights(dve, "ctx")
            for b in range(NB):
                ins = nc.vector.bn_stats(st[0:S, b, :], ctxn[0:S, b, :])
            setup(ins)
            drained(dve, "stats")
            for b in range(NB):
                ins = nc.vector.bn_aggr(mv[0:S, b, :], st[0:S, b, :])
            setup(ins)
            filled(dve, "cols")
            setup(nc.vector.tensor_copy(cols[:, 0:len(ROWS)], fill_bank("cols")[:, 0:len(ROWS)]))
            filled(dve, "ctxT")
            setup(nc.vector.tensor_copy(ctxT[:, :, :].rearrange("p b s -> p (b s)"), fill_bank("ctxT")[:, 0:NB * S]))
            dve.wait_ge(s_rstd, 2)
            drained(dve, "aggr")
            for b in range(NB):
                ins = nc.vector.tensor_scalar(ctxh[0:S, b, :], ctxn[0:S, b, :], mv[0:S, b, 0:1], rstd[0:S, b:b + 1],
                                              ALU.subtract, ALU.mult)
            setup(ins)
            front("ln0", 0)
            drained(dve, "cols")
            setup(nc.vector.tensor_copy(condrep[:, :, :], along(col("cond", 0, NB), H)))
            setup(nc.vector.tensor_copy(b2rep[:, :, :], along(col("e_b2", 0, E), H)))
            filled(dve, "ctxhT")
            setup(nc.vector.tensor_copy(ctxhT[:, :, :].rearrange("p b s -> p (b s)"), fill_bank("ctxhT")[:, 0:NB * S]))
            filled(dve, "wq0T")
            setup(nc.vector.tensor_copy(wq0T[:, :], fill_bank("wq0T")[:, 0:H]))
            front("nxT", 0)
            filled(dve, "kpT")
            setup(nc.vector.tensor_copy(kpT[:, :, :].rearrange("p b s -> p (b s)"), fill_bank("kpT")[:, 0:NB * S]))
            filled(dve, "G")
            setup(nc.vector.tensor_copy(fpar_all[:, :, F_G:F_G + S],
                                        fill_bank("G")[:, 0:NB * S].rearrange("p (b s) -> p b s", b=NB)))
            weights(dve, "w0")
            setup(nc.vector.tensor_copy(fpar_all[:, :, F_WR:F_WR + E],
                                        wr[:, 0:1, :].to_broadcast([P, NB, E])))
            filled(dve, "vp")
            setup(nc.vector.tensor_copy(fpar_all[0:S, :, F_VP:F_VP + H],
                                        fill_bank("vp")[0:S, :].rearrange("p (b h) -> p b h", b=NB)))
            filled(dve, "kc")
            setup(nc.vector.tensor_scalar(kcf[:, :], fill_bank("kc")[:, 0:NB * S], col("b_kc"), None, ALU.add))
            drained(dve, "kcf")
            setup(nc.vector.tensor_copy(kcp[:, HI, :], kcf[:, :]))
            drained(dve, "kpart1")
            setup(nc.vector.tensor_tensor(kcf[:, :], kcf[:, :], kcp[:, HI, :], ALU.subtract))
            drained(dve, "krest")
            setup(nc.vector.tensor_copy(kcp[:, MID, :], kcf[:, :]))
            drained(dve, "kpart2")
            setup(nc.vector.tensor_tensor(kcp[:, LO, :], kcf[:, :], kcp[:, MID, :], ALU.subtract))
            filled(dve, "vc")
            weights(dve, "mod")
            for b in range(NB):
                ins = nc.vector.tensor_tensor(vc_all[0:S, b, :, 0:HD],
                                              chunk(fill_bank("vc"), b)[0:S, :].rearrange("p (h d) -> p h d", d=HD),
                                              bvc[0:S, :].rearrange("p (h d) -> p h d", d=HD), ALU.add)
            setup(ins)
            filled(dve, "hb")
            setup(nc.vector.tensor_tensor(fpar_all[:, :, F_HB:F_HB + NZ],
                                          fill_bank("hb")[:, 0:NZ * NB].rearrange("p (z b) -> p b z", b=NB),
                                          over(cols[:, 0:NZ], NB), ALU.add))
            filled(dve, "rbias")
            setup(nc.vector.tensor_tensor(fpar_all[:, :, F_RB:F_RB + E],
                                          fill_bank("rbias")[:, 0:NB * E].rearrange("p (b e) -> p b e", e=E),
                                          over(rbb, NB), ALU.add))
            drained(dve, "rbias")
            front("scores", 0)
            dve.wait_ge(s_silu, 1)
            setup(nc.vector.tensor_copy(silurep[:, :, :], along(silc[:, :], H)))
            filled(dve, "mod")
            mods = fill_bank("mod")[:, 0:4 * NB].rearrange("p (j b) -> p j b", b=NB)
            for n, (j, plus, dst) in enumerate(((0, 0.0, fpar_all[:, :, F_SHA]), (1, 1.0, fpar_all[:, :, F_SCA]),
                                                (3, 0.0, bpar_all[:, :, B_SHM]), (4, 1.0, bpar_all[:, :, B_SCM]))):
                ins = nc.vector.tensor_scalar(dst, mods[:, n, :], col("b_mod", j), plus, ALU.add, ALU.add)
            setup(ins)
            front("wT", 0)
            for half in range(2):
                filled(dve, f"gates{half}")
                setup(nc.vector.tensor_tensor(
                    gates[:, 2 * half:2 * half + 2, :, :],
                    fill_bank(f"gates{half}").rearrange("p (b j h) -> p b j h", b=2, j=2),
                    bgates[:, :, :].unsqueeze(1).to_broadcast([P, 2, 2, H]), ALU.add))
            for step, dst, n, w in (("ew2Ta", ew2T, 4, 0), ("ew2Tb", ew2T, 2, 4), ("w2oa", w2o, 4, 0), ("w2ob", w2o, 2, 4)):
                filled(dve, step)
                half = 0.5 if dst is w2o else 1.0
                setup(nc.vector.tensor_scalar(dst[:, w:w + n, :].rearrange("p j h -> p (j h)"),
                                              fill_bank(step)[:, 0:n * H], half, None, ALU.mult))
            front("router", 0)
            filled(dve, "b2o")
            weights(dve, "experts", "front", "rest")
            zero(nc.vector.tensor_scalar(gw2, gw2, 0.5, None, ALU.mult))
            setup(nc.vector.tensor_tensor(b2oB[:, :, :], fill_bank("b2o")[:, 0:E * H].rearrange("p (e h) -> p e h", e=E),
                                          over(bout, E), ALU.add))
            dve.wait_ge(s_azeros, 2)
            nc.vector.memset(vc_all[0:S, :, :, HD], 1.0)
            zero(nc.vector.memset(vS[:, :, :, HD], 1.0))
            dve.wait_ge(s_vzeros, VZEROS)
            drained(dve, "b2o")

            iterations(run)

        @block.tensor
        def _(pe):
            begin(pe, ["front_filled", "nat_scored", "s_scored", "av_used", "m_filled", "o_filled", "back_filled",
                       "cn_scored", "cs_scored"])
            mm = nc.tensor.matmul

            def transposes(out_, ins_, ident):
                rows_ = ins_[0].shape[0]
                for c, t in enumerate(ins_):
                    last = nc.tensor.transpose(out_[0:t.shape[1], c * rows_:(c + 1) * rows_], t, ident[0:rows_, 0:rows_])
                return last

            def fill(step):
                n = FILLS.index(step)
                if n >= SETUP_BANKS:
                    before = FILLS[n - SETUP_BANKS]
                    drain_of = {"kc": "kcf"}.get(before, before)
                    drained(pe, drain_of)
                return fill_bank(step)

            def filled_by(ins):
                ins.then_inc(s_filled, 1)

            last_natural, last_scores = [upto("nat_reduced", 0, 0)], [upto("exp_done", 0, 0)]
            cross_in_nat, cross_in_sco = [None], [None]

            def front(step, b):
                fb = front_bank(step, b) if step in FRONT else None
                if step not in FRONT:
                    return
                n = FRONT.index(step)
                if n >= front_width(step, b):
                    after_drain(pe, "front", b, FRONT[n - front_width(step, b)])
                else:
                    after_batch(pe, "front", b - 1)
                if b == 2 and n == len(EARLY):
                    after_drain(pe, "front", b, FRONT[n - 2])
                if step in NEEDS:
                    after_drain(pe, "front", b, NEEDS[step])
                if step in ("nxT", "xnT"):
                    after(pe, "front_vec", b, FRONT_VEC, "xhat" if step == "nxT" else "xhat1")
                    ins = transposes(fb, [xh[:, c, :] for c in range(C)], identf)
                if step == "scores":
                    for c in range(C):
                        ins = mm(fb[:, c * (S + E):(c + 1) * (S + E)], chunk(nxT, c), fpar_all[:, b, F_G:F_G + S + E],
                                 start=True, stop=True)
                if step == "wT":
                    after(pe, "front_vec", b, FRONT_VEC, "pnorm")
                    ins = transposes(fb, [pw[:, c, :] for c in range(C)], identf)
                if step == "evT":
                    ins = mm(fb, fpar_all[0:KP, b, F_VP:F_VP + H], wT[0:KP, :], start=True, stop=True)
                if step == "router":
                    for c in range(C):
                        ins = mm(fb[:, c * E:(c + 1) * E], chunk(evT, c), wr[:, 1, :], start=True, stop=True)
                if step[0] == "h":
                    zi = HIDDEN[int(step[1])]
                    mm(fb, w1[:, 0, zi, :], nxT[:, :], start=True, stop=False)
                    ins = mm(fb, w1[:, 1, zi, :], evT[:, :], start=False, stop=True)
                if step == "gate":
                    after(pe, "front_vec", b, FRONT_VEC, "silu0")
                    for c in range(C):
                        ins = mm(chunk(fb, c), chunk(z[:, 2 * E, :], c), gw2, start=True, stop=True)
                if step in ("e0", "e1", "e2"):
                    e = int(step[1])
                    after(pe, "front_vec", b, FRONT_VEC, f"silu{2 * e + 2}")
                    for c in range(C):
                        for r in range(2):
                            ins = mm(chunk(fb, c), chunk(z[:, 2 * e + r, :], c), w2o[:, 2 * e + r, :],
                                     start=r == 0, stop=r == 1)
                if step in ("q", "k"):
                    ins = mm(fb, chunk(wqkv, "qk".index(step)), xnT[:, :], start=True, stop=True)
                if step == "v":
                    for c in range(C):
                        ins = mm(chunk(fb, c), chunk(xnT, c), wqkv[:, 2 * H:3 * H], start=True, stop=True)
                ins.then_inc(sem["front_filled"], 1)

            def attn(step, b):
                if step == "av":
                    weighted(b, NH - 1)
                if step[0] == "m":
                    g = int(step[1])
                    pe.wait_ge(sem["m_vec"], upto("m_vec", b, 4 * (g + 1)))
                    if g < 2:
                        after(pe, "o_drained", b - 1, OUT, ("o2", "proj")[g])
                    else:
                        after(pe, "o_drained", b, OUT, f"o{g - 2}")
                    transposes(m_bank, [mp[:, c, :, :].rearrange("p s g -> p (s g)") for c in range(C)], identb
                               ).then_inc(sem["m_filled"], 1)
                if step in ("o0", "o1", "o2", "o3"):
                    g = int(step[1])
                    after(pe, "av_drained", b, range(NG), g)
                    if g < 3:
                        after(pe, "m_drained", b, range(NG), g + 1)
                    elif b == NB - 1:
                        after(pe, "o_drained", b, OUT, "o2")
                    else:
                        after(pe, "m_drained", b + 1, range(NG), 0)
                    transposes(xb, [chunk(oT, c) for c in range(C)], identf).then_inc(sem["o_filled"], 1)
                if step == "aT":
                    after(pe, "o_drained", b, OUT, "o3")
                    transposes(xb, [an[:, c, :, :].rearrange("p h d -> p (h d)") for c in range(C)], identf
                               ).then_inc(sem["o_filled"], 1)
                if step == "proj":
                    after(pe, "o_drained", b, OUT, "aT")
                    after(pe, "attn_pool", b, ATTN_POOL, "wpg")
                    for c in range(C):
                        ins = mm(chunk(xb, c), chunk(aT, c), wpg[:, :], start=True, stop=True)
                    ins.then_inc(sem["o_filled"], 1)

            def back(step, b, has_attn):
                bb = back_bank(step, b) if step in BACK else None
                if step[:2] == "cn":
                    first = PAIR * int(step[2])
                    if first == 0:
                        pe.wait_ge(sem["qc_placed"], upto("qc_placed", b, 16 * len(RUNS)))
                        pe.wait_ge(sem["kc_placed"], upto("kc_placed", b, per["kc_placed"]))
                    for h in range(first, first + PAIR):
                        if h >= cross_banks(b):
                            pe.wait_ge(sem["cn_reduced"], upto("cn_reduced", b, h + 1 - cross_banks(b)))
                        if b == NB - 1:
                            pe.wait_ge(sem["exp_done"], last_scores[0] - 1 + h % 2)
                        pe.wait_ge(sem["nat_reduced"], last_natural[0] - 1 + h % 2)
                        for c in range(C):
                            ins = mm(cross_bank(nat, sco, h, b)[:, c * S:(c + 1) * S], chunk(qcS[:, h, :], c), kcS[:, h, :],
                                     start=True, stop=True)
                        ins.then_inc(sem["cn_scored"], 1)
                    cross_in_nat[0] = upto("cn_reduced", b, first + PAIR)
                    return
                if step[:2] == "cs":
                    first = PAIR * int(step[2])
                    moved = BESIDE if b == NB - 1 else 0
                    if first == moved:
                        pe.wait_ge(sem["cm_placed"], upto("cm_placed", b, 16))
                    elif first == 0:
                        after_drain(pe, "back", b, "cm")
                        pe.wait_ge(s_heads, 2)
                    for h in range(first, first + PAIR):
                        if h >= cross_banks(b):
                            pe.wait_ge(sem["cexp_done"], upto("cexp_done", b, h + 1 - cross_banks(b)))
                        pe.wait_ge(sem["exp_done"], last_scores[0] - 1 + h % 2)
                        bank = cross_bank(sco, nat, h, b)[0:S, :]
                        ins = mm(bank, kcS[:, h, :], qcS[:, h, :], start=True, stop=h >= moved)
                        if h < moved:
                            ins = mm(bank, of_head[:, h:h + 1].to_broadcast([3 * NH, S]), cmrow[:, :], start=False, stop=True)
                        ins.then_inc(sem["cs_scored"], 1)
                    cross_in_sco[0] = upto("cexp_done", b, first + PAIR)
                    return
                if step not in BACK:
                    return
                n = BACK.index(step)
                if n >= back_width(b):
                    after_drain(pe, "back", b, BACK[n - back_width(b)])
                else:
                    after_batch(pe, "back", b - 1)
                if step in NEEDS:
                    after_drain(pe, "back", b, NEEDS[step])
                if step == "cT" and b == 0:
                    for n in (1, 2):
                        after_drain(pe, "front", 2, EARLY[-n])
                if step == "cT" and b == NB - 2:
                    after_batch(pe, "front", NB - 1)
                if step == "cT":
                    after(pe, "back_vec", b, BACK_VEC, "xhat1")
                    ins = transposes(bb, [bxh[:, c, :] for c in range(C)], identf)
                if step == "qc":
                    ins = mm(bb, wqc, cT[:, :], start=True, stop=True)
                if step == "cm":
                    after(pe, "back_vec", b, BACK_VEC, "n3")
                    ins = transposes(bb.bitcast(BF16),
                                     [cmp_[:, c, :, :].rearrange("p s h -> p (s h)") for c in range(C)], identb)
                if step[:3] == "cav":
                    g = int(step[3])
                    for hh in range(G):
                        h = g * G + hh
                        pe.wait_ge(sem["cexp_done"], upto("cexp_done", b, h + 1))
                        ins = mm(bb[TILE * hh:TILE * (hh + 1), :], bpar_all[0:KP, b, B_VC + h * TILE:B_VC + (h + 1) * TILE],
                                 cross_tile(h, has_attn)[0:KP, :], start=True, stop=True)
                if step in ("co0", "co1", "co2", "co3"):
                    ins = transposes(bb, [chunk(coT, c) for c in range(C)], identf)
                if step == "caT":
                    ins = transposes(bb, [can[:, c, :, :].rearrange("p h d -> p (h d)") for c in range(C)], identf)
                if step == "cproj":
                    for c in range(C):
                        ins = mm(chunk(bb, c), chunk(caT, c), wcproj, start=True, stop=True)
                if step == "xT":
                    after(pe, "back_vec", b, BACK_VEC, "xhat2")
                    ins = transposes(bb, [bxh[:, c, :] for c in range(C)], identf)
                if step in ("m0", "m1", "m2", "m3"):
                    ins = mm(bb, chunk(wm1, int(step[1])), mT[:, :], start=True, stop=True)
                if step == "mlp":
                    after(pe, "back_pool", b, BACK_POOL, "gbm")
                    for c in range(C):
                        for j in range(4):
                            if c == 0 and b < NB - 1:
                                after(pe, "gelu_done", b, range(4), j)
                            elif c == 0:
                                after_drain(pe, "back", b, f"m{j}")
                            ins = mm(chunk(bb, c), chunk(hm[:, j, :], c), w2g[:, j, :], start=j == 0, stop=j == 3)
                ins.then_inc(sem["back_filled"], 1)

            def natural(b, h, pair):
                if h % (NH // 2) == 0 and pair == 0:
                    half = h // (NH // 2)
                    pe.wait_ge(sem[f"half{half}"], upto(f"half{half}", b, 16 * HALF))
                for c in (2 * pair, 2 * pair + 1):
                    pe.wait_ge(sem["nat_reduced"], upto("nat_reduced", b, h * C + c - 1))
                    if cross_in_nat[0]:
                        pe.wait_ge(sem["cn_reduced"], cross_in_nat[0] - 1 + c % 2)
                    mm(nat[:, c % 2, :], chunk(qS[:, h, :], c), kS[:, h, :], start=True, stop=True
                       ).then_inc(sem["nat_scored"], 1)
                cross_in_nat[0] = None
                last_natural[0] = upto("nat_reduced", b, h * C + 2 * pair + 2)

            def scores(b, s, pair):
                g, kc = divmod(s, C)
                if kc == 0 and pair == 0:
                    pe.wait_ge(sem["m_placed"], upto("m_placed", b, 16 * (g + 1)))
                for hh in (2 * pair, 2 * pair + 1):
                    j, h = s * G + hh, g * G + hh
                    pe.wait_ge(sem["exp_done"], upto("exp_done", b, j - 1))
                    if cross_in_sco[0]:
                        pe.wait_ge(sem["cexp_done"], cross_in_sco[0] - 1 + j % 2)
                    mm(sco[:, j % 2, :], chunk(kS[:, h, :], kc), qS[:, h, :], start=True, stop=True
                       ).then_inc(sem["s_scored"], 1)
                cross_in_sco[0] = None
                last_scores[0] = upto("exp_done", b, s * G + 2 * pair + 2)

            def weighted(b, s):
                g, kc = divmod(s, C)
                if s == 0:
                    pe.wait_ge(sem["v_placed"], upto("v_placed", b, 1))
                if kc == 0:
                    pe.wait_ge(sem["av_drained"], upto("av_drained", b, g))
                for hh in range(G):
                    j = s * G + hh
                    pe.wait_ge(sem["exp_done"], upto("exp_done", b, j + 1))
                    mm(avb[TILE * hh:TILE * (hh + 1), :], vS[:, kc, g * G + hh, :], pT[:, j % RING, :],
                       start=kc == 0, stop=kc == C - 1).then_inc(sem["av_used"], 1)

            def run(b, has_attn, has_front):
                engine = {"front": front, "attn": attn, "back": back}
                for s, places in enumerate(places_of("T", b)):
                    ahead = (b, s + LAG, has_attn) if s + LAG < NH else (b + 1, s + LAG - NH, has_front)
                    for n, place in enumerate(places):
                        if has_attn and n < 2:
                            scores(b, s, n)
                        if ahead[2] and n < 2:
                            natural(ahead[0], ahead[1], n)
                        if has_attn and n == 2 and s:
                            weighted(b, s - 1)
                        do_place(place, engine)

            pe.wait_ge(s_consts, CONSTS)
            weights(pe, "rows")
            filled_by(transposes(fill("cols"), [rows[0:len(ROWS), :]], identf))
            weights(pe, "ctx")
            filled_by(transposes(fill("ctxT"), [ctxn[0:S, b, :] for b in range(NB)], identf))
            drained(pe, "ctxhat")
            filled_by(transposes(fill("ctxhT"), [ctxh[0:S, b, :] for b in range(NB)], identf))
            weights(pe, "w0")
            filled_by(transposes(fill("wq0T"), [wqkv0[:, 0, :]], identf))
            drained(pe, "ctxT")
            filled_by(mm(fill("kpT")[:, 0:NB * S], wqkv0[:, 1, :], ctxT[:, :, :].rearrange("p b s -> p (b s)"),
                         start=True, stop=True))
            drained(pe, "kpT")
            filled_by(mm(fill("G")[:, 0:NB * S], wq0T[:, :], kpT[:, :, :].rearrange("p b s -> p (b s)"),
                         start=True, stop=True))
            front("nxT", 0)
            bank = fill("vp")
            for b in range(NB):
                ins = mm(chunk(bank, b)[0:S, :], ctxT[:, b, :], wqkv0[:, 2, :], start=True, stop=True)
            filled_by(ins)
            drained(pe, "ctxhT")
            filled_by(mm(fill("kc")[:, 0:NB * S], wkvc[:, 0:H], ctxhT[:, :, :].rearrange("p b s -> p (b s)"),
                         start=True, stop=True))
            bank = fill("vc")
            for b in range(NB):
                ins = mm(chunk(bank, b)[0:S, :], ctxhT[:, b, :], wkvc[:, H:2 * H], start=True, stop=True)
            filled_by(ins)
            weights(pe, "w1")
            bank = fill("hb")
            for zi in range(NZ):
                ins = mm(bank[:, zi * NB:(zi + 1) * NB], w1[:, 2, zi, :], col("cond", 0, NB), start=True, stop=True)
            filled_by(ins)
            bank = fill("rbias")
            for b in range(NB):
                ins = mm(bank[:, b * E:(b + 1) * E], condrep[:, b, :], wr[:, 2, :], start=True, stop=True)
            filled_by(ins)
            drained(pe, "wr")
            front("scores", 0)
            weights(pe, "mod")
            pe.wait_ge(s_silu, 1)
            bank = fill("mod")
            for n, j in enumerate((0, 1, 3, 4)):
                ins = mm(bank[:, n * NB:(n + 1) * NB], wmod[:, j, :], silc[:, :], start=True, stop=True)
            filled_by(ins)
            front("wT", 0)
            drained(pe, "silurep")
            for half in range(2):
                bank = fill(f"gates{half}")
                for n in range(4):
                    ins = mm(chunk(bank, n), silurep[:, 2 * half + n // 2, :], wmod[:, (2, 5)[n % 2], :],
                             start=True, stop=True)
                filled_by(ins)
            drained(pe, "vp")
            front("evT", 0)
            weights(pe, "experts")
            filled_by(transposes(fill("ew2Ta"), [ew2[:, j, :] for j in range(4)], identf))
            filled_by(transposes(fill("ew2Tb"), [ew2[:, j, :] for j in (4, 5)], identf))
            for step, blocks, drain_of in (("w2oa", (0, 1, 2, 3), "ew2Ta"), ("w2ob", (4, 5), "ew2Tb")):
                drained(pe, drain_of)
                bank = fill(step)
                for n, j in enumerate(blocks):
                    ins = mm(chunk(bank, n), ew2T[:, j, :], outw, start=True, stop=True)
                filled_by(ins)
            front("router", 0)
            bank = fill("b2o")
            for e in range(E):
                ins = mm(chunk(bank, e), b2rep[:, e, :], outw, start=True, stop=True)
            filled_by(ins)
            weights(pe, "front", "rest")
            drained(pe, "b2o")
            pe.wait_ge(s_vzeros, VZEROS)

            iterations(run)


def kernel(x, cond_1024, ctx_1024, **w):
    import numpy as _np
    import concourse.bacc as _bacc
    from concourse.bass_utils import run_bass_kernel_spmd as _run

    first = {n[len("L0_xcond_"):]: _np.asarray(t) for n, t in w.items() if n.startswith("L0_xcond_")}
    second = {n[len("L1_xcond_"):]: _np.asarray(t) for n, t in w.items() if n.startswith("L1_xcond_")}

    def by_rows(t):
        return t.reshape(-1, P, t.shape[-1]).transpose(1, 0, 2)

    def by_feature(t):
        return t.reshape(*t.shape[:-1], NH, HD).swapaxes(-1, -2).reshape(t.shape)

    def lay(load, parts):
        assert list(LOADS[load]) == list(parts)
        return _np.concatenate([_np.ascontiguousarray(t).reshape(P, -1) for t in parts.values()], axis=1)

    def lay_over(load, parts):
        assert list(LOADS[load]) == list(parts)
        return _np.concatenate([t.reshape(-1) for t in parts.values()])

    w_qkv, b_qkv, w_kvc, b_kvc = second["W_qkv"], second["b_qkv"], second["W_kvc"], second["b_kvc"]
    hidden = _np.concatenate([first["e_w1"][e] for e in range(E)] + [first["gate_w1"]], axis=1)
    b_mod = second["b_mod"].reshape(6, H)
    arrays = {
        "x": _np.ascontiguousarray(x),
        "ctx": _np.ascontiguousarray(ctx_1024),
        "rows": _np.concatenate([t.reshape(-1, H) for t in (
            first["e_b1"], first["gate_b1"], first["ln_gamma"], first["ln_beta"], b_mod, by_feature(b_qkv[:H]),
            by_feature(b_qkv[H:2 * H]), by_feature(second["b_qc"]), by_feature(b_kvc[:H]), second["b_mlp1"],
            _np.asarray(cond_1024), first["e_b2"])]),
        "w_first": lay("w_first", {
            "Wq Wk Wv": _np.concatenate([first["Wq"], first["Wk"], first["Wv"]], axis=1),
            "router_W": by_rows(first["router_W"]),
            "W_kvc": _np.concatenate([by_feature(w_kvc[:, :H]), w_kvc[:, H:]], axis=1)}),
        "w_hidden": lay("w_hidden", {"w1": by_rows(hidden)}),
        "w_mod": lay("w_mod", {"W_mod": second["W_mod"]}),
        "w_experts": lay("w_experts", {"e_w2": by_rows(first["e_w2"].reshape(-1, H)), "out_w": first["out_w"]}),
        "w_front": lay("w_front", {
            "gate_w2": first["gate_w2"],
            "W_qkv": _np.concatenate([by_feature(w_qkv[:, :H]), by_feature(w_qkv[:, H:2 * H]), w_qkv[:, 2 * H:]],
                                     axis=1)}),
        "w_back": lay("w_back", {
            "W_proj": second["W_proj"], "W_qc": by_feature(second["W_qc"]), "W_cproj": second["W_cproj"],
            "W_mlp1": second["W_mlp1"], "W_mlp2": by_rows(second["W_mlp2"])}),
        "over_setup": lay_over("over_setup", {
            "router_b": first["router_b"], "b_kvc v": b_kvc[H:], "b_mod gates": b_mod[[2, 5]], "out_b": first["out_b"]}),
        "over_front": lay_over("over_front", {"gate_b2": first["gate_b2"], "b_qkv v": b_qkv[2 * H:]}),
        "over_back": lay_over("over_back", {
            "b_proj": second["b_proj"], "b_cproj": second["b_cproj"], "b_mlp2": second["b_mlp2"]}),
    }

    nc = _bacc.Bacc("TRN2", target_bir_lowering=False, num_devices=1)
    args = {name: nc.dram_tensor(f"in_{name}", t.shape, mybir.dt.from_np(t.dtype), kind="ExternalInput").ap()
            for name, t in arrays.items()}
    out = nc.dram_tensor("out", (NB, T, H), F32, kind="ExternalOutput").ap()
    build(nc, args, out)
    r = _run(nc, [{f"in_{name}": t for name, t in arrays.items()}], core_ids=[0])
    return r.results[0]["out"]
```
